# Optimizing a Trainium2 kernel written in Bass

```python
import numpy as np
import jax
import jax.numpy as jnp

def _softmax(x, axis=-1):
    return jax.nn.softmax(x, axis=axis)

def _gelu(x):
    return jax.nn.gelu(x, approximate=True)

def _silu(x):
    return jax.nn.silu(x)

def _sigmoid(x):
    return jax.nn.sigmoid(x)

def _layernorm(x, axis=-1, eps=1e-05):
    m = jnp.mean(x, axis=axis, keepdims=True)
    v = jnp.var(x, axis=axis, keepdims=True)
    return (x - m) / jnp.sqrt(v + eps)

def _scatter_add(tgt, idx, src, axis=0):
    return tgt.at[idx].add(src)

def _segment_sum(src, seg, n):
    return jax.ops.segment_sum(src, seg, n)
kernel_name = 'mk_adj_resnorm_d4_adj_r2_ddf00f'

def setup_inputs(seed: int=0):
    np.random.seed(seed)
    _w = jnp.asarray

    def _rec_inputs():
        import jax
        import jax.numpy as jnp
        _gk = jax.random.key(seed)
        x = 7.22e-05 + 1 * jax.random.normal(jax.random.fold_in(_gk, 1), (16, 512, 128), jnp.float32)
        _w = (1.0 + jnp.arange(512, dtype=jnp.float32)) ** (-0.5)
        _w = _w / _w.mean()
        _pij = jnp.clip(0.03125 * _w[:, None] * _w[None, :], 0.0, 1.0)
        _a = jax.random.uniform(jax.random.fold_in(_gk, 2), (16, 512, 512)) < _pij
        _a = jnp.logical_or(_a, jnp.swapaxes(_a, -1, -2))
        _a = jnp.logical_or(_a, jnp.eye(512, dtype=bool))
        _af = _a.astype(jnp.float32)
        adj = _af
        return (x, adj)
    x, adj = _rec_inputs()

    def _L0_gnn_setup():
        import jax, jax.numpy as jnp
        import numpy as np
        from jax import lax
        DIM = 128
        EPS = 1e-05

        def _bn(h, g, b, m, v):
            scale = g / jnp.sqrt(v + EPS)
            return h * scale[None, :, None] + (b - m * scale)[None, :, None]

        def _conv1d(h, w, pad):
            return lax.conv_general_dilated(h, w, window_strides=(1,), padding=[(pad, pad)], dimension_numbers=('NCH', 'OIH', 'NCH'))
        key = jax.random.key(seed)
        ks = jax.random.split(key, 16)
        bs, n, d = (16, 1024, DIM)
        s = 0.05
        return {'x': jax.random.normal(ks[0], (bs, n, d), jnp.float32), 'mask': jnp.ones((bs, n, n), jnp.float32), 'w_se': jax.random.normal(ks[1], (3, d), jnp.float32) * s, 'b_se': jnp.zeros((3,), jnp.float32), 'conv1_w': jax.random.normal(ks[2], (d, d, 1), jnp.float32) * s, 'bn1_g': jnp.ones((d,), jnp.float32), 'bn1_b': jnp.zeros((d,), jnp.float32), 'bn1_m': jnp.zeros((d,), jnp.float32), 'bn1_v': jnp.ones((d,), jnp.float32), 'conv2_w': jax.random.normal(ks[3], (d, d, 17), jnp.float32) * s, 'bn2_g': jnp.ones((d,), jnp.float32), 'bn2_b': jnp.zeros((d,), jnp.float32), 'bn2_m': jnp.zeros((d,), jnp.float32), 'bn2_v': jnp.ones((d,), jnp.float32), 'w_msg': jax.random.normal(ks[4], (d, d), jnp.float32) * s, 'b_msg': jnp.zeros((d,), jnp.float32), 'w_ih': jax.random.normal(ks[5], (3 * d, 2 * d), jnp.float32) * s, 'b_ih': jnp.zeros((3 * d,), jnp.float32), 'w_hh': jax.random.normal(ks[6], (3 * d, d), jnp.float32) * s, 'b_hh': jnp.zeros((3 * d,), jnp.float32)}
    _L0_gnn_all = _L0_gnn_setup()
    _L0_gnn_in = {k: v for k, v in _L0_gnn_all.items() if k in ('w_se', 'b_se', 'conv1_w', 'bn1_g', 'bn1_b', 'bn1_m', 'bn1_v', 'conv2_w', 'bn2_g', 'bn2_b', 'bn2_m', 'bn2_v', 'w_msg', 'b_msg', 'w_ih', 'b_ih', 'w_hh', 'b_hh')}
    del _L0_gnn_all

    def _L1_gnn_setup():
        import jax, jax.numpy as jnp
        import numpy as np
        H = 4
        NEG = -9000000000000000.0
        key = jax.random.key(seed)
        k1, k2, k3, k4 = jax.random.split(key, 4)
        B, N, D = (8, 512, 128)
        dh = D // H
        return {'node_features': jax.random.normal(k1, (B, N, D), dtype=jnp.float32), 'adjacency': jax.random.uniform(k2, (B, N, N), dtype=jnp.float32), 'W_proj': jax.random.normal(k3, (D, D), dtype=jnp.float32) * (1.0 / np.sqrt(D)), 'a_w': jax.random.normal(k4, (1, 2 * dh + 1), dtype=jnp.float32) * 0.1, 'bias': jnp.zeros((D,), dtype=jnp.float32)}
    _L1_gnn_all = _L1_gnn_setup()
    _L1_gnn_in = {k: v for k, v in _L1_gnn_all.items() if k in ('W_proj', 'a_w', 'bias')}
    del _L1_gnn_all

    def _L2_gnn_setup():
        import jax, jax.numpy as jnp
        import numpy as np
        GROUPS = [list(range(25)), [0, 1, 2, 3, 4, 5, 6, 7, 8], [0, 9, 10, 11, 12, 13, 14], [6, 7, 8, 12, 13, 14], [3, 4, 5, 9, 10, 11]]
        B, N, D_IN, D_HID = (4096, 25, 128, 256)

        def _graph_conv(x, adj, W, b):
            n = adj.shape[-1]
            A = adj + jnp.eye(n, dtype=adj.dtype)
            deg = jnp.sum(A, axis=-1)
            deg_safe = jnp.where(deg == 0, 1.0, deg)
            dinv = jnp.where(deg == 0, 0.0, deg_safe ** (-0.5))
            norm_adj = dinv[:, :, None] * A * dinv[:, None, :]
            support = jnp.einsum('bnd,de->bne', x, W)
            out = jnp.einsum('bnm,bme->bne', norm_adj, support) + b
            return jax.nn.relu(out)
        key = jax.random.key(seed)
        ks = jax.random.split(key, 7)
        s1 = float(np.sqrt(6.0 / (D_IN + D_HID)))
        s2 = float(np.sqrt(6.0 / (D_HID + D_IN)))
        return {'x': jax.random.normal(ks[0], (B, N, D_IN), dtype=jnp.float32), 'adj': jax.random.uniform(ks[1], (B, N, N), dtype=jnp.float32), 'W1': jax.random.uniform(ks[2], (5, D_IN, D_HID), jnp.float32, -s1, s1), 'b1': jnp.zeros((5, D_HID), dtype=jnp.float32), 'W2': jax.random.uniform(ks[3], (5, D_HID, D_IN), jnp.float32, -s2, s2), 'b2': jnp.zeros((5, D_IN), dtype=jnp.float32), 'fusion_w': jnp.ones((5,), dtype=jnp.float32)}
    _L2_gnn_all = _L2_gnn_setup()
    _L2_gnn_in = {k: v for k, v in _L2_gnn_all.items() if k in ('W1', 'b1', 'W2', 'b2', 'fusion_w')}
    del _L2_gnn_all

    def _L3_gnn_setup():
        import jax, jax.numpy as jnp
        import numpy as np
        B, N, IN_DIM, OUT_DIM, H = (8, 512, 128, 128, 4)
        D = OUT_DIM // H
        NEG_INF = -9000000000000000.0
        LRELU_SLOPE = 0.2
        key = jax.random.key(seed)
        k1, k2, k3, k4 = jax.random.split(key, 4)
        x = jax.random.normal(k1, (B, N, IN_DIM), dtype=jnp.float32)
        adj = jax.random.randint(k2, (B, N, N), 0, 2).astype(jnp.float32)
        W = jax.random.normal(k3, (IN_DIM, H * D), dtype=jnp.float32) * jnp.sqrt(2.0 / (IN_DIM + H * D))
        a = jax.random.normal(k4, (H, 2 * D), dtype=jnp.float32) * jnp.sqrt(2.0 / (H + 2 * D))
        return {'x': x, 'adj': adj, 'W': W, 'a': a}
    _L3_gnn_all = _L3_gnn_setup()
    _L3_gnn_in = {k: v for k, v in _L3_gnn_all.items() if k in ('W', 'a')}
    del _L3_gnn_all
    return {'x': x, 'adj': adj, 'L0_gnn_w_se': _L0_gnn_in['w_se'], 'L0_gnn_b_se': _L0_gnn_in['b_se'], 'L0_gnn_conv1_w': _L0_gnn_in['conv1_w'], 'L0_gnn_bn1_g': _L0_gnn_in['bn1_g'], 'L0_gnn_bn1_b': _L0_gnn_in['bn1_b'], 'L0_gnn_bn1_m': _L0_gnn_in['bn1_m'], 'L0_gnn_bn1_v': _L0_gnn_in['bn1_v'], 'L0_gnn_conv2_w': _L0_gnn_in['conv2_w'], 'L0_gnn_bn2_g': _L0_gnn_in['bn2_g'], 'L0_gnn_bn2_b': _L0_gnn_in['bn2_b'], 'L0_gnn_bn2_m': _L0_gnn_in['bn2_m'], 'L0_gnn_bn2_v': _L0_gnn_in['bn2_v'], 'L0_gnn_w_msg': _L0_gnn_in['w_msg'], 'L0_gnn_b_msg': _L0_gnn_in['b_msg'], 'L0_gnn_w_ih': _L0_gnn_in['w_ih'], 'L0_gnn_b_ih': _L0_gnn_in['b_ih'], 'L0_gnn_w_hh': _L0_gnn_in['w_hh'], 'L0_gnn_b_hh': _L0_gnn_in['b_hh'], 'L1_gnn_W_proj': _L1_gnn_in['W_proj'], 'L1_gnn_a_w': _L1_gnn_in['a_w'], 'L1_gnn_bias': _L1_gnn_in['bias'], 'L2_gnn_W1': _L2_gnn_in['W1'], 'L2_gnn_b1': _L2_gnn_in['b1'], 'L2_gnn_W2': _L2_gnn_in['W2'], 'L2_gnn_b2': _L2_gnn_in['b2'], 'L2_gnn_fusion_w': _L2_gnn_in['fusion_w'], 'L3_gnn_W': _L3_gnn_in['W'], 'L3_gnn_a': _L3_gnn_in['a']}

def reference(x, adj, L0_gnn_w_se, L0_gnn_b_se, L0_gnn_conv1_w, L0_gnn_bn1_g, L0_gnn_bn1_b, L0_gnn_bn1_m, L0_gnn_bn1_v, L0_gnn_conv2_w, L0_gnn_bn2_g, L0_gnn_bn2_b, L0_gnn_bn2_m, L0_gnn_bn2_v, L0_gnn_w_msg, L0_gnn_b_msg, L0_gnn_w_ih, L0_gnn_b_ih, L0_gnn_w_hh, L0_gnn_b_hh, L1_gnn_W_proj, L1_gnn_a_w, L1_gnn_bias, L2_gnn_W1, L2_gnn_b1, L2_gnn_W2, L2_gnn_b2, L2_gnn_fusion_w, L3_gnn_W, L3_gnn_a):
    import jax
    import jax.numpy as jnp

    def _L0_gnn_ref(x, mask, w_se, b_se, conv1_w, bn1_g, bn1_b, bn1_m, bn1_v, conv2_w, bn2_g, bn2_b, bn2_m, bn2_v, w_msg, b_msg, w_ih, b_ih, w_hh, b_hh):
        import jax, jax.numpy as jnp
        import numpy as np
        from jax import lax
        DIM = 128
        EPS = 1e-05

        def _bn(h, g, b, m, v):
            scale = g / jnp.sqrt(v + EPS)
            return h * scale[None, :, None] + (b - m * scale)[None, :, None]

        def _conv1d(h, w, pad):
            return lax.conv_general_dilated(h, w, window_strides=(1,), padding=[(pad, pad)], dimension_numbers=('NCH', 'OIH', 'NCH'))
        d = x.shape[-1]
        xc = jnp.transpose(x, (0, 2, 1))
        h = _bn(_conv1d(xc, conv1_w, 0), bn1_g, bn1_b, bn1_m, bn1_v)
        h = jax.nn.relu(h)
        h = _bn(_conv1d(h, conv2_w, 8), bn2_g, bn2_b, bn2_m, bn2_v)
        x_conv = jnp.transpose(jax.nn.relu(h + xc), (0, 2, 1))
        s = x @ w_se.T + b_se
        sq = jnp.sum(s * s, axis=-1)
        dist = sq[:, :, None] + sq[:, None, :] - 2.0 * jnp.einsum('bnd,bmd->bnm', s, s)
        A = jnp.exp(-dist) * mask
        msg = jax.nn.relu(x @ w_msg.T + b_msg)
        x_nmp = jnp.einsum('bnm,bmd->bnd', A, msg)
        x_in = jnp.concatenate([x_conv, x_nmp], axis=-1)
        gi = x_in @ w_ih.T + b_ih
        gh = x @ w_hh.T + b_hh
        gi_r, gi_z, gi_n = (gi[..., :d], gi[..., d:2 * d], gi[..., 2 * d:])
        gh_r, gh_z, gh_n = (gh[..., :d], gh[..., d:2 * d], gh[..., 2 * d:])
        r = jax.nn.sigmoid(gi_r + gh_r)
        z = jax.nn.sigmoid(gi_z + gh_z)
        nn_ = jnp.tanh(gi_n + r * gh_n)
        return (1.0 - z) * nn_ + z * x

    def _L1_gnn_ref(node_features, adjacency, W_proj, a_w, bias):
        import jax, jax.numpy as jnp
        import numpy as np
        H = 4
        NEG = -9000000000000000.0
        B, N, D = node_features.shape
        dh = D // H
        h = (node_features @ W_proj.T).reshape(B, N, H, dh)
        w = a_w[0]
        wl, wr, we = (w[:dh], w[dh:2 * dh], w[2 * dh])
        s_left = jnp.einsum('bihd,d->bih', h, wl)
        s_right = jnp.einsum('bjhd,d->bjh', h, wr)
        scores = s_left[:, :, None, :] + s_right[:, None, :, :] + adjacency[..., None] * we
        scores = jax.nn.leaky_relu(scores, negative_slope=0.2)
        pad = (adjacency <= 1e-05).astype(scores.dtype)
        scores = scores + (NEG * pad)[..., None]
        attn = jax.nn.softmax(scores, axis=2)
        agg = jnp.einsum('bijh,bjhd->bihd', attn, h).reshape(B, N, D)
        out = jax.nn.leaky_relu(node_features + agg + bias, negative_slope=0.5)
        return out

    def _L2_gnn_ref(x, adj, W1, b1, W2, b2, fusion_w):
        import jax, jax.numpy as jnp
        import numpy as np
        GROUPS = [list(range(25)), [0, 1, 2, 3, 4, 5, 6, 7, 8], [0, 9, 10, 11, 12, 13, 14], [6, 7, 8, 12, 13, 14], [3, 4, 5, 9, 10, 11]]
        B, N, D_IN, D_HID = (4096, 25, 128, 256)

        def _graph_conv(x, adj, W, b):
            n = adj.shape[-1]
            A = adj + jnp.eye(n, dtype=adj.dtype)
            deg = jnp.sum(A, axis=-1)
            deg_safe = jnp.where(deg == 0, 1.0, deg)
            dinv = jnp.where(deg == 0, 0.0, deg_safe ** (-0.5))
            norm_adj = dinv[:, :, None] * A * dinv[:, None, :]
            support = jnp.einsum('bnd,de->bne', x, W)
            out = jnp.einsum('bnm,bme->bne', norm_adj, support) + b
            return jax.nn.relu(out)
        norm_w = jax.nn.softmax(fusion_w)
        fused = jnp.zeros_like(x)
        for g, idx_list in enumerate(GROUPS):
            idx = jnp.asarray(idx_list)
            x_g = x[:, idx, :]
            adj_g = adj[:, idx][:, :, idx]
            h = _graph_conv(x_g, adj_g, W1[g], b1[g])
            out_g = _graph_conv(h, adj_g, W2[g], b2[g])
            fused = fused.at[:, idx, :].add(norm_w[g] * out_g)
        return fused

    def _L3_gnn_ref(x, adj, W, a):
        import jax, jax.numpy as jnp
        import numpy as np
        B, N, IN_DIM, OUT_DIM, H = (8, 512, 128, 128, 4)
        D = OUT_DIM // H
        NEG_INF = -9000000000000000.0
        LRELU_SLOPE = 0.2
        h = jnp.einsum('bni,io->bno', x, W).reshape(x.shape[0], x.shape[1], H, D)
        h = h.transpose(0, 2, 1, 3)
        a1, a2 = (a[:, :D], a[:, D:])
        e_i = jnp.einsum('bhnd,hd->bhn', h, a1)
        e_j = jnp.einsum('bhmd,hd->bhm', h, a2)
        e = e_i[:, :, :, None] + e_j[:, :, None, :]
        e = jnp.where(e > 0, e, LRELU_SLOPE * e)
        e = jnp.where(adj[:, None, :, :] > 0, e, NEG_INF)
        attn = jax.nn.softmax(e, axis=-1)
        out = jnp.einsum('bhnm,bhmd->bhnd', attn, h)
        out = out.transpose(0, 2, 1, 3).reshape(x.shape[0], x.shape[1], H * D)
        return out
    x = _layernorm(x + _L0_gnn_ref(x, adj, L0_gnn_w_se, L0_gnn_b_se, L0_gnn_conv1_w, L0_gnn_bn1_g, L0_gnn_bn1_b, L0_gnn_bn1_m, L0_gnn_bn1_v, L0_gnn_conv2_w, L0_gnn_bn2_g, L0_gnn_bn2_b, L0_gnn_bn2_m, L0_gnn_bn2_v, L0_gnn_w_msg, L0_gnn_b_msg, L0_gnn_w_ih, L0_gnn_b_ih, L0_gnn_w_hh, L0_gnn_b_hh), axis=-1)
    x = _layernorm(x + _L1_gnn_ref(x, adj, L1_gnn_W_proj, L1_gnn_a_w, L1_gnn_bias), axis=-1)
    x = _layernorm(x + _L2_gnn_ref(x, adj, L2_gnn_W1, L2_gnn_b1, L2_gnn_W2, L2_gnn_b2, L2_gnn_fusion_w), axis=-1)
    x = _layernorm(x + _L3_gnn_ref(x, adj, L3_gnn_W, L3_gnn_a), axis=-1)
    return x

_drawn_inputs = setup_inputs


def setup_inputs(seed=0):
    import zlib

    import numpy as np

    out = dict(_drawn_inputs(seed))
    spreads = {'L0_gnn_b_se': (0.0, 2.0),
     'L0_gnn_bn1_g': (1.0, 0.6),
     'L0_gnn_bn1_b': (0.0, 0.489),
     'L0_gnn_bn1_m': (0.0, 0.421),
     'L0_gnn_bn1_v': (1.0, 0.6),
     'L0_gnn_bn2_g': (1.0, 0.6),
     'L0_gnn_bn2_b': (0.0, 0.696),
     'L0_gnn_bn2_m': (0.0, 0.635),
     'L0_gnn_bn2_v': (1.0, 0.6),
     'L0_gnn_b_msg': (0.0, 0.1),
     'L0_gnn_b_ih': (0.0, 0.1),
     'L0_gnn_b_hh': (0.0, 0.318),
     'L1_gnn_bias': (0.0, 0.1),
     'L2_gnn_b1': (0.0, 0.8),
     'L2_gnn_b2': (0.0, 2.0),
     'L2_gnn_fusion_w': (1.0, 0.6)}
    factors = {'L2_gnn_W1': 5.194, 'L2_gnn_W2': 4.192}
    for name, (base, spread) in spreads.items():
        noise = np.random.default_rng([zlib.crc32(name.encode()), seed]).standard_normal(out[name].shape)
        drawn = base * np.exp(spread * noise) if base else spread * noise
        out[name] = jnp.asarray(drawn.astype(out[name].dtype))
    for name, factor in factors.items():
        out[name] = (out[name] * factor).astype(out[name].dtype)
    return out
```

```python
from contextlib import ExitStack

import concourse.bass as bass
from concourse import mybir

F32 = mybir.dt.float32
F32R = mybir.dt.float32r
F16 = mybir.dt.float16
ALU = mybir.AluOpType
ACT = mybir.ActivationFunctionType
AX_X = mybir.AxisListType.X
RMAX = bass.bass_isa.ReduceOp.max

P = 128
B, N, D = 16, 512, 128
NT = N // P
TAPS, PAD = 17, 8
H, DH = 4, 32
HC = DH + 1
XY = 2 * HC
WP = D + 2 * H
NODES, SLOT, GROUPS = 25, 32, 5
PACK = P // SLOT
HID = 256
EPS = 1e-5
LOG_SCALE = 5.545177444479562
C1, C2, CM, CS, CG = 0, D, D + TAPS * D, D + TAPS * D + D, D + TAPS * D + D + 96
NW = CG + 3 * 3 * D


def build_program(nc, a):
    with ExitStack() as ctx:
        def sb(name, shape, dt=F32):
            return ctx.enter_context(nc.sbuf_tensor(name, shape, dt))

        def sem(name):
            return ctx.enter_context(nc.semaphore(name))

        def ge(eng, s, n):
            if isinstance(n, int) and n <= 0:
                return
            eng.wait_ge(s, n)

        bank_a = ctx.enter_context(nc.psum_tensor("bank_a", [P, N], F32))
        bank_b = ctx.enter_context(nc.psum_tensor("bank_b", [P, N], F32))
        bank_c = ctx.enter_context(nc.psum_tensor("bank_c", [P, N], F32))
        bank_d = ctx.enter_context(nc.psum_tensor("bank_d", [P, N], F32))
        gat_ps = ctx.enter_context(nc.psum_tensor("gat_ps", [P, NT, 512], F32))
        gat_bank = [gat_ps[:, t, :] for t in range(NT)]

        ident = sb("ident", [P, P])
        w_hi = sb("w_hi", [P, NW], F32R)
        w_lo = sb("w_lo", [P, NW], F32R)
        cols = sb("cols", [P, 14])
        bn_sc = sb("bn_sc", [P, 2])
        bn_sh = sb("bn_sh", [P, 2])
        bn_t = sb("bn_t", [P, 2])
        half_b = sb("half_b", [P, 2])
        bse = sb("bse", [96, 1])
        bmsg = sb("bmsg", [P, D])
        bias1 = sb("bias1", [P, D])
        we = sb("we", [P, 1])
        zero1 = sb("zero1", [P, 1])
        warm = sb("warm", [P, 1])
        ln_scale = sb("ln_scale", [P, 1])
        mhalf = sb("mhalf", [P, 8])
        gp_hi = [sb(f"gp_hi{l}", [P, WP], F32R) for l in range(2)]
        gp_lo = [sb(f"gp_lo{l}", [P, WP], F32R) for l in range(2)]
        ga_hi = [sb(f"ga_hi{l}", [P, H, P], F32R) for l in range(2)]
        ga_lo = [sb(f"ga_lo{l}", [P, H, P], F32R) for l in range(2)]
        xres = sb("xres", [P, B, NT, D])

        bn_v = cols[:, 0:8].rearrange("p (l c) -> p l c", c=4)

        with ExitStack() as tmp:
            wf = tmp.enter_context(nc.sbuf_tensor("wf", [P, NW], F32))
            gpf = [tmp.enter_context(nc.sbuf_tensor(f"gpf{l}", [P, WP], F32)) for l in range(2)]
            gw = [tmp.enter_context(nc.sbuf_tensor(f"gw{l}", [P, P], F32)) for l in range(2)]
            bd = [tmp.enter_context(nc.sbuf_tensor(f"bd{l}", [P, 2 * H], F32)) for l in range(2)]
            w_in = tmp.enter_context(nc.semaphore("w_in"))
            zeroed = tmp.enter_context(nc.semaphore("zeroed"))
            w_rounded = tmp.enter_context(nc.semaphore("w_rounded"))
            w_split = tmp.enter_context(nc.semaphore("w_split"))
            score_w = tmp.enter_context(nc.semaphore("score_w"))
            score_w_sb = tmp.enter_context(nc.semaphore("score_w_sb"))
            bn_ready = tmp.enter_context(nc.semaphore("bn_ready"))
            bn_pow = tmp.enter_context(nc.semaphore("bn_pow"))
            block = tmp.enter_context(nc.Block())
            N_ZEROED = 5
            loads = [
                (wf[:, C1:C1 + D], a["conv1_wT"]),
                (wf[:, C2:CM], a["conv2_wT"].rearrange("c k o -> c (k o)")),
                (wf[:, CM:CM + D], a["w_msgT"]),
                (wf[:, CG:CG + 384], a["w_ihT"][0:P, :]),
                (wf[:, CG + 384:CG + 768], a["w_ihT"][P:2 * P, :]),
                (wf[:, CG + 768:CG + 1152], a["w_hhT"]),
                (ident[:, :], a["ident"]),
                (cols[:, :], a["cols"]),
                (bmsg[:, :], a["b_msg"].partition_broadcast(P)),
                (bias1[:, :], a["bias1"].partition_broadcast(P)),
                (we[:, :], a["a1_w"][64:65].partition_broadcast(P)),
                (gpf[0][:, 0:D], a["w1_projT"]),
                (gpf[1][:, 0:D], a["w3"]),
                (gw[0][:, :], a["w1_proj"]),
                (gw[1][:, :], a["w3T"]),
            ]
            padded = [(wf[:, CS + 32 * r:CS + 32 * r + 3], a["w_seT"]) for r in range(3)]
            padded += [(bse[32 * r:32 * r + 3, :], a["b_se"]) for r in range(3)]
            for h in range(H):
                for side in range(2):
                    padded.append((bd[0][DH * h:DH * h + DH, side * H + h:side * H + h + 1],
                                   a["a1_w"][side * DH:(side + 1) * DH].unsqueeze(1)))
                    padded.append((bd[1][DH * h:DH * h + DH, side * H + h:side * H + h + 1],
                                   a["a3"][h * 2 * DH + side * DH:h * 2 * DH + (side + 1) * DH].unsqueeze(1)))

            @block.sync
            def _(sp):
                for dst, src in loads:
                    sp.dma_start(dst, src).then_inc(w_in, 16)
                sp.wait_ge(zeroed, N_ZEROED)
                for dst, src in padded:
                    sp.dma_start(dst, src).then_inc(w_in, 16)

            ALL_IN = 16 * (len(loads) + len(padded))

            @block.gpsimd
            def _(pool):
                pool.memset(wf[:, CS:CS + 96], 0.0).then_inc(zeroed, 1)
                pool.memset(bse[:, :], 0.0).then_inc(zeroed, 1)
                pool.memset(bd[0][:, :], 0.0).then_inc(zeroed, 1)
                pool.memset(bd[1][:, :], 0.0).then_inc(zeroed, 1)
                pool.memset(mhalf[:, :], -0.5).then_inc(zeroed, 1)
                pool.memset(zero1[:, :], 0.0)
                pool.memset(ln_scale[:, :], LOG_SCALE)
                pool.wait_ge(zeroed, N_ZEROED)
                pool.wait_ge(bn_ready, 1)
                pool.tensor_tensor(bn_t[:, :], bn_t[:, :], mhalf[:, 0:2], ALU.pow).then_inc(bn_pow, 1)

            @block.tensor
            def _(pe):
                pe.wait_ge(w_in, ALL_IN)
                for l in range(2):
                    pe.matmul(bank_a[:, 8 * l:8 * l + 8], gw[l][:, :], bd[l][:, :],
                              start=True, stop=True).then_inc(score_w, 1)

            @block.vector
            def _(dve):
                dve.wait_ge(w_in, ALL_IN)
                dve.tensor_scalar(bn_t[:, :], bn_v[:, :, 3], EPS, None, ALU.add).then_inc(bn_ready, 1)
                dve.tensor_copy(w_hi[:, :], wf[:, :]).then_inc(w_rounded, 1)
                dve.wait_ge(w_rounded, 1)
                dve.tensor_tensor(w_lo[:, :], wf[:, :], w_hi[:, :].bitcast(F32), ALU.subtract).then_inc(w_split, 1)
                dve.wait_ge(score_w, 2)
                for l in range(2):
                    dve.tensor_copy(gpf[l][:, D:WP], bank_a[:, 8 * l:8 * l + 8]).then_inc(score_w_sb, 1)
                dve.wait_ge(score_w_sb, 2)
                for l in range(2):
                    dve.tensor_copy(gp_hi[l][:, :], gpf[l][:, :]).then_inc(w_rounded, 1)
                dve.wait_ge(w_rounded, 3)
                for l in range(2):
                    dve.tensor_tensor(gp_lo[l][:, :], gpf[l][:, :], gp_hi[l][:, :].bitcast(F32),
                                      ALU.subtract).then_inc(w_split, 1)
                dve.wait_ge(w_split, 3)
                for l in range(2):
                    for src, dst in ((gp_hi, ga_hi), (gp_lo, ga_lo)):
                        dve.tensor_copy(dst[l][:, :, :],
                                        src[l][:, D:D + H].bitcast(F32).unsqueeze(2).to_broadcast([P, H, P]))
                dve.tensor_tensor(half_b[:, :], cols[:, 8:10], cols[:, 11:13], ALU.add).then_inc(bn_ready, 1)
                dve.wait_ge(bn_pow, 1)
                dve.tensor_tensor(bn_sc[:, :], bn_v[:, :, 0], bn_t[:, :], ALU.mult).then_inc(bn_ready, 1)
                dve.wait_ge(bn_ready, 3)
                dve.tensor_scalar(half_b[:, :], half_b[:, :], 0.5, None, ALU.mult)
                dve.tensor_tensor(bn_t[:, :], bn_v[:, :, 2], bn_sc[:, :], ALU.mult).then_inc(bn_ready, 1)
                dve.wait_ge(bn_ready, 4)
                dve.tensor_tensor(bn_sh[:, :], bn_v[:, :, 1], bn_t[:, :], ALU.subtract)

        class Attention:
            pass

        def attention(ctx2, l, tag, front, agg_steps):
            g = Attention()

            def s2(n, shape, dt=F32):
                return ctx2.enter_context(nc.sbuf_tensor(tag + n, shape, dt))

            def m2(n):
                return ctx2.enter_context(nc.semaphore(tag + n))
            g.l = l
            g.agg_steps = agg_steps
            g.x_bank, g.proj_bank, g.row_bank = front
            g.x_in = [s2(f"x_in{i}", [P, NT, D]) for i in range(2)]
            g.mask = [s2(f"mask{i}", [P, NT, N], F16) for i in range(2)]
            g.xt_hi, g.xt_lo = s2("xt_hi", [P, N], F32R), s2("xt_lo", [P, N], F32R)
            g.proj = s2("proj", [P, NT, WP])
            g.a_row = s2("a_row", [P, H, N])
            g.bmax, g.ball = s2("bmax", [P, H]), s2("ball", [P, H])
            g.b_rel, g.t, g.nb, g.r = (s2(n, [P, NT, H]) for n in ("b_rel", "t", "nb", "r"))
            g.xy = s2("xy", [P, NT, H, XY])
            g.xy_hi, g.xy_lo = s2("xy_hi", [P, NT, H, XY], F16), s2("xy_lo", [P, NT, H, XY], F16)
            g.s = s2("s", [P, H, NT, N], F16)
            g.masked = s2("masked", [P, NT, H, HC])
            g.num = s2("num", [P, NT, H, HC])
            g.rden = s2("rden", [P, NT, H])
            g.agg = s2("agg", [P, NT, D])
            g.xb = s2("xb", [P, NT, D])
            g.y = g.agg
            g.stats, g.mv, g.ve, g.rs = s2("stats", [P, NT, 6]), s2("mv", [P, NT, 2]), s2("ve", [P, NT]), s2("rs", [P, NT])
            g.x_ready = m2("x_ready")
            g.mask_ready = m2("mask_ready")
            g.xt_done = m2("xt_done")
            g.xt_hi_ready = m2("xt_hi_ready")
            g.xt_lo_ready = m2("xt_lo_ready")
            g.proj_done = m2("proj_done")
            g.proj_sb = m2("proj_sb")
            g.arow_done = m2("arow_done")
            g.arow_sb = m2("arow_sb")
            g.bmax_ready = m2("bmax_ready")
            g.ball_ready = m2("ball_ready")
            g.rel_ready = m2("rel_ready")
            g.small_ready = m2("small_ready")
            g.t_ready = m2("t_ready")
            g.exp_ready = m2("exp_ready")
            g.xy_ready = m2("xy_ready")
            g.hi_ready = m2("hi_ready")
            g.lo_ready = m2("lo_ready")
            g.s_built = m2("s_built")
            g.mask_mm = m2("mask_mm")
            g.s_mm = m2("s_mm")
            g.masked_sb = m2("masked_sb")
            g.num_ready = m2("num_ready")
            g.agg_ready = m2("agg_ready")
            g.xb_ready = m2("xb_ready")
            g.y_ready = m2("y_ready")
            g.stat_ready = m2("stat_ready")
            g.ve_ready = m2("ve_ready")
            g.rs_ready = m2("rs_ready")
            g.out_ready = m2("out_ready")
            return g

        def pe_transpose_x(pe, g, c, p):
            ge(pe, g.x_ready, NT * (c + 1))
            ge(pe, g.arow_sb, H * c)
            if g.x_bank is gat_bank[0]:
                ge(pe, g.num_ready, 3 * c)
            for t in range(NT):
                mm = pe.transpose(g.x_bank[:, t * P:(t + 1) * P], g.x_in[p][:, t, :], ident[:, :])
            mm.then_inc(g.xt_done, 1)

        def pe_project(pe, g, c):
            pe.wait_ge(g.xt_lo_ready, c + 1)
            for t in range(NT):
                out = g.proj_bank[t // 2][:, (t % 2) * WP:(t % 2 + 1) * WP]
                tok = slice(t * P, (t + 1) * P)
                pe.matmul(out, g.xt_lo[:, tok], gp_hi[g.l][:, :], start=True, stop=False)
                pe.matmul(out, g.xt_hi[:, tok], gp_lo[g.l][:, :], start=False, stop=False)
                mm = pe.matmul(out, g.xt_hi[:, tok], gp_hi[g.l][:, :], start=False, stop=True)
                if t % 2:
                    mm.then_inc(g.proj_done, 1)

        def pe_a_row(pe, g, c, h):
            if h >= 2:
                pe.wait_ge(g.arow_sb, H * c + h - 1)
            out = g.row_bank[h % 2]
            pe.matmul(out, ga_lo[g.l][:, h, :], g.xt_hi[:, :], start=True, stop=False)
            pe.matmul(out, ga_hi[g.l][:, h, :], g.xt_lo[:, :], start=False, stop=False)
            pe.matmul(out, ga_hi[g.l][:, h, :], g.xt_hi[:, :], start=False, stop=True).then_inc(g.arow_done, 1)

        def pe_mask_sums(pe, g, c, p):
            pe.wait_ge(g.mask_ready, c + 1)
            pe.wait_ge(g.hi_ready, c + 1)
            pe.wait_ge(g.lo_ready, c + 1)
            pe.wait_ge(g.proj_sb, 2 * c + 2)
            pe.wait_ge(g.arow_sb, H * c + H)
            ge(pe, g.num_ready, 3 * c)
            for it in range(NT):
                for jt in range(NT):
                    for part in (g.xy_lo, g.xy_hi):
                        mm = pe.matmul(gat_ps[:, it, H * XY:H * XY + H * HC],
                                       g.mask[p][:, jt, it * P:(it + 1) * P], part[:, jt, :, HC:XY],
                                       start=(jt == 0 and part is g.xy_lo), stop=(jt == NT - 1 and part is g.xy_hi),
                                       skip_group_check=True)
            mm.then_inc(g.mask_mm, 1)

        def pe_head(pe, g, c, h):
            pe.wait_ge(g.s_built, NT * H * c + NT * (h + 1))
            for it in range(NT):
                for jt in range(NT):
                    for part in (g.xy_lo, g.xy_hi):
                        mm = pe.matmul(gat_ps[:, it, h * XY:(h + 1) * XY],
                                       g.s[:, h, jt, it * P:(it + 1) * P], part[:, jt, h, :],
                                       start=False, stop=(jt == NT - 1 and part is g.xy_hi),
                                       skip_group_check=True)
            mm.then_inc(g.s_mm, 1)

        def act_round_x(act, g, c):
            act.wait_ge(g.xt_done, c + 1)
            ge(act, g.arow_done, H * c)
            act.activation(g.xt_hi[:, :], g.x_bank, ACT.Copy).then_inc(g.xt_hi_ready, 1)

        def act_projection(act, g, c):
            for k in range(2):
                act.wait_ge(g.proj_done, 2 * c + k + 1)
                if k == 0:
                    ge(act, g.xy_ready, 2 * c)
                    ge(act, g.t_ready, 2 * c)
                act.activation(g.proj[:, 2 * k:2 * k + 2, :],
                               g.proj_bank[k][:, 0:2 * WP].rearrange("p (t w) -> p t w", w=WP),
                               ACT.Copy).then_inc(g.proj_sb, 1)

        def act_a_row(act, g, c, h):
            act.wait_ge(g.arow_done, H * c + h + 1)
            ge(act, g.s_built, NT * H * (c - 1) + NT * (h + 1))
            act.activation(g.a_row[:, h, :], g.row_bank[h % 2], ACT.Copy).then_inc(g.arow_sb, 1)

        def act_exps(act, g, c):
            act.wait_ge(g.rel_ready, c + 1)
            ge(act, g.lo_ready, c)
            act.activation(g.xy[:, :, :, DH], g.b_rel[:, :, :], ACT.Exp, bias=ln_scale[:, 0:1]).then_inc(g.exp_ready, 1)
            act.activation(g.xy[:, :, :, HC + DH], g.b_rel[:, :, :], ACT.Exp, bias=ln_scale[:, 0:1],
                           scale=0.2).then_inc(g.exp_ready, 1)
            act.wait_ge(g.t_ready, 2 * c + 2)
            ge(act, g.num_ready, 3 * c)
            act.activation(g.r[:, :, :], g.t[:, :, :], ACT.Exp, scale=-0.8).then_inc(g.exp_ready, 1)

        def act_round_xy(act, g, c):
            act.wait_ge(g.xy_ready, 2 * c + 2)
            ge(act, g.s_mm, H * c)
            act.activation(g.xy_hi[:, :, :, :], g.xy[:, :, :, :], ACT.Copy).then_inc(g.hi_ready, 1)

        def act_masked(act, g, c):
            act.wait_ge(g.s_mm, H * c + H)
            act.activation(g.masked[:, :, :, :].rearrange("p t h e -> p t (h e)"),
                           gat_ps[:, :, H * XY:H * XY + H * HC], ACT.Copy).then_inc(g.masked_sb, 1)

        def pool_ball(pool, g, c):
            pool.wait_ge(g.bmax_ready, c + 1)
            ge(pool, g.t_ready, 2 * c)
            pool.nop(nofuse=True)
            pool.partition_all_reduce(g.ball[:, :], g.bmax[:, :], P, RMAX).then_inc(g.ball_ready, 1)

        def pool_xy(pool, g, c):
            pool.wait_ge(g.exp_ready, 3 * c + 2)
            pool.wait_ge(g.proj_sb, 2 * c + 2)
            pool.tensor_tensor(g.xy[:, :, :, HC:HC + DH], g.proj[:, :, 0:D].rearrange("p t (h e) -> p t h e", h=H),
                               g.xy[:, :, :, HC + DH:XY].to_broadcast([P, NT, H, DH]), ALU.mult).then_inc(g.xy_ready, 1)

        def pool_bias(pool, g, c, p):
            pool.wait_ge(g.x_ready, NT * (c + 1))
            ge(pool, g.agg_ready, 3 * c)
            pool.tensor_tensor(g.xb[:, :, :], g.x_in[p][:, :, :],
                               bias1[:, :].unsqueeze(1).to_broadcast([P, NT, D]), ALU.add).then_inc(g.xb_ready, 1)

        def pool_rstd(pool, ve, rs, ve_ready, rs_ready, c):
            pool.wait_ge(ve_ready, c + 1)
            pool.tensor_tensor(rs[:, :], ve[:, :], mhalf[:, 0:NT], ALU.pow).then_inc(rs_ready, 1)

        def dve_xt_lo(dve, g, c):
            dve.wait_ge(g.xt_hi_ready, c + 1)
            dve.tensor_tensor(g.xt_lo[:, :], g.x_bank, g.xt_hi[:, :].bitcast(F32),
                              ALU.subtract).then_inc(g.xt_lo_ready, 1)

        def dve_scores(dve, g, c, we_col):
            dve.wait_ge(g.proj_sb, 2 * c + 2)
            ge(dve, g.ball_ready, c)
            left, right = g.proj[:, :, D:D + H], g.proj[:, :, D + H:WP]
            dve.tensor_reduce(g.bmax[:, :], right.rearrange("p t h -> p h t"), AX_X, ALU.max).then_inc(g.bmax_ready, 1)
            ge(dve, g.s_built, NT * H * c)
            dve.tensor_scalar(g.nb[:, :, :], right, -1.0, we_col, ALU.mult, ALU.subtract).then_inc(g.small_ready, 1)
            dve.wait_ge(g.ball_ready, c + 1)
            ball = g.ball[:, :].unsqueeze(1).to_broadcast([P, NT, H])
            ge(dve, g.exp_ready, 3 * c)
            dve.tensor_tensor(g.b_rel[:, :, :], right, ball, ALU.subtract).then_inc(g.rel_ready, 1)
            dve.tensor_tensor(g.t[:, :, :], left, ball, ALU.add).then_inc(g.t_ready, 1)
            dve.wait_ge(g.t_ready, 2 * c + 1)
            dve.tensor_scalar(g.t[:, :, :], g.t[:, :, :], we_col, 0.0, ALU.add, ALU.max).then_inc(g.t_ready, 1)

        def dve_xy(dve, g, c):
            dve.wait_ge(g.exp_ready, 3 * c + 1)
            dve.tensor_tensor(g.xy[:, :, :, 0:DH], g.proj[:, :, 0:D].rearrange("p t (h e) -> p t h e", h=H),
                              g.xy[:, :, :, DH:HC].to_broadcast([P, NT, H, DH]), ALU.mult).then_inc(g.xy_ready, 1)

        def dve_xy_lo(dve, g, c):
            dve.wait_ge(g.hi_ready, c + 1)
            dve.tensor_tensor(g.xy_lo[:, :, :, :].rearrange("p t h e -> p (t h e)"),
                              g.xy[:, :, :, :].rearrange("p t h e -> p (t h e)"),
                              g.xy_hi[:, :, :, :].rearrange("p t h e -> p (t h e)"), ALU.subtract).then_inc(g.lo_ready, 1)

        def dve_select(dve, g, c, p, h):
            dve.wait_ge(g.small_ready, c + 1)
            dve.wait_ge(g.arow_sb, H * c + h + 1)
            dve.wait_ge(g.mask_ready, c + 1)
            ge(dve, g.s_mm, H * (c - 1) + h + 1)
            for jt in range(NT):
                dve.scalar_tensor_tensor(g.s[:, h, jt, :], g.a_row[:, h, :], g.nb[:, jt, h:h + 1],
                                         g.mask[p][:, jt, :], ALU.is_gt, ALU.mult).then_inc(g.s_built, 1)

        def dve_combine(dve, g, c):
            dve.wait_ge(g.masked_sb, c + 1)
            sums = gat_ps[:, :, 0:H * XY].rearrange("p t (h e) -> p t h e", h=H)
            dve.tensor_tensor(g.num[:, :, :, :], g.masked[:, :, :, :], sums[:, :, :, HC:XY],
                              ALU.subtract).then_inc(g.num_ready, 1)
            dve.wait_ge(g.num_ready, 3 * c + 1)
            dve.tensor_tensor(g.num[:, :, :, :], g.num[:, :, :, :],
                              g.r[:, :, :].unsqueeze(3).to_broadcast([P, NT, H, HC]), ALU.mult).then_inc(g.num_ready, 1)
            dve.wait_ge(g.num_ready, 3 * c + 2)
            dve.tensor_tensor(g.num[:, :, :, :], g.num[:, :, :, :], sums[:, :, :, 0:HC],
                              ALU.add).then_inc(g.num_ready, 1)
            dve.wait_ge(g.num_ready, 3 * c + 3)
            dve.reciprocal(g.rden[:, :, :], g.num[:, :, :, DH]).then_inc(g.agg_ready, 1)
            dve.wait_ge(g.agg_ready, g.agg_steps * c + 1)
            dve.tensor_tensor(g.agg[:, :, :].rearrange("p t (h e) -> p t h e", h=H), g.num[:, :, :, 0:DH],
                              g.rden[:, :, :].unsqueeze(3).to_broadcast([P, NT, H, DH]), ALU.mult).then_inc(g.agg_ready, 1)
            dve.wait_ge(g.agg_ready, g.agg_steps * c + 2)

        def dve_norm_stats(dve, src, stats, mv, ve, stat_ready, ve_ready, c):
            for t in range(NT):
                dve.bn_stats(stats[:, t, :], src(t)).then_inc(stat_ready, 1)
            dve.wait_ge(stat_ready, 2 * NT * c + NT)
            dve.nop(nofuse=True)
            for t in range(NT):
                dve.bn_aggr(mv[:, t, :], stats[:, t, :]).then_inc(stat_ready, 1)
            dve.wait_ge(stat_ready, 2 * NT * (c + 1))
            dve.tensor_scalar(ve[:, :], mv[:, :, 1], EPS, None, ALU.add).then_inc(ve_ready, 1)

        def dve_norm_apply(dve, src, dst, mv, rs, rs_ready, out_ready, c):
            dve.wait_ge(rs_ready, c + 1)
            for t in range(NT):
                dve.tensor_scalar(dst(t), src(t), mv[:, t, 0:1], rs[:, t:t + 1],
                                  ALU.subtract, ALU.mult).then_inc(out_ready, 1)

        with ExitStack() as tmp:
            def s3(n, shape, dt=F32):
                return tmp.enter_context(nc.sbuf_tensor(n, shape, dt))

            def m3(n):
                return tmp.enter_context(nc.semaphore(n))
            g1 = attention(tmp, 0, "g1_", (gat_bank[0], gat_bank[1:3], [gat_bank[3], gat_bank[0]]), 3)
            xT = [s3(f"xT{i}", [P, N]) for i in range(2)]
            adjT = [s3(f"adjT{i}", [P, NT, N]) for i in range(2)]
            x_hi, x_lo = s3("x_hi", [P, N], F32R), s3("x_lo", [P, N], F32R)
            h32 = s3("h32", [P, N])
            xc = h32
            h_hi, h_lo = s3("h_hi", [P, N + 2 * PAD], F32R), s3("h_lo", [P, N + 2 * PAD], F32R)
            s_l, s_r = s3("s_l", [96, N]), s3("s_r", [96, N])
            expd = s3("expd", [P, NT, N])
            msg = s3("msg", [P, NT, D])
            xc_hi, xc_lo = s3("xc_hi", [P, N], F32R), s3("xc_lo", [P, N], F32R)
            nm_hi, nm_lo = s3("nm_hi", [P, N], F32R), s3("nm_lo", [P, N], F32R)
            t_r, t_z, u, cand, diff, xn, yT = (s3(n, [P, N]) for n in
                                                  ("t_r", "t_z", "u", "cand", "diff", "xn", "yT"))
            stats, mv, ve, rs = s3("stats", [P, NT, 6]), s3("mv", [P, NT, 2]), s3("ve", [P, NT]), s3("rs", [P, NT])

            x_in = [m3("x_in0"), m3("x_in1")]
            adj_in = [m3("adj_in0"), m3("adj_in1")]
            (const_ready, x_hi_ready, x_lo_ready, conv1_done, h_ready, h_hi_ready, h_lo_ready, s_done, s_rows, l_rows,
             msg_done, msg_sum, msg_ready, dist_done, exp_done, att_ready, conv2_done, pre_ready, xc_ready, xc_hi_ready,
             xc_lo_ready, nmp_done, nm_hi_ready, nm_lo_ready, r_done, z_done, in_done, hn_done, r_ready, z_ready,
             rr_ready, u_ready, v_ready, cand_ready, diff_ready, xn_ready, w_ready, y_ready, yt_done, stat_ready,
             ve_ready, rs_ready) = (m3(n) for n in (
                 "const_ready x_hi_ready x_lo_ready conv1_done h_ready h_hi_ready h_lo_ready s_done s_rows l_rows "
                 "msg_done msg_sum msg_ready dist_done exp_done att_ready conv2_done pre_ready xc_ready xc_hi_ready "
                 "xc_lo_ready nmp_done nm_hi_ready nm_lo_ready r_done z_done in_done hn_done r_ready z_ready "
                 "rr_ready u_ready v_ready cand_ready diff_ready xn_ready w_ready y_ready yt_done stat_ready "
                 "ve_ready rs_ready").split())
            block = tmp.enter_context(nc.Block())
            LAST = B - 1
            N_CONST = 6

            def steps(eng, body):
                for b in range(4):
                    body(b, b % 2, b // 2)
                with eng.Fori(2, B // 2) as q:
                    for p in range(2):
                        body(2 * q + p, p, q)
                for b in (B, B + 1):
                    body(b, b % 2, b // 2)

            def layer0(b):
                return not isinstance(b, int) or b < B

            def norm0(b):
                return not isinstance(b, int) or 1 <= b <= B

            def layer1(b):
                return not isinstance(b, int) or b >= 2

            @block.sync
            def _(sp):
                def body(b, p, q):
                    if layer0(b):
                        ge(sp, xn_ready, b - 1)
                        row = bass.ds(b, 1)
                        sp.dma_start(xT[p][:, :], a["xT"][row].rearrange("a f n -> (a f) n")).then_inc(x_in[p], 16)
                        ge(sp, att_ready, NT * (b - 1))
                        ge(sp, g1.mask_ready, b - 1)
                        sp.dma_start(adjT[p][:, :, :],
                                     a["adjT"][row].rearrange("a (t p) n -> p (a t) n", p=P)).then_inc(adj_in[p], 16)
                steps(sp, body)

            def w(c, part):
                return (w_hi, w_lo)[part][:, c:c + D]

            def mm3(pe, out, wc, hi, lo, first, last):
                pe.matmul(out, w(wc, 1), hi, start=first, stop=False)
                pe.matmul(out, w(wc, 0), lo, start=False, stop=False)
                return pe.matmul(out, w(wc, 0), hi, start=False, stop=last)

            @block.tensor
            def _(pe):
                pe.wait_ge(const_ready, N_CONST)

                def conv2_taps(b, lo, hi):
                    for k in range(lo, hi):
                        mm = mm3(pe, bank_b[:, :], C2 + k * D, h_hi[:, k:k + N], h_lo[:, k:k + N],
                                 k == 0, k == TAPS - 1)
                    return mm

                def distance(b, t):
                    if t >= 2:
                        pe.wait_ge(exp_done, NT * b + t - 1)
                    pe.matmul((bank_c, bank_d)[t % 2][:, :], s_l[:, t * P:(t + 1) * P], s_r[:, :],
                              start=True, stop=True).then_inc(dist_done, 1)

                def body(b, p, q):
                    c = b - 2
                    if layer0(b):
                        pe.wait_ge(x_hi_ready, b + 1)
                        pe.wait_ge(x_lo_ready, b + 1)
                        ge(pe, r_ready, b)
                        mm3(pe, bank_a[:, :], C1, x_hi[:, :], x_lo[:, :], True, True).then_inc(conv1_done, 1)
                        ge(pe, z_ready, b)
                        wlo, whi = w_lo[:, CS:CS + 96], w_hi[:, CS:CS + 96]
                        pe.matmul(bank_b[0:96, :], wlo, x_hi[:, :], start=True, stop=False)
                        pe.matmul(bank_b[0:96, :], whi, x_lo[:, :], start=False, stop=False)
                        pe.matmul(bank_b[0:96, :], whi, x_hi[:, :], start=False, stop=True).then_inc(s_done, 1)
                    if layer1(b):
                        pe_transpose_x(pe, g1, c, p)
                    if layer0(b):
                        pe.wait_ge(h_ready, b + 1)
                        for t in range(NT):
                            out = bank_a[:, t * D:(t + 1) * D]
                            tok = slice(t * P, (t + 1) * P)
                            pe.matmul(out, x_lo[:, tok], w(CM, 0), start=True, stop=False)
                            pe.matmul(out, x_hi[:, tok], w(CM, 1), start=False, stop=False)
                            mm = pe.matmul(out, x_hi[:, tok], w(CM, 0), start=False, stop=True)
                        mm.then_inc(msg_done, 1)
                    if layer1(b):
                        pe_project(pe, g1, c)
                    if layer0(b):
                        pe.wait_ge(l_rows, 2 * b + 2)
                        ge(pe, v_ready, b)
                        ge(pe, u_ready, b)
                    for t in range(NT):
                        if layer0(b):
                            distance(b, t)
                        if layer1(b):
                            pe_a_row(pe, g1, c, t)
                    if layer0(b):
                        pe.wait_ge(h_hi_ready, b + 1)
                        pe.wait_ge(h_lo_ready, b + 1)
                        conv2_taps(b, 0, 9)
                    if layer1(b):
                        pe_mask_sums(pe, g1, c, p)
                        pe_head(pe, g1, c, 0)
                    if layer0(b):
                        conv2_taps(b, 9, TAPS).then_inc(conv2_done, 1)
                    if norm0(b):
                        pe.wait_ge(y_ready, b)
                        ge(pe, exp_done, NT * (b + 1) if layer0(b) else 0)
                        for t in range(NT):
                            mm = pe.transpose(bank_d[:, t * P:(t + 1) * P], yT[:, t * P:(t + 1) * P], ident[:, :])
                        mm.then_inc(yt_done, 1)
                    if layer0(b):
                        pe.wait_ge(att_ready, NT * (b + 1))
                        pe.wait_ge(msg_ready, b + 1)
                        pe.wait_ge(exp_done, NT * (b + 1))
                        for t in range(NT):
                            mm = pe.matmul(bank_c[:, :], msg[:, t, :], expd[:, t, :], start=(t == 0), stop=(t == NT - 1))
                        mm.then_inc(nmp_done, 1)
                        mm3(pe, bank_a[:, :], CG + 6 * D, x_hi[:, :], x_lo[:, :], True, False)
                    if layer1(b):
                        pe_head(pe, g1, c, 1)
                    if layer0(b):
                        pe.wait_ge(xc_hi_ready, b + 1)
                        pe.wait_ge(xc_lo_ready, b + 1)
                        mm3(pe, bank_a[:, :], CG, xc_hi[:, :], xc_lo[:, :], False, False)
                        mm3(pe, bank_b[:, :], CG + 7 * D, x_hi[:, :], x_lo[:, :], True, False)
                        mm3(pe, bank_b[:, :], CG + D, xc_hi[:, :], xc_lo[:, :], False, False)
                        pe.wait_ge(nm_lo_ready, b + 1)
                        mm3(pe, bank_a[:, :], CG + 3 * D, nm_hi[:, :], nm_lo[:, :], False, True).then_inc(r_done, 1)
                        ge(pe, g1.x_ready, NT * b)
                        mm3(pe, bank_d[:, :], CG + 8 * D, x_hi[:, :], x_lo[:, :], True, True).then_inc(hn_done, 1)
                        mm3(pe, bank_c[:, :], CG + 2 * D, xc_hi[:, :], xc_lo[:, :], True, False)
                        mm3(pe, bank_c[:, :], CG + 5 * D, nm_hi[:, :], nm_lo[:, :], False, True).then_inc(in_done, 1)
                        mm3(pe, bank_b[:, :], CG + 4 * D, nm_hi[:, :], nm_lo[:, :], False, True).then_inc(z_done, 1)
                    if layer1(b):
                        pe_head(pe, g1, c, 2)
                        pe_head(pe, g1, c, 3)
                steps(pe, body)

            @block.scalar
            def _(act):
                act.activation(warm[:, :], zero1[:, :], ACT.Exp)
                act.wait_ge(const_ready, N_CONST)

                def body(b, p, q):
                    c = b - 2
                    if layer0(b):
                        act.wait_ge(conv1_done, b + 1)
                        ge(act, xc_hi_ready, b)
                        ge(act, xc_lo_ready, b)
                        act.activation(h32[:, :], bank_a[:, :], ACT.Relu, bias=bn_sh[:, 0:1],
                                       scale=bn_sc[:, 0:1]).then_inc(h_ready, 1)
                        act.wait_ge(s_done, b + 1)
                        ge(act, dist_done, NT * b)
                        act.activation(s_r[0:32, :], bank_b[0:32, :], ACT.Identity,
                                       bias=bse[0:32, :]).then_inc(s_rows, 1)
                        act.activation(s_r[64:96, :], bank_b[64:96, :], ACT.Square,
                                       bias=bse[64:96, :]).then_inc(s_rows, 1)
                    if layer1(b):
                        act_round_x(act, g1, c)
                        act_projection(act, g1, c)
                    for t in range(NT):
                        if layer0(b):
                            act.wait_ge(dist_done, NT * b + t + 1)
                            ge(act, nmp_done, b)
                            act.activation(expd[:, t, :], (bank_c, bank_d)[t % 2][:, :], ACT.Exp).then_inc(exp_done, 1)
                        if layer1(b):
                            act_a_row(act, g1, c, t)
                            if t == 1:
                                act_exps(act, g1, c)
                            if t == 3:
                                act_round_xy(act, g1, c)
                    if layer0(b):
                        act.wait_ge(pre_ready, b + 1)
                        act.activation(xc[:, :], xc[:, :], ACT.Relu, bias=bn_sh[:, 1:2]).then_inc(xc_ready, 1)
                        act.wait_ge(nmp_done, b + 1)
                        ge(act, z_done, b)
                        act.activation(nm_hi[:, :], bank_c[:, :], ACT.Copy).then_inc(nm_hi_ready, 1)
                        act.wait_ge(r_done, b + 1)
                        ge(act, rr_ready, b)
                        act.activation(t_r[:, :], bank_a[:, :], ACT.Tanh, bias=half_b[:, 0:1],
                                       scale=0.5).then_inc(r_ready, 1)
                        act.wait_ge(z_done, b + 1)
                        ge(act, w_ready, b)
                        act.activation(t_z[:, :], bank_b[:, :], ACT.Tanh, bias=half_b[:, 1:2],
                                       scale=0.5).then_inc(z_ready, 1)
                        act.wait_ge(v_ready, b + 1)
                        ge(act, xn_ready, b)
                        act.activation(cand[:, :], u[:, :], ACT.Tanh, bias=cols[:, 10:11]).then_inc(cand_ready, 1)
                    if layer1(b):
                        act_masked(act, g1, c)
                steps(act, body)

            @block.gpsimd
            def _(pool):
                for k, (dst, value) in enumerate((
                        (s_l[:, :], 0.0), (s_r[:, :], 0.0), (s_l[64:96, :], -1.0), (s_r[32:64, :], 1.0),
                        (h_hi[:, :].bitcast(F32), 0.0), (h_lo[:, :].bitcast(F32), 0.0))):
                    ge(pool, const_ready, k)
                    pool.memset(dst, value).then_inc(const_ready, 1)
                pool.wait_ge(const_ready, N_CONST)

                def body(b, p, q):
                    c = b - 2
                    if layer0(b):
                        pool.wait_ge(x_hi_ready, b + 1)
                        ge(pool, hn_done, b)
                        pool.tensor_tensor(x_lo[:, :], xT[p][:, :], x_hi[:, :].bitcast(F32),
                                           ALU.subtract).then_inc(x_lo_ready, 1)
                        pool.wait_ge(h_hi_ready, b + 1)
                        pool.tensor_tensor(h_lo[:, PAD:PAD + N], h32[:, :], h_hi[:, PAD:PAD + N].bitcast(F32),
                                           ALU.subtract).then_inc(h_lo_ready, 1)
                    if layer1(b):
                        pool_ball(pool, g1, c)
                        pool_xy(pool, g1, c)
                    if layer0(b):
                        pool.wait_ge(adj_in[p], 16 * (q + 1))
                        for t in range(NT):
                            pool.wait_ge(exp_done, NT * b + t + 1)
                            pool.tensor_tensor(expd[:, t, :], expd[:, t, :], adjT[p][:, t, :],
                                               ALU.mult).then_inc(att_ready, 1)
                    if layer1(b):
                        pool_bias(pool, g1, c, p)
                    if layer0(b):
                        pool.wait_ge(xc_hi_ready, b + 1)
                        pool.tensor_tensor(xc_lo[:, :], xc[:, :], xc_hi[:, :].bitcast(F32),
                                           ALU.subtract).then_inc(xc_lo_ready, 1)
                    if norm0(b):
                        pool_rstd(pool, ve, rs, ve_ready, rs_ready, b - 1)
                    if layer0(b):
                        pool.wait_ge(cand_ready, b + 1)
                        ge(pool, w_ready, b)
                        pool.tensor_tensor(diff[:, :], xT[p][:, :], cand[:, :], ALU.subtract).then_inc(diff_ready, 1)
                        ge(pool, y_ready, b)
                        pool.tensor_tensor(xn[:, :], xT[p][:, :], cand[:, :], ALU.add).then_inc(xn_ready, 1)
                    if layer1(b):
                        pool_rstd(pool, g1.ve, g1.rs, g1.ve_ready, g1.rs_ready, c)
                steps(pool, body)

            @block.vector
            def _(dve):
                dve.wait_ge(const_ready, N_CONST)

                def body(b, p, q):
                    c = b - 2
                    if layer0(b):
                        dve.wait_ge(x_in[p], 16 * (q + 1))
                        ge(dve, hn_done, b)
                        ge(dve, in_done, b)
                        ge(dve, z_done, b)
                        dve.tensor_copy(x_hi[:, :], xT[p][:, :]).then_inc(x_hi_ready, 1)
                    if layer1(b):
                        dve_xt_lo(dve, g1, c)
                    if layer0(b):
                        dve.wait_ge(h_ready, b + 1)
                        ge(dve, conv2_done, b)
                        dve.tensor_copy(h_hi[:, PAD:PAD + N], h32[:, :]).then_inc(h_hi_ready, 1)
                        dve.wait_ge(s_rows, 2 * b + 2)
                        dve.tensor_scalar(s_l[0:32, :], s_r[0:32, :], 2.0, None, ALU.mult).then_inc(l_rows, 1)
                        dve.tensor_scalar(s_l[32:64, :], s_r[64:96, :], -1.0, None, ALU.mult).then_inc(l_rows, 1)
                        dve.wait_ge(msg_done, b + 1)
                        ge(dve, nmp_done, b)
                        dve.tensor_tensor(msg[:, :, :], bank_a[:, :].rearrange("p (t d) -> p t d", t=NT),
                                          bmsg[:, :].unsqueeze(1).to_broadcast([P, NT, D]), ALU.add).then_inc(msg_sum, 1)
                        dve.wait_ge(msg_sum, b + 1)
                        dve.tensor_scalar(msg[:, :, :], msg[:, :, :], 0.0, None, ALU.max).then_inc(msg_ready, 1)
                    if layer1(b):
                        dve_scores(dve, g1, c, we[:, 0:1])
                        dve_xy(dve, g1, c)
                        dve_select(dve, g1, c, p, 0)
                        dve_xy_lo(dve, g1, c)
                        dve_select(dve, g1, c, p, 1)
                    if layer0(b):
                        dve.wait_ge(conv2_done, b + 1)
                        dve.wait_ge(h_lo_ready, b + 1)
                        dve.scalar_tensor_tensor(xc[:, :], bank_b[:, :], bn_sc[:, 1:2], xT[p][:, :],
                                                 ALU.mult, ALU.add).then_inc(pre_ready, 1)
                    if layer1(b):
                        dve_select(dve, g1, c, p, 2)
                    if layer0(b):
                        dve.wait_ge(xc_ready, b + 1)
                        ge(dve, z_done, b)
                        dve.tensor_copy(xc_hi[:, :], xc[:, :]).then_inc(xc_hi_ready, 1)
                    if norm0(b):
                        dve.wait_ge(yt_done, b)
                        dve_norm_stats(dve, lambda t: bank_d[:, t * P:(t + 1) * P], stats, mv, ve,
                                       stat_ready, ve_ready, b - 1)
                    if layer0(b):
                        dve.wait_ge(nm_hi_ready, b + 1)
                        dve.tensor_tensor(nm_lo[:, :], bank_c[:, :], nm_hi[:, :].bitcast(F32),
                                          ALU.subtract).then_inc(nm_lo_ready, 1)
                    if norm0(b):
                        ge(dve, g1.y_ready, 2 * (b - 2))
                        o = 1 - p
                        dve_norm_apply(dve, lambda t: bank_d[:, t * P:(t + 1) * P], lambda t: g1.x_in[o][:, t, :],
                                       mv, rs, rs_ready, g1.x_ready, b - 1)
                    if layer1(b):
                        dve_select(dve, g1, c, p, 3)
                    if layer0(b):
                        dve.wait_ge(r_ready, b + 1)
                        dve.tensor_scalar(t_r[:, :], t_r[:, :], 0.5, 0.5, ALU.mult, ALU.add).then_inc(rr_ready, 1)
                        dve.wait_ge(hn_done, b + 1)
                        dve.wait_ge(rr_ready, b + 1)
                        dve.scalar_tensor_tensor(u[:, :], bank_d[:, :], cols[:, 13:14], t_r[:, :],
                                                 ALU.add, ALU.mult).then_inc(u_ready, 1)
                        dve.wait_ge(in_done, b + 1)
                        dve.wait_ge(u_ready, b + 1)
                        ge(dve, cand_ready, b)
                        dve.tensor_tensor(u[:, :], bank_c[:, :], u[:, :], ALU.add).then_inc(v_ready, 1)
                        if layer1(b):
                            dve.wait_ge(g1.s_built, NT * H * (c + 1))
                            dve.wait_ge(g1.mask_mm, c + 1)
                        dve.wait_ge(adj_in[p], 16 * (q + 1))
                        dve.tensor_scalar(g1.mask[p][:, :, :], adjT[p][:, :, :], 0.0, None,
                                          ALU.is_gt).then_inc(g1.mask_ready, 1)
                    if layer1(b):
                        dve_combine(dve, g1, c)
                        dve.wait_ge(g1.xb_ready, c + 1)
                        dve.tensor_tensor(g1.agg[:, :, :], g1.agg[:, :, :], g1.xb[:, :, :],
                                          ALU.add).then_inc(g1.agg_ready, 1)
                        dve.wait_ge(g1.agg_ready, 3 * c + 3)
                        dve.scalar_tensor_tensor(g1.y[:, :, :], g1.agg[:, :, :], 0.5, g1.agg[:, :, :],
                                                 ALU.mult, ALU.max).then_inc(g1.y_ready, 1)
                        dve.wait_ge(g1.y_ready, 2 * c + 1)
                        dve.tensor_tensor(g1.y[:, :, :], g1.y[:, :, :], g1.x_in[p][:, :, :],
                                          ALU.add).then_inc(g1.y_ready, 1)
                    if layer0(b):
                        dve.wait_ge(diff_ready, b + 1)
                        dve.wait_ge(z_ready, b + 1)
                        dve.scalar_tensor_tensor(u[:, :], t_z[:, :], 1.0, diff[:, :],
                                                 ALU.add, ALU.mult).then_inc(w_ready, 1)
                        dve.wait_ge(w_ready, b + 1)
                        dve.wait_ge(xn_ready, b + 1)
                        ge(dve, yt_done, b)
                        dve.scalar_tensor_tensor(yT[:, :], u[:, :], 0.5, xn[:, :],
                                                 ALU.mult, ALU.add).then_inc(y_ready, 1)
                    if layer1(b):
                        dve.wait_ge(g1.y_ready, 2 * c + 2)
                        dve_norm_stats(dve, lambda t: g1.y[:, t, :], g1.stats, g1.mv, g1.ve,
                                       g1.stat_ready, g1.ve_ready, c)
                        dve_norm_apply(dve, lambda t: g1.y[:, t, :],
                                       (lambda t: xres[:, bass.ds(c, 1), t, :].rearrange("p a d -> p (a d)")),
                                       g1.mv, g1.rs, g1.rs_ready, g1.out_ready, c)
                steps(dve, body)


        with ExitStack() as tmp:
            def s4(n, shape, dt=F32):
                return tmp.enter_context(nc.sbuf_tensor("l2_" + n, shape, dt))

            def m4(n):
                return tmp.enter_context(nc.semaphore("l2_" + n))
            l2_w1 = s4("w1", [P, GROUPS, HID])
            l2_w2 = s4("w2", [P, 2 * GROUPS, D])
            l2_b1 = s4("b1", [P, 2 * GROUPS])
            l2_b2 = s4("b2", [P, GROUPS, D])
            l2_fw = s4("fw", [P, GROUPS])
            in_group = s4("in_group", [P, GROUPS])
            adjb, adji = s4("adjb", [P, P]), s4("adji", [P, P])
            group_row = s4("group_row", [P, GROUPS, P])
            ag = s4("ag", [P, GROUPS, P])
            deg, deg0, dinv = s4("deg", [P, GROUPS]), s4("deg0", [P, GROUPS]), s4("dinv", [P, GROUPS])
            nadj = s4("nadj", [P, GROUPS, P])
            x4 = s4("x4", [P, D])
            zt = s4("zt", [P, GROUPS, P])
            ht = s4("ht", [P, 2 * GROUPS, P])
            sup = s4("sup", [P, GROUPS, D])
            og = s4("og", [P, GROUPS, D])
            acc = s4("acc", [P, D])
            back = s4("back", [SLOT, PACK, D])
            fmax, fsum = s4("fmax", [P, 1]), s4("fsum", [P, 1])
            gw_n = s4("gw_n", [P, GROUPS])
            (cleared, wts_in, adj_in2, fw_sub, fw_exp, fw_ready, chain, pow_ready, tr_done, nadj_ready, x4_ready,
             z_done2, z_sb, h_done, h_sb, sup_done, sup_sb, o_done, o_read, acc_step, back_ready, pack_done) = (
                m4(n) for n in ("cleared wts_in adj_in fw_sub fw_exp fw_ready chain pow_ready tr_done nadj_ready "
                                "x4_ready z_done z_sb h_done h_sb sup_done sup_sb o_done o_read acc_step back_ready "
                                "pack_done").split())
            block = tmp.enter_context(nc.Block())
            NPACK = B // PACK
            split = ((slice(0, 4), 4), (slice(4, 5), 1))

            loads = [
                (l2_w1[:, :, :], a["l2_w1"].rearrange("g f e -> f g e")),
                (l2_w2[:, :, :], a["l2_w2"].rearrange("g (k e) d -> e (g k) d", k=2)),
                (l2_b1[:, :], a["l2_b1T"]),
                (l2_b2[:, :, :].rearrange("p g d -> p (g d)"), a["l2_b2"].partition_broadcast(P)),
                (l2_fw[:, :], a["l2_fw"].partition_broadcast(P)),
                (in_group[:, :], a["in_group"]),
                (group_row[:, :, :].rearrange("p g n -> p (g n)"), a["group_row"].partition_broadcast(P)),
            ]

            def packs(eng, body):
                body(0)
                with eng.Fori(1, NPACK) as q:
                    body(q)

            @block.sync
            def _(sp):
                for dst, src in loads:
                    sp.dma_start(dst, src).then_inc(wts_in, 16)
                sp.wait_ge(cleared, 1)

                def body(q):
                    ge(sp, chain, 5 * q)
                    for r in range(PACK):
                        sp.dma_start(adjb[SLOT * r:SLOT * r + NODES, SLOT * r:SLOT * r + NODES],
                                     a["adj_nodes"][bass.ds(PACK * q + r, 1)].rearrange("a n m -> (a n) m")
                                     ).then_inc(adj_in2, 16)
                packs(sp, body)

            @block.gpsimd
            def _(pool):
                pool.memset(adjb[:, :], 0.0).then_inc(cleared, 1)

                def body(q):
                    pool.wait_ge(chain, 5 * q + 4)
                    pool.tensor_tensor(deg[:, :], deg[:, :], mhalf[:, 0:GROUPS], ALU.pow).then_inc(pow_ready, 1)
                packs(pool, body)

            @block.tensor
            def _(pe):
                def body(q):
                    pe.wait_ge(chain, 5 * q + 5)
                    ge(pe, sup_sb, 2 * q)
                    ge(pe, z_sb, 2 * q)
                    ge(pe, o_read, 2 * q)
                    for g in range(GROUPS):
                        mm = pe.transpose(gat_ps[:, g // 4, (g % 4) * P:(g % 4 + 1) * P], ag[:, g, :], ident[:, :])
                    mm.then_inc(tr_done, 1)
                    pe.wait_ge(x4_ready, PACK * (q + 1))
                    pe.wait_ge(nadj_ready, 2 * q + 2)
                    for k, (gs, n) in enumerate(split):
                        pe.matmul(gat_ps[:, 2 + k, 0:n * P], x4[:, :],
                                  nadj[:, gs, :].rearrange("p g n -> p (g n)"), start=True, stop=True).then_inc(z_done2, 1)
                    pe.wait_ge(z_sb, 2 * q + 2)
                    ge(pe, h_sb, 2 * GROUPS * q)
                    for i in range(2 * GROUPS):
                        g, half = i // 2, i % 2
                        pe.matmul((bank_a, bank_b, bank_c)[i // 4][:, (i % 4) * P:(i % 4 + 1) * P],
                                  l2_w1[:, g, half * P:(half + 1) * P], zt[:, g, :],
                                  start=True, stop=True).then_inc(h_done, 1)
                    pe.wait_ge(h_sb, 2 * GROUPS * (q + 1))
                    for g in range(GROUPS):
                        out = bank_d[:, g * D:(g + 1) * D] if g < 4 else gat_ps[:, 0, 0:D]
                        for half in range(2):
                            mm = pe.matmul(out, ht[:, 2 * g + half, :], l2_w2[:, 2 * g + half, :],
                                           start=(half == 0), stop=(half == 1))
                        if g >= 3:
                            mm.then_inc(sup_done, 1)
                    pe.wait_ge(sup_sb, 2 * q + 2)
                    for g in range(GROUPS):
                        mm = pe.matmul(gat_ps[:, 1 + g // 4, (g % 4) * D:(g % 4 + 1) * D], nadj[:, g, :],
                                       sup[:, g, :], start=True, stop=True)
                        if g >= 3:
                            mm.then_inc(o_done, 1)
                packs(pe, body)

            @block.scalar
            def _(act):
                act.wait_ge(fw_sub, 1)
                act.activation(l2_fw[:, :], l2_fw[:, :], ACT.Exp).then_inc(fw_exp, 1)

                def body(q):
                    for k, (gs, n) in enumerate(split):
                        act.wait_ge(z_done2, 2 * q + k + 1)
                        ge(act, h_done, 2 * GROUPS * q)
                        act.activation(zt[:, gs, :].rearrange("p g n -> p (g n)"), gat_ps[:, 2 + k, 0:n * P],
                                       ACT.Copy).then_inc(z_sb, 1)
                    ge(act, sup_done, 2 * q)
                    for i in range(2 * GROUPS):
                        act.wait_ge(h_done, 2 * GROUPS * q + min(4 * (i // 4) + 4, 2 * GROUPS))
                        act.activation(ht[:, i, :], (bank_a, bank_b, bank_c)[i // 4][:, (i % 4) * P:(i % 4 + 1) * P],
                                       ACT.Relu, bias=l2_b1[:, i:i + 1]).then_inc(h_sb, 1)
                packs(act, body)

            @block.vector
            def _(dve):
                dve.wait_ge(wts_in, 16 * len(loads))
                dve.tensor_reduce(fmax[:, :], l2_fw[:, :], AX_X, ALU.max).then_inc(fw_ready, 1)
                dve.wait_ge(fw_ready, 1)
                dve.tensor_scalar(l2_fw[:, :], l2_fw[:, :], fmax[:, 0:1], None, ALU.subtract).then_inc(fw_sub, 1)
                dve.wait_ge(fw_exp, 1)
                dve.tensor_reduce(fsum[:, :], l2_fw[:, :], AX_X, ALU.add).then_inc(fw_ready, 1)
                dve.wait_ge(fw_ready, 2)
                dve.reciprocal(fsum[:, :], fsum[:, :]).then_inc(fw_ready, 1)
                dve.wait_ge(fw_ready, 3)
                dve.scalar_tensor_tensor(gw_n[:, :], l2_fw[:, :], fsum[:, 0:1], in_group[:, :],
                                         ALU.mult, ALU.mult).then_inc(fw_ready, 1)
                dve.wait_ge(fw_ready, 4)

                def body(q):
                    dve.wait_ge(adj_in2, 16 * PACK * (q + 1))
                    dve.tensor_tensor(adji[:, :], adjb[:, :], ident[:, :], ALU.add).then_inc(chain, 1)
                    dve.wait_ge(chain, 5 * q + 1)
                    ge(dve, tr_done, q)
                    for g in range(GROUPS):
                        mm = dve.scalar_tensor_tensor(ag[:, g, :], adji[:, :], in_group[:, g:g + 1],
                                                      group_row[:, g, :], ALU.mult, ALU.mult)
                    mm.then_inc(chain, 1)
                    dve.wait_ge(chain, 5 * q + 2)
                    dve.tensor_reduce(deg[:, :], ag[:, :, :], AX_X, ALU.add).then_inc(chain, 1)
                    dve.wait_ge(chain, 5 * q + 3)
                    dve.tensor_scalar(deg0[:, :], deg[:, :], 0.0, None, ALU.is_equal).then_inc(fw_ready, 1)
                    dve.wait_ge(fw_ready, 3 * q + 5)
                    dve.tensor_tensor(deg[:, :], deg[:, :], deg0[:, :], ALU.add).then_inc(chain, 1)
                    dve.tensor_scalar(deg0[:, :], deg0[:, :], -1.0, 1.0, ALU.mult, ALU.add).then_inc(fw_ready, 1)
                    dve.wait_ge(fw_ready, 3 * q + 6)
                    dve.wait_ge(pow_ready, q + 1)
                    dve.tensor_tensor(dinv[:, :], deg[:, :], deg0[:, :], ALU.mult).then_inc(fw_ready, 1)
                    dve.wait_ge(fw_ready, 3 * q + 7)
                    dve.tensor_tensor(ag[:, :, :], ag[:, :, :], dinv[:, :].unsqueeze(2).to_broadcast([P, GROUPS, P]),
                                      ALU.mult).then_inc(chain, 1)
                    ge(dve, z_done2, 2 * q)
                    for r in range(PACK):
                        dve.tensor_copy(x4[SLOT * r:SLOT * (r + 1), :],
                                        xres[0:SLOT, bass.ds(PACK * q + r, 1), 0, :].rearrange("p a d -> p (a d)")
                                        ).then_inc(x4_ready, 1)
                    dve.wait_ge(tr_done, q + 1)
                    ge(dve, o_done, 2 * q)
                    for k, (gs, n) in enumerate(split):
                        dve.tensor_tensor(nadj[:, gs, :], gat_ps[:, k, 0:n * P].rearrange("p (g n) -> p g n", n=P),
                                          dinv[:, gs].unsqueeze(2).to_broadcast([P, n, P]),
                                          ALU.mult).then_inc(nadj_ready, 1)
                    dve.wait_ge(sup_done, 2 * q + 2)
                    dve.tensor_copy(sup[:, 0:4, :].rearrange("p g d -> p (g d)"), bank_d[:, :]).then_inc(sup_sb, 1)
                    dve.tensor_copy(sup[:, 4, :], gat_ps[:, 0, 0:D]).then_inc(sup_sb, 1)
                    dve.wait_ge(o_done, 2 * q + 2)
                    for k, (gs, n) in enumerate(split):
                        dve.tensor_tensor(og[:, gs, :], gat_ps[:, 1 + k, 0:n * D].rearrange("p (g d) -> p g d", d=D),
                                          l2_b2[:, gs, :], ALU.add).then_inc(o_read, 1)
                    dve.wait_ge(o_read, 2 * q + 2)
                    dve.tensor_scalar(og[:, :, :], og[:, :, :], 0.0, None, ALU.max).then_inc(acc_step, 1)
                    dve.wait_ge(acc_step, 6 * q + 1)
                    dve.tensor_scalar(acc[:, :], og[:, 0, :], gw_n[:, 0:1], None, ALU.mult).then_inc(acc_step, 1)
                    for g in range(1, GROUPS):
                        dve.wait_ge(acc_step, 6 * q + 1 + g)
                        dve.scalar_tensor_tensor(acc[:, :], og[:, g, :], gw_n[:, g:g + 1], acc[:, :],
                                                 ALU.mult, ALU.add).then_inc(acc_step, 1)
                    dve.wait_ge(acc_step, 6 * q + 6)
                    for r in range(PACK):
                        dve.tensor_copy(back[:, r, :], acc[SLOT * r:SLOT * (r + 1), :]).then_inc(back_ready, 1)
                    dve.wait_ge(back_ready, PACK * (q + 1))
                    for r in range(PACK):
                        row = xres[0:NODES, bass.ds(PACK * q + r, 1), 0, :].rearrange("p a d -> p (a d)")
                        dve.tensor_tensor(row, row, back[0:NODES, r, :], ALU.add).then_inc(pack_done, 1)
                packs(dve, body)

        with ExitStack() as tmp:
            def s5(n, shape, dt=F32):
                return tmp.enter_context(nc.sbuf_tensor(n, shape, dt))

            def m5(n):
                return tmp.enter_context(nc.semaphore(n))
            g3 = attention(tmp, 1, "g3_", (bank_a[:, :], [bank_b[:, :], bank_c[:, :]], [bank_d[:, :], bank_a[:, :]]), 2)
            adjT = [s5(f"c_adjT{i}", [P, NT, N]) for i in range(2)]
            out_t = [s5(f"out_t{i}", [P, NT, D]) for i in range(2)]
            stats, mv, ve, rs = (s5("c_stats", [P, NT, 6]), s5("c_mv", [P, NT, 2]), s5("c_ve", [P, NT]),
                                 s5("c_rs", [P, NT]))
            adj_in = [m5("c_adj_in0"), m5("c_adj_in1")]
            stored = [m5("stored0"), m5("stored1")]
            stat_ready, ve_ready, rs_ready = m5("c_stat_ready"), m5("c_ve_ready"), m5("c_rs_ready")
            block = tmp.enter_context(nc.Block())

            def steps(eng, body):
                for b in range(4):
                    body(b, b % 2, b // 2)
                with eng.Fori(2, B // 2) as q:
                    for p in range(2):
                        body(2 * q + p, p, q)
                body(B, 0, B // 2)

            def front(b):
                return not isinstance(b, int) or b < B

            def behind(b):
                return not isinstance(b, int) or b >= 1

            @block.sync
            def _(sp):
                def body(b, p, q):
                    if front(b):
                        ge(sp, g3.mask_ready, b - 1)
                        sp.dma_start(adjT[p][:, :, :],
                                     a["adjT"][bass.ds(b, 1)].rearrange("a (t p) n -> p (a t) n", p=P)
                                     ).then_inc(adj_in[p], 16)
                steps(sp, body)

            @block.tensor
            def _(pe):
                def body(b, p, q):
                    if front(b):
                        pe_transpose_x(pe, g3, b, p)
                        pe_project(pe, g3, b)
                        for h in range(H):
                            pe_a_row(pe, g3, b, h)
                        pe_mask_sums(pe, g3, b, p)
                        for h in range(H):
                            pe_head(pe, g3, b, h)
                steps(pe, body)

            @block.scalar
            def _(act):
                act.activation(warm[:, :], zero1[:, :], ACT.Exp)

                def store(c, p, q):
                    act.wait_ge(g3.out_ready, NT * (c + 1))
                    act.dma_start(a["out"][bass.ds(c, 1)].rearrange("a (t p) d -> p (a t) d", p=P),
                                  out_t[p][:, :, :]).then_inc(stored[p], 16)

                def body(b, p, q):
                    if front(b):
                        act_round_x(act, g3, b)
                        act_projection(act, g3, b)
                        act_a_row(act, g3, b, 0)
                        act_a_row(act, g3, b, 1)
                        act_exps(act, g3, b)
                        act_a_row(act, g3, b, 2)
                        act_a_row(act, g3, b, 3)
                        act_round_xy(act, g3, b)
                    if behind(b):
                        store(b - 1, 1 - p, q)
                    if front(b):
                        act_masked(act, g3, b)
                steps(act, body)
                for p in range(2):
                    act.wait_ge(stored[p], 16 * (B // 2))

            @block.gpsimd
            def _(pool):
                pool_rstd(pool, ve, rs, ve_ready, rs_ready, 0)

                def body(b, p, q):
                    if front(b):
                        pool_ball(pool, g3, b)
                        pool_xy(pool, g3, b)
                    if behind(b):
                        pool_rstd(pool, g3.ve, g3.rs, g3.ve_ready, g3.rs_ready, b - 1)
                    if not isinstance(b, int) or b < B - 1:
                        pool_rstd(pool, ve, rs, ve_ready, rs_ready, b + 1)
                for b in range(4):
                    body(b, b % 2, b // 2)
                with pool.Fori(2, B // 2 - 1) as q:
                    for p in range(2):
                        body(2 * q + p, p, q)
                for b in (B - 2, B - 1, B):
                    body(b, b % 2, b // 2)

            @block.vector
            def _(dve):
                def norm2(b, p, q):
                    def src(t):
                        return xres[:, bass.ds(b, 1), t, :].rearrange("p a d -> p (a d)")
                    dve_norm_stats(dve, src, stats, mv, ve, stat_ready, ve_ready, b)
                    ge(dve, g3.y_ready, b - 1)
                    dve_norm_apply(dve, src, lambda t: g3.x_in[p][:, t, :], mv, rs, rs_ready, g3.x_ready, b)

                def new_mask(b, p, q):
                    dve.wait_ge(adj_in[p], 16 * (q + 1))
                    ge(dve, g3.mask_mm, b - 1)
                    dve.tensor_scalar(g3.mask[p][:, :, :], adjT[p][:, :, :], 0.0, None,
                                      ALU.is_gt).then_inc(g3.mask_ready, 1)

                norm2(0, 0, 0)
                new_mask(0, 0, 0)

                def body(b, p, q):
                    c, o = b - 1, 1 - p
                    if front(b):
                        dve_xt_lo(dve, g3, b)
                        dve_scores(dve, g3, b, zero1[:, 0:1])
                        dve_xy(dve, g3, b)
                    if behind(b):
                        dve_combine(dve, g3, c)
                        dve.tensor_tensor(g3.y[:, :, :], g3.agg[:, :, :], g3.x_in[o][:, :, :],
                                          ALU.add).then_inc(g3.y_ready, 1)
                        dve.wait_ge(g3.y_ready, c + 1)
                        dve_norm_stats(dve, lambda t: g3.y[:, t, :], g3.stats, g3.mv, g3.ve,
                                       g3.stat_ready, g3.ve_ready, c)
                    if front(b):
                        dve_select(dve, g3, b, p, 0)
                        dve_xy_lo(dve, g3, b)
                    if behind(b):
                        ge(dve, stored[o], 16 * (q if p == 0 else q) - (16 if p == 0 else 0))
                        dve_norm_apply(dve, lambda t: g3.y[:, t, :], lambda t: out_t[o][:, t, :],
                                       g3.mv, g3.rs, g3.rs_ready, g3.out_ready, c)
                    if front(b):
                        dve_select(dve, g3, b, p, 1)
                        if not isinstance(b, int) or b < B - 1:
                            norm2(b + 1, o, q + p)
                            new_mask(b + 1, o, q + p)
                        dve_select(dve, g3, b, p, 2)
                        dve_select(dve, g3, b, p, 3)
                for b in range(4):
                    body(b, b % 2, b // 2)
                with dve.Fori(2, B // 2 - 1) as q:
                    for p in range(2):
                        body(2 * q + p, p, q)
                for b in (B - 2, B - 1, B):
                    body(b, b % 2, b // 2)


def kernel(**inputs):
    import numpy as _np
    import concourse.bacc as _bacc
    from concourse import mybir as _mybir
    from concourse.bass_utils import run_bass_kernel_spmd as _run

    x = {k: _np.asarray(v) for k, v in inputs.items()}
    p = "L0_gnn_"
    bn = [x[p + f"bn{i}_{c}"] for i in (1, 2) for c in "gbmv"]
    gate_b = [x[p + n].reshape(3, 128)[i] for n in ("b_ih", "b_hh") for i in range(3)]
    node_groups = [range(25), range(9), (0, *range(9, 15)), (6, 7, 8, 12, 13, 14), (3, 4, 5, 9, 10, 11)]
    member = _np.zeros((4, 32, 5), _np.float32)
    for g, nodes in enumerate(node_groups):
        member[:, list(nodes), g] = 1.0
    member = member.reshape(128, 5)
    arrays = {
        "xT": x["x"].transpose(0, 2, 1),
        "adjT": x["adj"].transpose(0, 2, 1),
        "adj_nodes": x["adj"][:, :25, :25],
        "conv1_wT": x[p + "conv1_w"][:, :, 0].T,
        "conv2_wT": x[p + "conv2_w"].transpose(1, 2, 0),
        "w_msgT": x[p + "w_msg"].T,
        "w_seT": x[p + "w_se"].T,
        "b_se": x[p + "b_se"].reshape(3, 1),
        "w_ihT": x[p + "w_ih"].T,
        "w_hhT": x[p + "w_hh"].T,
        "cols": _np.stack(bn + gate_b, axis=1),
        "b_msg": x[p + "b_msg"],
        "w1_proj": x["L1_gnn_W_proj"],
        "w1_projT": x["L1_gnn_W_proj"].T,
        "a1_w": x["L1_gnn_a_w"].reshape(65),
        "bias1": x["L1_gnn_bias"],
        "w3": x["L3_gnn_W"],
        "w3T": x["L3_gnn_W"].T,
        "a3": x["L3_gnn_a"].reshape(256),
        "l2_w1": x["L2_gnn_W1"],
        "l2_w2": x["L2_gnn_W2"],
        "l2_b1T": x["L2_gnn_b1"].reshape(10, 128).T,
        "l2_b2": x["L2_gnn_b2"].reshape(640),
        "l2_fw": x["L2_gnn_fusion_w"],
        "in_group": member,
        "group_row": member.T.reshape(640),
        "ident": _np.eye(128, dtype=_np.float32),
    }
    nc = _bacc.Bacc("TRN2", target_bir_lowering=False, num_devices=1)
    aps, feed = {}, {}
    for name, v in arrays.items():
        v = _np.ascontiguousarray(v)
        feed[f"in_{name}"] = v
        aps[name] = nc.dram_tensor(f"in_{name}", v.shape, _mybir.dt.from_np(v.dtype), kind="ExternalInput").ap()
    aps["out"] = nc.dram_tensor("out_0", x["x"].shape, _mybir.dt.float32, kind="ExternalOutput").ap()
    build_program(nc, aps)
    r = _run(nc, [feed], core_ids=[0])
    return r.results[0]["out_0"]
```

```python
from contextlib import ExitStack

import concourse.bass as bass
from concourse import mybir

F32 = mybir.dt.float32
F32R = mybir.dt.float32r
F16 = mybir.dt.float16
ALU = mybir.AluOpType
ACT = mybir.ActivationFunctionType
AX_X = mybir.AxisListType.X
RMAX = bass.bass_isa.ReduceOp.max

P = 128
B, N, D = 16, 512, 128
NT = N // P
TAPS, PAD = 17, 8
H, DH = 4, 32
HC = DH + 1
XY = 2 * HC
WP = D + 2 * H
NODES, SLOT, GROUPS = 25, 32, 5
POOL_HEAD = 0
PACK = P // SLOT
HID = 256
EPS = 1e-5
LOG_SCALE = 5.545177444479562
C1, C2, CM, CS, CG = 0, D, D + TAPS * D, D + TAPS * D + D, D + TAPS * D + D + 96
NW = CG + 3 * 3 * D


def build_program(nc, a):
    with ExitStack() as ctx:
        def sb(name, shape, dt=F32):
            return ctx.enter_context(nc.sbuf_tensor(name, shape, dt))

        def sem(name):
            return ctx.enter_context(nc.semaphore(name))

        def ge(eng, s, n):
            if isinstance(n, int) and n <= 0:
                return
            eng.wait_ge(s, n)

        bank_a = ctx.enter_context(nc.psum_tensor("bank_a", [P, N], F32))
        bank_b = ctx.enter_context(nc.psum_tensor("bank_b", [P, N], F32))
        bank_c = ctx.enter_context(nc.psum_tensor("bank_c", [P, N], F32))
        bank_d = ctx.enter_context(nc.psum_tensor("bank_d", [P, N], F32))
        gat_ps = ctx.enter_context(nc.psum_tensor("gat_ps", [P, NT, 512], F32))
        gat_bank = [gat_ps[:, t, :] for t in range(NT)]

        ident = sb("ident", [P, P])
        w_hi = sb("w_hi", [P, NW], F32R)
        w_lo = sb("w_lo", [P, NW], F32R)
        cols = sb("cols", [P, 14])
        bn_sc = sb("bn_sc", [P, 2])
        bn_sh = sb("bn_sh", [P, 2])
        bn_t = sb("bn_t", [P, 2])
        half_b = sb("half_b", [P, 2])
        bse = sb("bse", [96, 1])
        bmsg = sb("bmsg", [P, D])
        bias1 = sb("bias1", [P, D])
        we = sb("we", [P, 1])
        zero1 = sb("zero1", [P, 1])
        warm = sb("warm", [P, 1])
        ln_scale = sb("ln_scale", [P, 1])
        mhalf = sb("mhalf", [P, 8])
        gp_hi = [sb(f"gp_hi{l}", [P, WP], F32R) for l in range(2)]
        gp_lo = [sb(f"gp_lo{l}", [P, WP], F32R) for l in range(2)]
        ga_hi = [sb(f"ga_hi{l}", [P, H, P], F32R) for l in range(2)]
        ga_lo = [sb(f"ga_lo{l}", [P, H, P], F32R) for l in range(2)]
        xres = sb("xres", [P, B, NT, D])

        bn_v = cols[:, 0:8].rearrange("p (l c) -> p l c", c=4)

        with ExitStack() as tmp:
            wf = tmp.enter_context(nc.sbuf_tensor("wf", [P, NW], F32))
            gpf = [tmp.enter_context(nc.sbuf_tensor(f"gpf{l}", [P, WP], F32)) for l in range(2)]
            gw = [tmp.enter_context(nc.sbuf_tensor(f"gw{l}", [P, P], F32)) for l in range(2)]
            bd = [tmp.enter_context(nc.sbuf_tensor(f"bd{l}", [P, 2 * H], F32)) for l in range(2)]
            w_in = tmp.enter_context(nc.semaphore("w_in"))
            zeroed = tmp.enter_context(nc.semaphore("zeroed"))
            w_rounded = tmp.enter_context(nc.semaphore("w_rounded"))
            w_split = tmp.enter_context(nc.semaphore("w_split"))
            score_w = tmp.enter_context(nc.semaphore("score_w"))
            score_w_sb = tmp.enter_context(nc.semaphore("score_w_sb"))
            bn_ready = tmp.enter_context(nc.semaphore("bn_ready"))
            bn_pow = tmp.enter_context(nc.semaphore("bn_pow"))
            block = tmp.enter_context(nc.Block())
            N_ZEROED = 5
            loads = [
                (wf[:, C1:C1 + D], a["conv1_wT"]),
                (wf[:, C2:CM], a["conv2_wT"].rearrange("c k o -> c (k o)")),
                (wf[:, CM:CM + D], a["w_msgT"]),
                (wf[:, CG:CG + 384], a["w_ihT"][0:P, :]),
                (wf[:, CG + 384:CG + 768], a["w_ihT"][P:2 * P, :]),
                (wf[:, CG + 768:CG + 1152], a["w_hhT"]),
                (ident[:, :], a["ident"]),
                (cols[:, :], a["cols"]),
                (bmsg[:, :], a["b_msg"].partition_broadcast(P)),
                (bias1[:, :], a["bias1"].partition_broadcast(P)),
                (we[:, :], a["a1_w"][64:65].partition_broadcast(P)),
                (gpf[0][:, 0:D], a["w1_projT"]),
                (gpf[1][:, 0:D], a["w3"]),
                (gw[0][:, :], a["w1_proj"]),
                (gw[1][:, :], a["w3T"]),
            ]
            padded = [(wf[:, CS + 32 * r:CS + 32 * r + 3], a["w_seT"]) for r in range(3)]
            padded += [(bse[32 * r:32 * r + 3, :], a["b_se"]) for r in range(3)]
            for h in range(H):
                for side in range(2):
                    padded.append((bd[0][DH * h:DH * h + DH, side * H + h:side * H + h + 1],
                                   a["a1_w"][side * DH:(side + 1) * DH].unsqueeze(1)))
                    padded.append((bd[1][DH * h:DH * h + DH, side * H + h:side * H + h + 1],
                                   a["a3"][h * 2 * DH + side * DH:h * 2 * DH + (side + 1) * DH].unsqueeze(1)))

            @block.sync
            def _(sp):
                for dst, src in loads:
                    sp.dma_start(dst, src).then_inc(w_in, 16)
                sp.wait_ge(zeroed, N_ZEROED)
                for dst, src in padded:
                    sp.dma_start(dst, src).then_inc(w_in, 16)

            ALL_IN = 16 * (len(loads) + len(padded))

            @block.gpsimd
            def _(pool):
                pool.memset(wf[:, CS:CS + 96], 0.0).then_inc(zeroed, 1)
                pool.memset(bse[:, :], 0.0).then_inc(zeroed, 1)
                pool.memset(bd[0][:, :], 0.0).then_inc(zeroed, 1)
                pool.memset(bd[1][:, :], 0.0).then_inc(zeroed, 1)
                pool.memset(mhalf[:, :], -0.5).then_inc(zeroed, 1)
                pool.memset(zero1[:, :], 0.0)
                pool.memset(ln_scale[:, :], LOG_SCALE)
                pool.wait_ge(zeroed, N_ZEROED)
                pool.wait_ge(bn_ready, 1)
                pool.tensor_tensor(bn_t[:, :], bn_t[:, :], mhalf[:, 0:2], ALU.pow).then_inc(bn_pow, 1)

            @block.tensor
            def _(pe):
                pe.wait_ge(w_in, ALL_IN)
                for l in range(2):
                    pe.matmul(bank_a[:, 8 * l:8 * l + 8], gw[l][:, :], bd[l][:, :],
                              start=True, stop=True).then_inc(score_w, 1)

            @block.vector
            def _(dve):
                dve.wait_ge(w_in, ALL_IN)
                dve.tensor_scalar(bn_t[:, :], bn_v[:, :, 3], EPS, None, ALU.add).then_inc(bn_ready, 1)
                dve.tensor_copy(w_hi[:, :], wf[:, :]).then_inc(w_rounded, 1)
                dve.wait_ge(w_rounded, 1)
                dve.tensor_tensor(w_lo[:, :], wf[:, :], w_hi[:, :].bitcast(F32), ALU.subtract).then_inc(w_split, 1)
                dve.wait_ge(score_w, 2)
                for l in range(2):
                    dve.tensor_copy(gpf[l][:, D:WP], bank_a[:, 8 * l:8 * l + 8]).then_inc(score_w_sb, 1)
                dve.wait_ge(score_w_sb, 2)
                for l in range(2):
                    dve.tensor_copy(gp_hi[l][:, :], gpf[l][:, :]).then_inc(w_rounded, 1)
                dve.wait_ge(w_rounded, 3)
                for l in range(2):
                    dve.tensor_tensor(gp_lo[l][:, :], gpf[l][:, :], gp_hi[l][:, :].bitcast(F32),
                                      ALU.subtract).then_inc(w_split, 1)
                dve.wait_ge(w_split, 3)
                for l in range(2):
                    for src, dst in ((gp_hi, ga_hi), (gp_lo, ga_lo)):
                        dve.tensor_copy(dst[l][:, :, :],
                                        src[l][:, D:D + H].bitcast(F32).unsqueeze(2).to_broadcast([P, H, P]))
                dve.tensor_tensor(half_b[:, :], cols[:, 8:10], cols[:, 11:13], ALU.add).then_inc(bn_ready, 1)
                dve.wait_ge(bn_pow, 1)
                dve.tensor_tensor(bn_sc[:, :], bn_v[:, :, 0], bn_t[:, :], ALU.mult).then_inc(bn_ready, 1)
                dve.wait_ge(bn_ready, 3)
                dve.tensor_scalar(half_b[:, :], half_b[:, :], 0.5, None, ALU.mult)
                dve.tensor_tensor(bn_t[:, :], bn_v[:, :, 2], bn_sc[:, :], ALU.mult).then_inc(bn_ready, 1)
                dve.wait_ge(bn_ready, 4)
                dve.tensor_tensor(bn_sh[:, :], bn_v[:, :, 1], bn_t[:, :], ALU.subtract)

        class Attention:
            pass

        def attention(ctx2, l, tag, front, agg_steps, depth, signs):
            g = Attention()

            def s2(n, shape, dt=F32):
                return ctx2.enter_context(nc.sbuf_tensor(tag + n, shape, dt))

            def m2(n):
                return ctx2.enter_context(nc.semaphore(tag + n))
            g.l = l
            g.agg_steps = agg_steps
            g.depth = depth
            g.signs = signs
            g.x_bank, g.proj_bank, g.row_bank = front
            g.x_in = [s2(f"x_in{i}", [P, NT, D]) for i in range(1 if signs else 2)]
            g.mask = [s2(f"mask{i}", [P, NT, N], F16) for i in range(2)]
            g.xt_hi, g.xt_lo = s2("xt_hi", [P, N], F32R), s2("xt_lo", [P, N], F32R)
            g.proj = s2("proj", [P, NT, WP])
            if not signs:
                g.a_row = s2("a_row", [P, H, N])
            g.bmax, g.ball = s2("bmax", [P, H]), s2("ball", [P, H])
            g.b_rel, g.t, g.nb = (s2(n, [P, NT, H]) for n in ("b_rel", "t", "nb"))
            g.r = [s2(f"r{i}", [P, NT, H]) for i in range(depth)] * (2 // depth)
            g.xy = s2("xy", [P, NT, H, XY])
            g.xy_hi = [s2(f"xy_hi{i}", [P, NT, H, XY], F16) for i in range(depth)] * (2 // depth)
            g.xy_lo = [s2(f"xy_lo{i}", [P, NT, H, XY], F16) for i in range(depth)] * (2 // depth)
            g.s = [s2(f"s{i}", [P, H, NT, N], F16) for i in range(depth)] * (2 // depth)
            g.masked = s2("masked", [P, NT, H, HC])
            g.num = s2("num", [P, NT, H, HC])
            g.rden = s2("rden", [P, NT, H])
            g.agg = s2("agg", [P, NT, D])
            if not signs:
                g.xb = s2("xb", [P, NT, D])
            g.y = g.agg
            g.stats, g.mv, g.ve, g.rs = s2("stats", [P, NT, 6]), s2("mv", [P, NT, 2]), s2("ve", [P, NT]), s2("rs", [P, NT])
            g.x_ready = m2("x_ready")
            g.mask_ready = m2("mask_ready")
            g.xt_done = m2("xt_done")
            g.xt_hi_ready = m2("xt_hi_ready")
            g.xt_lo_ready = m2("xt_lo_ready")
            g.proj_done = m2("proj_done")
            g.proj_sb = m2("proj_sb")
            g.arow_done = m2("arow_done")
            g.arow_sb = m2("arow_sb")
            g.bmax_ready = m2("bmax_ready")
            g.ball_ready = m2("ball_ready")
            g.rel_ready = m2("rel_ready")
            g.small_ready = m2("small_ready")
            g.t_ready = m2("t_ready")
            g.exp_ready = m2("exp_ready")
            g.xy_ready = m2("xy_ready")
            g.hi_ready = m2("hi_ready")
            g.lo_ready = m2("lo_ready")
            g.s_built = m2("s_built")
            g.mask_mm = m2("mask_mm")
            g.s_mm = m2("s_mm")
            g.masked_sb = m2("masked_sb")
            g.num_ready = m2("num_ready")
            g.agg_ready = m2("agg_ready")
            g.xb_ready = m2("xb_ready")
            g.y_ready = m2("y_ready")
            g.stat_ready = m2("stat_ready")
            g.ve_ready = m2("ve_ready")
            g.rs_ready = m2("rs_ready")
            g.out_ready = m2("out_ready")
            g.sign_ready = m2("sign_ready")
            g.s_pool = m2("s_pool")
            return g

        def pe_transpose_x(pe, g, c, src):
            pe.wait_ge(g.x_ready, NT * (c + 1))
            if g.signs:
                ge(pe, g.proj_sb, 2 * c)
            else:
                ge(pe, g.arow_sb, H * c)
            if g.x_bank is gat_bank[0]:
                ge(pe, g.num_ready, 3 * c)
            for t in range(NT):
                mm = pe.transpose(g.x_bank[:, t * P:(t + 1) * P], src(t), ident[:, :])
            mm.then_inc(g.xt_done, 1)

        def pe_project(pe, g, c):
            pe.wait_ge(g.xt_lo_ready, c + 1)
            ge(pe, g.proj_sb, 2 * c)
            for t in range(NT):
                out = g.proj_bank[t // 2][:, (t % 2) * WP:(t % 2 + 1) * WP]
                tok = slice(t * P, (t + 1) * P)
                pe.matmul(out, g.xt_lo[:, tok], gp_hi[g.l][:, :], start=True, stop=False)
                pe.matmul(out, g.xt_hi[:, tok], gp_lo[g.l][:, :], start=False, stop=False)
                mm = pe.matmul(out, g.xt_hi[:, tok], gp_hi[g.l][:, :], start=False, stop=True)
                if t % 2:
                    mm.then_inc(g.proj_done, 1)

        def pe_a_row(pe, g, c, h):
            if g.signs:
                ge(pe, g.sign_ready, NT * (H * c + h - 1))
            elif h >= 2:
                pe.wait_ge(g.arow_sb, H * c + h - 1)
            out = g.row_bank[h % 2]
            pe.matmul(out, ga_lo[g.l][:, h, :], g.xt_hi[:, :], start=True, stop=False)
            pe.matmul(out, ga_hi[g.l][:, h, :], g.xt_lo[:, :], start=False, stop=False)
            pe.matmul(out, ga_hi[g.l][:, h, :], g.xt_hi[:, :], start=False, stop=True).then_inc(g.arow_done, 1)

        def pe_mask_sums(pe, g, c, p):
            pe.wait_ge(g.mask_ready, c + 1)
            pe.wait_ge(g.hi_ready, c + 1)
            pe.wait_ge(g.lo_ready, c + 1)
            if not g.signs:
                pe.wait_ge(g.proj_sb, 2 * c + 2)
                pe.wait_ge(g.arow_sb, H * c + H)
            ge(pe, g.num_ready, 3 * c)
            for it in range(NT):
                for jt in range(NT):
                    for k, part in enumerate((g.xy_lo[p], g.xy_hi[p])):
                        mm = pe.matmul(gat_ps[:, it, H * XY:H * XY + H * HC],
                                       g.mask[p][:, jt, it * P:(it + 1) * P], part[:, jt, :, HC:XY],
                                       start=(jt == 0 and k == 0), stop=(jt == NT - 1 and k == 1),
                                       skip_group_check=True)
                        if g.signs:
                            mm = pe.matmul(gat_ps[:, it, 0:H * XY].rearrange("p (h e) -> p h e", h=H)[:, :, 0:HC],
                                           g.mask[p][:, jt, it * P:(it + 1) * P], part[:, jt, :, 0:HC],
                                           start=False, stop=False, skip_group_check=True)
            mm.then_inc(g.mask_mm, 1)

        def pe_head(pe, g, c, p, h):
            if not g.signs:
                pe.wait_ge(g.s_built, NT * (H * c + h + 1))
            elif h == POOL_HEAD:
                pe.wait_ge(g.s_pool, c + 1)
            else:
                pe.wait_ge(g.s_built, (H - 1) * c + h)
            for it in range(NT):
                for jt in range(NT):
                    for k, part in enumerate((g.xy_lo[p], g.xy_hi[p])):
                        mm = pe.matmul(gat_ps[:, it, h * XY:(h + 1) * XY],
                                       g.s[p][:, h, jt, it * P:(it + 1) * P], part[:, jt, h, :],
                                       start=False, stop=(jt == NT - 1 and k == 1),
                                       skip_group_check=True)
            mm.then_inc(g.s_mm, 1)

        def act_round_x(act, g, c):
            act.wait_ge(g.xt_done, c + 1)
            ge(act, g.arow_done, H * c)
            act.activation(g.xt_hi[:, :], g.x_bank, ACT.Copy).then_inc(g.xt_hi_ready, 1)

        def act_projection(act, g, c):
            for k in range(2):
                act.wait_ge(g.proj_done, 2 * c + k + 1)
                if k == 0:
                    ge(act, g.xy_ready, 2 * c)
                    ge(act, g.t_ready, 2 * c)
                    if g.signs:
                        ge(act, g.sign_ready, NT * H * c)
                act.activation(g.proj[:, 2 * k:2 * k + 2, :],
                               g.proj_bank[k][:, 0:2 * WP].rearrange("p (t w) -> p t w", w=WP),
                               ACT.Copy).then_inc(g.proj_sb, 1)

        def act_a_row(act, g, c, h):
            act.wait_ge(g.arow_done, H * c + h + 1)
            ge(act, g.s_built, NT * H * (c - 1) + NT * (h + 1))
            act.activation(g.a_row[:, h, :], g.row_bank[h % 2], ACT.Copy).then_inc(g.arow_sb, 1)

        def act_signs(act, g, c, p, h):
            act.wait_ge(g.arow_done, H * c + h + 1)
            act.wait_ge(g.proj_sb, 2 * c + 2)
            ge(act, g.s_mm, H * (c - g.depth) + h + 1)
            for jt in range(NT):
                act.activation(g.s[p][:, h, jt, :], g.row_bank[h % 2], ACT.Sign,
                               bias=g.proj[:, jt, D + H + h:D + H + h + 1]).then_inc(g.sign_ready, 1)

        def act_exps(act, g, c, p):
            act.wait_ge(g.rel_ready, c + 1)
            ge(act, g.lo_ready, c)
            act.activation(g.xy[:, :, :, DH], g.b_rel[:, :, :], ACT.Exp, bias=ln_scale[:, 0:1]).then_inc(g.exp_ready, 1)
            act.activation(g.xy[:, :, :, HC + DH], g.b_rel[:, :, :], ACT.Exp, bias=ln_scale[:, 0:1],
                           scale=0.2).then_inc(g.exp_ready, 1)
            act.wait_ge(g.t_ready, 2 * c + 2)
            ge(act, g.num_ready, 3 * (c - g.depth + 1))
            act.activation(g.r[p][:, :, :], g.t[:, :, :], ACT.Exp, scale=-0.8).then_inc(g.exp_ready, 1)

        def act_round_xy(act, g, c, p):
            act.wait_ge(g.xy_ready, 2 * c + 2)
            ge(act, g.s_mm, H * (c - g.depth + 1))
            act.activation(g.xy_hi[p][:, :, :, :], g.xy[:, :, :, :], ACT.Copy).then_inc(g.hi_ready, 1)

        def act_masked(act, g, c):
            act.wait_ge(g.s_mm, H * c + H)
            act.activation(g.masked[:, :, :, :].rearrange("p t h e -> p t (h e)"),
                           gat_ps[:, :, H * XY:H * XY + H * HC], ACT.Copy).then_inc(g.masked_sb, 1)

        def pool_ball(pool, g, c):
            pool.wait_ge(g.bmax_ready, c + 1)
            ge(pool, g.t_ready, 2 * c)
            pool.nop(nofuse=True)
            pool.partition_all_reduce(g.ball[:, :], g.bmax[:, :], P, RMAX).then_inc(g.ball_ready, 1)

        def pool_xy(pool, g, c):
            pool.wait_ge(g.exp_ready, 3 * c + 2)
            pool.wait_ge(g.proj_sb, 2 * c + 2)
            pool.tensor_tensor(g.xy[:, :, :, HC:HC + DH], g.proj[:, :, 0:D].rearrange("p t (h e) -> p t h e", h=H),
                               g.xy[:, :, :, HC + DH:XY].to_broadcast([P, NT, H, DH]), ALU.mult).then_inc(g.xy_ready, 1)

        def pool_bias(pool, g, c, p):
            pool.wait_ge(g.x_ready, NT * (c + 1))
            ge(pool, g.agg_ready, 3 * c)
            pool.tensor_tensor(g.xb[:, :, :], g.x_in[p][:, :, :],
                               bias1[:, :].unsqueeze(1).to_broadcast([P, NT, D]), ALU.add).then_inc(g.xb_ready, 1)

        def pool_rstd(pool, ve, rs, ve_ready, rs_ready, c):
            pool.wait_ge(ve_ready, c + 1)
            pool.tensor_tensor(rs[:, :], ve[:, :], mhalf[:, 0:NT], ALU.pow).then_inc(rs_ready, 1)

        def dve_xt_lo(dve, g, c):
            dve.wait_ge(g.xt_hi_ready, c + 1)
            dve.tensor_tensor(g.xt_lo[:, :], g.x_bank, g.xt_hi[:, :].bitcast(F32),
                              ALU.subtract).then_inc(g.xt_lo_ready, 1)

        def dve_scores(dve, g, c, we_col):
            dve.wait_ge(g.proj_sb, 2 * c + 2)
            ge(dve, g.ball_ready, c)
            left, right = g.proj[:, :, D:D + H], g.proj[:, :, D + H:WP]
            dve.tensor_reduce(g.bmax[:, :], right.rearrange("p t h -> p h t"), AX_X, ALU.max).then_inc(g.bmax_ready, 1)
            if not g.signs:
                ge(dve, g.s_built, NT * H * c)
                dve.tensor_scalar(g.nb[:, :, :], right, -1.0, we_col, ALU.mult, ALU.subtract).then_inc(g.small_ready, 1)
            dve.wait_ge(g.ball_ready, c + 1)
            ball = g.ball[:, :].unsqueeze(1).to_broadcast([P, NT, H])
            ge(dve, g.exp_ready, 3 * c)
            dve.tensor_tensor(g.b_rel[:, :, :], right, ball, ALU.subtract).then_inc(g.rel_ready, 1)
            dve.tensor_tensor(g.t[:, :, :], left, ball, ALU.add).then_inc(g.t_ready, 1)
            dve.wait_ge(g.t_ready, 2 * c + 1)
            dve.tensor_scalar(g.t[:, :, :], g.t[:, :, :], we_col, 0.0, ALU.add, ALU.max).then_inc(g.t_ready, 1)

        def dve_xy(dve, g, c):
            dve.wait_ge(g.exp_ready, 3 * c + 1)
            dve.tensor_tensor(g.xy[:, :, :, 0:DH], g.proj[:, :, 0:D].rearrange("p t (h e) -> p t h e", h=H),
                              g.xy[:, :, :, DH:HC].to_broadcast([P, NT, H, DH]), ALU.mult).then_inc(g.xy_ready, 1)

        def split_xy(eng, g, c, p):
            eng.wait_ge(g.hi_ready, c + 1)
            ge(eng, g.s_mm, H * (c - g.depth + 1))
            eng.tensor_tensor(g.xy_lo[p][:, :, :, :].rearrange("p t h e -> p (t h e)"),
                              g.xy[:, :, :, :].rearrange("p t h e -> p (t h e)"),
                              g.xy_hi[p][:, :, :, :].rearrange("p t h e -> p (t h e)"), ALU.subtract).then_inc(g.lo_ready, 1)

        def dve_select(dve, g, c, p, h):
            dve.wait_ge(g.small_ready, c + 1)
            dve.wait_ge(g.arow_sb, H * c + h + 1)
            dve.wait_ge(g.mask_ready, c + 1)
            ge(dve, g.s_mm, H * (c - 1) + h + 1)
            for jt in range(NT):
                dve.scalar_tensor_tensor(g.s[p][:, h, jt, :], g.a_row[:, h, :], g.nb[:, jt, h:h + 1],
                                         g.mask[p][:, jt, :], ALU.is_gt, ALU.mult).then_inc(g.s_built, 1)

        def mask_signs(eng, g, c, p, h, done):
            eng.wait_ge(g.sign_ready, NT * (H * c + h + 1))
            eng.wait_ge(g.mask_ready, c + 1)
            eng.tensor_tensor(g.s[p][:, h, :, :].rearrange("p t n -> p (t n)"), g.s[p][:, h, :, :].rearrange("p t n -> p (t n)"),
                              g.mask[p][:, :, :].rearrange("p t n -> p (t n)"), ALU.mult).then_inc(done, 1)

        def dve_sums(dve, g, c, p):
            dve.wait_ge(g.masked_sb, c + 1)
            sums = gat_ps[:, :, 0:H * XY].rearrange("p t (h e) -> p t h e", h=H)
            dve.tensor_tensor(g.num[:, :, :, :], g.masked[:, :, :, :], sums[:, :, :, HC:XY],
                              ALU.subtract).then_inc(g.num_ready, 1)
            dve.wait_ge(g.num_ready, 3 * c + 1)
            dve.tensor_tensor(g.num[:, :, :, :], g.num[:, :, :, :],
                              g.r[p][:, :, :].unsqueeze(3).to_broadcast([P, NT, H, HC]), ALU.mult).then_inc(g.num_ready, 1)
            dve.wait_ge(g.num_ready, 3 * c + 2)
            dve.tensor_tensor(g.num[:, :, :, :], g.num[:, :, :, :], sums[:, :, :, 0:HC],
                              ALU.add).then_inc(g.num_ready, 1)

        def dve_quotient(dve, g, c):
            dve.wait_ge(g.num_ready, 3 * c + 3)
            dve.reciprocal(g.rden[:, :, :], g.num[:, :, :, DH]).then_inc(g.agg_ready, 1)
            dve.wait_ge(g.agg_ready, g.agg_steps * c + 1)
            if g.signs:
                ge(dve, g.out_ready, NT * c)
            dve.tensor_tensor(g.agg[:, :, :].rearrange("p t (h e) -> p t h e", h=H), g.num[:, :, :, 0:DH],
                              g.rden[:, :, :].unsqueeze(3).to_broadcast([P, NT, H, DH]), ALU.mult).then_inc(g.agg_ready, 1)
            dve.wait_ge(g.agg_ready, g.agg_steps * c + 2)

        def dve_norm_stats(dve, src, stats, mv, ve, stat_ready, ve_ready, c):
            for t in range(NT):
                dve.bn_stats(stats[:, t, :], src(t)).then_inc(stat_ready, 1)
            dve.wait_ge(stat_ready, 2 * NT * c + NT)
            dve.nop(nofuse=True)
            for t in range(NT):
                dve.bn_aggr(mv[:, t, :], stats[:, t, :]).then_inc(stat_ready, 1)
            dve.wait_ge(stat_ready, 2 * NT * (c + 1))
            dve.tensor_scalar(ve[:, :], mv[:, :, 1], EPS, None, ALU.add).then_inc(ve_ready, 1)

        def dve_norm_apply(dve, src, dst, mv, rs, rs_ready, out_ready, c):
            dve.wait_ge(rs_ready, c + 1)
            for t in range(NT):
                dve.tensor_scalar(dst(t), src(t), mv[:, t, 0:1], rs[:, t:t + 1],
                                  ALU.subtract, ALU.mult).then_inc(out_ready, 1)

        with ExitStack() as tmp:
            def s3(n, shape, dt=F32):
                return tmp.enter_context(nc.sbuf_tensor(n, shape, dt))

            def m3(n):
                return tmp.enter_context(nc.semaphore(n))
            g1 = attention(tmp, 0, "g1_", (gat_bank[0], gat_bank[1:3], [gat_bank[3], gat_bank[0]]), 3, 1, False)
            xT = [s3(f"xT{i}", [P, N]) for i in range(2)]
            adjT = [s3(f"adjT{i}", [P, NT, N]) for i in range(2)]
            xs_hi = [s3(f"x_hi{i}", [P, N], F32R) for i in range(2)]
            xs_lo = [s3(f"x_lo{i}", [P, N], F32R) for i in range(2)]
            h32 = s3("h32", [P, N])
            xc = h32
            h_hi, h_lo = s3("h_hi", [P, N + 2 * PAD], F32R), s3("h_lo", [P, N + 2 * PAD], F32R)
            s_l, s_r = s3("s_l", [96, N]), s3("s_r", [96, N])
            expd = s3("expd", [P, NT, N])
            msg = s3("msg", [P, NT, D])
            xc_hi, xc_lo = s3("xc_hi", [P, N], F32R), s3("xc_lo", [P, N], F32R)
            nm_hi, nm_lo = s3("nm_hi", [P, N], F32R), s3("nm_lo", [P, N], F32R)
            t_r, t_z, u, cand, diff, xn, yT = (s3(n, [P, N]) for n in
                                                  ("t_r", "t_z", "u", "cand", "diff", "xn", "yT"))
            stats, mv, ve, rs = s3("stats", [P, NT, 6]), s3("mv", [P, NT, 2]), s3("ve", [P, NT]), s3("rs", [P, NT])

            x_in = [m3("x_in0"), m3("x_in1")]
            adj_in = [m3("adj_in0"), m3("adj_in1")]
            (const_ready, x_hi_ready, x_lo_ready, conv1_done, h_ready, h_hi_ready, h_lo_ready, s_done, s_rows, l_rows,
             msg_done, msg_sum, msg_ready, dist_done, exp_done, att_ready, conv2_done, pre_ready, xc_ready, xc_hi_ready,
             xc_lo_ready, nmp_done, nm_hi_ready, nm_lo_ready, r_done, z_done, in_done, hn_done, r_ready, z_ready,
             rr_ready, u_ready, v_ready, cand_ready, diff_ready, xn_ready, w_ready, y_ready, yt_done, stat_ready,
             ve_ready, rs_ready) = (m3(n) for n in (
                 "const_ready x_hi_ready x_lo_ready conv1_done h_ready h_hi_ready h_lo_ready s_done s_rows l_rows "
                 "msg_done msg_sum msg_ready dist_done exp_done att_ready conv2_done pre_ready xc_ready xc_hi_ready "
                 "xc_lo_ready nmp_done nm_hi_ready nm_lo_ready r_done z_done in_done hn_done r_ready z_ready "
                 "rr_ready u_ready v_ready cand_ready diff_ready xn_ready w_ready y_ready yt_done stat_ready "
                 "ve_ready rs_ready").split())
            block = tmp.enter_context(nc.Block())
            LAST = B - 1
            N_CONST = 6

            def steps(eng, body):
                for b in range(4):
                    body(b, b % 2, b // 2)
                with eng.Fori(2, B // 2 - 1) as q:
                    for p in range(2):
                        body(2 * q + p, p, q)
                for b in range(B - 2, B + 3):
                    body(b, b % 2, b // 2)

            def works(b, first, last):
                return not isinstance(b, int) or first <= b <= last

            def layer0(b):
                return works(b, 0, B - 1)

            def more0(b):
                return works(b, 0, B - 2)

            def norm0(b):
                return works(b, 1, B)

            def layer1(b):
                return works(b, 2, B + 1)

            def norm1(b):
                return works(b, 3, B + 2)

            @block.sync
            def _(sp):
                def body(b, p, q):
                    if layer0(b):
                        row = bass.ds(b, 1)
                        ge(sp, xn_ready, b - 1)
                        sp.dma_start(xT[p][:, :], a["xT"][row].rearrange("a f n -> (a f) n")).then_inc(x_in[p], 16)
                        ge(sp, att_ready, NT * (b - 1))
                        ge(sp, g1.mask_ready, b - 1)
                        sp.dma_start(adjT[p][:, :, :],
                                     a["adjT"][row].rearrange("a (t p) n -> p (a t) n", p=P)).then_inc(adj_in[p], 16)
                steps(sp, body)

            def w(c, part):
                return (w_hi, w_lo)[part][:, c:c + D]

            def mm3(pe, out, wc, hi, lo, first, last):
                pe.matmul(out, w(wc, 1), hi, start=first, stop=False)
                pe.matmul(out, w(wc, 0), lo, start=False, stop=False)
                return pe.matmul(out, w(wc, 0), hi, start=False, stop=last)

            @block.tensor
            def _(pe):
                pe.wait_ge(const_ready, N_CONST)

                def conv2_taps(b, lo, hi):
                    for k in range(lo, hi):
                        mm = mm3(pe, bank_b[:, :], C2 + k * D, h_hi[:, k:k + N], h_lo[:, k:k + N],
                                 k == 0, k == TAPS - 1)
                    return mm

                def distance(b, t):
                    if t >= 2:
                        pe.wait_ge(exp_done, NT * b + t - 1)
                    pe.matmul((bank_c, bank_d)[t % 2][:, :], s_l[:, t * P:(t + 1) * P], s_r[:, :],
                              start=True, stop=True).then_inc(dist_done, 1)

                def body(b, p, q):
                    c = b - 2
                    x_hi, x_lo = xs_hi[p], xs_lo[p]
                    if layer0(b):
                        pe.wait_ge(x_hi_ready, b + 1)
                        pe.wait_ge(x_lo_ready, b + 1)
                        ge(pe, r_ready, b)
                        mm3(pe, bank_a[:, :], C1, x_hi[:, :], x_lo[:, :], True, True).then_inc(conv1_done, 1)
                        ge(pe, z_ready, b)
                        wlo, whi = w_lo[:, CS:CS + 96], w_hi[:, CS:CS + 96]
                        pe.matmul(bank_b[0:96, :], wlo, x_hi[:, :], start=True, stop=False)
                        pe.matmul(bank_b[0:96, :], whi, x_lo[:, :], start=False, stop=False)
                        pe.matmul(bank_b[0:96, :], whi, x_hi[:, :], start=False, stop=True).then_inc(s_done, 1)
                        pe.wait_ge(h_ready, b + 1)
                        for t in range(NT):
                            out = bank_a[:, t * D:(t + 1) * D]
                            tok = slice(t * P, (t + 1) * P)
                            pe.matmul(out, x_lo[:, tok], w(CM, 0), start=True, stop=False)
                            pe.matmul(out, x_hi[:, tok], w(CM, 1), start=False, stop=False)
                            mm = pe.matmul(out, x_hi[:, tok], w(CM, 0), start=False, stop=True)
                        mm.then_inc(msg_done, 1)
                        pe.wait_ge(l_rows, 2 * b + 2)
                        ge(pe, v_ready, b)
                        ge(pe, u_ready, b)
                        distance(b, 0)
                        distance(b, 1)
                    if layer1(b):
                        pe_transpose_x(pe, g1, c, lambda t: g1.x_in[p][:, t, :])
                    if layer0(b):
                        distance(b, 2)
                        distance(b, 3)
                    if layer1(b):
                        pe_project(pe, g1, c)
                        pe_a_row(pe, g1, c, 0)
                        pe_a_row(pe, g1, c, 1)
                    if layer0(b):
                        pe.wait_ge(h_hi_ready, b + 1)
                        pe.wait_ge(h_lo_ready, b + 1)
                        conv2_taps(b, 0, 2)
                    if layer1(b):
                        pe_a_row(pe, g1, c, 2)
                        pe_a_row(pe, g1, c, 3)
                    if layer0(b):
                        conv2_taps(b, 2, TAPS).then_inc(conv2_done, 1)
                    if layer1(b):
                        pe_mask_sums(pe, g1, c, p)
                        pe_head(pe, g1, c, p, 0)
                    if norm0(b):
                        pe.wait_ge(y_ready, b)
                        ge(pe, exp_done, NT * (b + 1) if layer0(b) else 0)
                        for t in range(NT):
                            mm = pe.transpose(bank_d[:, t * P:(t + 1) * P], yT[:, t * P:(t + 1) * P], ident[:, :])
                        mm.then_inc(yt_done, 1)
                    if layer0(b):
                        pe.wait_ge(att_ready, NT * (b + 1))
                        pe.wait_ge(msg_ready, b + 1)
                        pe.wait_ge(exp_done, NT * (b + 1))
                        for t in range(NT):
                            mm = pe.matmul(bank_c[:, :], msg[:, t, :], expd[:, t, :], start=(t == 0), stop=(t == NT - 1))
                        mm.then_inc(nmp_done, 1)
                        mm3(pe, bank_a[:, :], CG + 6 * D, x_hi[:, :], x_lo[:, :], True, False)
                    if layer1(b):
                        pe_head(pe, g1, c, p, 1)
                    if layer0(b):
                        pe.wait_ge(xc_hi_ready, b + 1)
                        pe.wait_ge(xc_lo_ready, b + 1)
                        mm3(pe, bank_a[:, :], CG, xc_hi[:, :], xc_lo[:, :], False, False)
                        mm3(pe, bank_b[:, :], CG + 7 * D, x_hi[:, :], x_lo[:, :], True, False)
                        mm3(pe, bank_b[:, :], CG + D, xc_hi[:, :], xc_lo[:, :], False, False)
                    if layer1(b):
                        pe_head(pe, g1, c, p, 2)
                    if layer0(b):
                        pe.wait_ge(nm_lo_ready, b + 1)
                        mm3(pe, bank_a[:, :], CG + 3 * D, nm_hi[:, :], nm_lo[:, :], False, True).then_inc(r_done, 1)
                        ge(pe, g1.x_ready, NT * b)
                        mm3(pe, bank_d[:, :], CG + 8 * D, x_hi[:, :], x_lo[:, :], True, True).then_inc(hn_done, 1)
                        mm3(pe, bank_c[:, :], CG + 2 * D, xc_hi[:, :], xc_lo[:, :], True, False)
                        mm3(pe, bank_c[:, :], CG + 5 * D, nm_hi[:, :], nm_lo[:, :], False, True).then_inc(in_done, 1)
                        mm3(pe, bank_b[:, :], CG + 4 * D, nm_hi[:, :], nm_lo[:, :], False, True).then_inc(z_done, 1)
                    if layer1(b):
                        pe_head(pe, g1, c, p, 3)
                steps(pe, body)

            @block.scalar
            def _(act):
                act.activation(warm[:, :], zero1[:, :], ACT.Exp)
                act.wait_ge(const_ready, N_CONST)

                def body(b, p, q):
                    c = b - 2

                    def distances_exp(t):
                        act.wait_ge(dist_done, NT * b + t + 1)
                        ge(act, nmp_done, b)
                        act.activation(expd[:, t, :], (bank_c, bank_d)[t % 2][:, :], ACT.Exp).then_inc(exp_done, 1)
                    if layer0(b):
                        act.wait_ge(conv1_done, b + 1)
                        ge(act, xc_hi_ready, b)
                        ge(act, xc_lo_ready, b)
                        act.activation(h32[:, :], bank_a[:, :], ACT.Relu, bias=bn_sh[:, 0:1],
                                       scale=bn_sc[:, 0:1]).then_inc(h_ready, 1)
                        act.wait_ge(s_done, b + 1)
                        ge(act, dist_done, NT * b)
                        act.activation(s_r[0:32, :], bank_b[0:32, :], ACT.Identity,
                                       bias=bse[0:32, :]).then_inc(s_rows, 1)
                        act.activation(s_r[64:96, :], bank_b[64:96, :], ACT.Square,
                                       bias=bse[64:96, :]).then_inc(s_rows, 1)
                    if norm1(b):
                        act_masked(act, g1, c - 1)
                    if layer0(b):
                        distances_exp(0)
                        distances_exp(1)
                    if layer1(b):
                        act_round_x(act, g1, c)
                    if layer0(b):
                        distances_exp(2)
                        distances_exp(3)
                    if layer1(b):
                        act_projection(act, g1, c)
                        act_a_row(act, g1, c, 0)
                        act_a_row(act, g1, c, 1)
                        act_exps(act, g1, c, p)
                        act_a_row(act, g1, c, 2)
                        act_a_row(act, g1, c, 3)
                        act_round_xy(act, g1, c, p)
                    if layer0(b):
                        act.wait_ge(pre_ready, b + 1)
                        act.activation(xc[:, :], xc[:, :], ACT.Relu, bias=bn_sh[:, 1:2]).then_inc(xc_ready, 1)
                        act.wait_ge(nmp_done, b + 1)
                        ge(act, z_done, b)
                        act.activation(nm_hi[:, :], bank_c[:, :], ACT.Copy).then_inc(nm_hi_ready, 1)
                        act.wait_ge(r_done, b + 1)
                        ge(act, u_ready, b)
                        act.activation(t_r[:, :], bank_a[:, :], ACT.Tanh, bias=half_b[:, 0:1],
                                       scale=0.5).then_inc(r_ready, 1)
                        act.wait_ge(z_done, b + 1)
                        ge(act, w_ready, b)
                        act.activation(t_z[:, :], bank_b[:, :], ACT.Tanh, bias=half_b[:, 1:2],
                                       scale=0.5).then_inc(z_ready, 1)
                        act.wait_ge(v_ready, b + 1)
                        ge(act, xn_ready, b)
                        act.activation(cand[:, :], u[:, :], ACT.Tanh, bias=cols[:, 10:11]).then_inc(cand_ready, 1)
                steps(act, body)

            @block.gpsimd
            def _(pool):
                for k, (dst, value) in enumerate((
                        (s_l[:, :], 0.0), (s_r[:, :], 0.0), (s_l[64:96, :], -1.0), (s_r[32:64, :], 1.0),
                        (h_hi[:, :].bitcast(F32), 0.0), (h_lo[:, :].bitcast(F32), 0.0))):
                    ge(pool, const_ready, k)
                    pool.memset(dst, value).then_inc(const_ready, 1)
                pool.wait_ge(const_ready, N_CONST)

                def split_x(b, p):
                    pool.wait_ge(x_hi_ready, b + 1)
                    ge(pool, z_done, b - 1)
                    pool.tensor_tensor(xs_lo[p][:, :], xT[p][:, :], xs_hi[p][:, :].bitcast(F32),
                                       ALU.subtract).then_inc(x_lo_ready, 1)

                def body(b, p, q):
                    c, o = b - 2, 1 - p
                    if layer0(b):
                        pool.wait_ge(h_hi_ready, b + 1)
                        pool.tensor_tensor(h_lo[:, PAD:PAD + N], h32[:, :], h_hi[:, PAD:PAD + N].bitcast(F32),
                                           ALU.subtract).then_inc(h_lo_ready, 1)
                    if norm0(b):
                        pool.wait_ge(cand_ready, b)
                        ge(pool, w_ready, b - 1)
                        pool.tensor_tensor(diff[:, :], xT[o][:, :], cand[:, :], ALU.subtract).then_inc(diff_ready, 1)
                        ge(pool, y_ready, b - 1)
                        pool.tensor_tensor(xn[:, :], xT[o][:, :], cand[:, :], ALU.add).then_inc(xn_ready, 1)
                    if layer1(b):
                        pool_ball(pool, g1, c)
                        pool_xy(pool, g1, c)
                    if norm1(b):
                        pool_rstd(pool, g1.ve, g1.rs, g1.ve_ready, g1.rs_ready, c - 1)
                    if layer0(b):
                        pool.wait_ge(adj_in[p], 16 * (q + 1))
                        for t in range(NT):
                            pool.wait_ge(exp_done, NT * b + t + 1)
                            pool.tensor_tensor(expd[:, t, :], expd[:, t, :], adjT[p][:, t, :],
                                               ALU.mult).then_inc(att_ready, 1)
                    if layer1(b):
                        pool_bias(pool, g1, c, p)
                    if layer0(b):
                        pool.wait_ge(xc_hi_ready, b + 1)
                        pool.tensor_tensor(xc_lo[:, :], xc[:, :], xc_hi[:, :].bitcast(F32),
                                           ALU.subtract).then_inc(xc_lo_ready, 1)
                    if norm0(b):
                        pool_rstd(pool, ve, rs, ve_ready, rs_ready, b - 1)
                    if more0(b):
                        split_x(b + 1, o)
                split_x(0, 0)
                steps(pool, body)

            @block.vector
            def _(dve):
                dve.wait_ge(const_ready, N_CONST)

                def split_x(b, p, q):
                    dve.wait_ge(x_in[p], 16 * (q + 1))
                    ge(dve, z_done, b - 1)
                    dve.tensor_copy(xs_hi[p][:, :], xT[p][:, :]).then_inc(x_hi_ready, 1)

                def body(b, p, q):
                    c, e, o = b - 2, b - 3, 1 - p
                    if layer0(b):
                        dve.wait_ge(h_ready, b + 1)
                        ge(dve, conv2_done, b)
                        dve.tensor_copy(h_hi[:, PAD:PAD + N], h32[:, :]).then_inc(h_hi_ready, 1)
                        dve.wait_ge(s_rows, 2 * b + 2)
                        dve.tensor_scalar(s_l[0:32, :], s_r[0:32, :], 2.0, None, ALU.mult).then_inc(l_rows, 1)
                        dve.tensor_scalar(s_l[32:64, :], s_r[64:96, :], -1.0, None, ALU.mult).then_inc(l_rows, 1)
                    if norm1(b):
                        dve_sums(dve, g1, e, o)
                    if layer0(b):
                        dve.wait_ge(msg_done, b + 1)
                        ge(dve, nmp_done, b)
                        dve.tensor_tensor(msg[:, :, :], bank_a[:, :].rearrange("p (t d) -> p t d", t=NT),
                                          bmsg[:, :].unsqueeze(1).to_broadcast([P, NT, D]), ALU.add).then_inc(msg_sum, 1)
                        dve.wait_ge(msg_sum, b + 1)
                        dve.tensor_scalar(msg[:, :, :], msg[:, :, :], 0.0, None, ALU.max).then_inc(msg_ready, 1)
                    if layer1(b):
                        dve_xt_lo(dve, g1, c)
                    if norm1(b):
                        dve_quotient(dve, g1, e)
                        dve.wait_ge(g1.xb_ready, e + 1)
                        dve.tensor_tensor(g1.agg[:, :, :], g1.agg[:, :, :], g1.xb[:, :, :],
                                          ALU.add).then_inc(g1.agg_ready, 1)
                        dve.wait_ge(g1.agg_ready, 3 * e + 3)
                        dve.scalar_tensor_tensor(g1.y[:, :, :], g1.agg[:, :, :], 0.5, g1.agg[:, :, :],
                                                 ALU.mult, ALU.max).then_inc(g1.y_ready, 1)
                        dve.wait_ge(g1.y_ready, 2 * e + 1)
                        dve.tensor_tensor(g1.y[:, :, :], g1.y[:, :, :], g1.x_in[o][:, :, :],
                                          ALU.add).then_inc(g1.y_ready, 1)
                        dve.wait_ge(g1.y_ready, 2 * e + 2)
                        dve_norm_stats(dve, lambda t: g1.y[:, t, :], g1.stats, g1.mv, g1.ve,
                                       g1.stat_ready, g1.ve_ready, e)
                    if layer1(b):
                        dve_scores(dve, g1, c, we[:, 0:1])
                    if norm0(b):
                        dve.wait_ge(diff_ready, b)
                        dve.wait_ge(z_ready, b)
                        dve.scalar_tensor_tensor(u[:, :], t_z[:, :], 1.0, diff[:, :],
                                                 ALU.add, ALU.mult).then_inc(w_ready, 1)
                        dve.wait_ge(w_ready, b)
                        dve.wait_ge(xn_ready, b)
                        ge(dve, yt_done, b - 1)
                        dve.scalar_tensor_tensor(yT[:, :], u[:, :], 0.5, xn[:, :],
                                                 ALU.mult, ALU.add).then_inc(y_ready, 1)
                    if layer1(b):
                        dve_xy(dve, g1, c)
                    if norm1(b):
                        dve_norm_apply(dve, lambda t: g1.y[:, t, :],
                                       (lambda t: xres[:, bass.ds(e, 1), t, :].rearrange("p a d -> p (a d)")),
                                       g1.mv, g1.rs, g1.rs_ready, g1.out_ready, e)
                    if layer1(b):
                        dve_select(dve, g1, c, p, 0)
                        split_xy(dve, g1, c, p)
                        dve_select(dve, g1, c, p, 1)
                    if norm0(b):
                        if norm1(b):
                            dve.wait_ge(g1.s_built, NT * H * (e + 1))
                            dve.wait_ge(g1.mask_mm, e + 1)
                        dve.wait_ge(adj_in[o], 16 * (q + p))
                        dve.tensor_scalar(g1.mask[o][:, :, :], adjT[o][:, :, :], 0.0, None,
                                          ALU.is_gt).then_inc(g1.mask_ready, 1)
                    if layer0(b):
                        dve.wait_ge(conv2_done, b + 1)
                        dve.wait_ge(h_lo_ready, b + 1)
                        dve.scalar_tensor_tensor(xc[:, :], bank_b[:, :], bn_sc[:, 1:2], xT[p][:, :],
                                                 ALU.mult, ALU.add).then_inc(pre_ready, 1)
                    if layer1(b):
                        dve_select(dve, g1, c, p, 2)
                    if layer0(b):
                        dve.wait_ge(xc_ready, b + 1)
                        ge(dve, z_done, b)
                        dve.tensor_copy(xc_hi[:, :], xc[:, :]).then_inc(xc_hi_ready, 1)
                    if norm0(b):
                        dve.wait_ge(yt_done, b)
                        dve_norm_stats(dve, lambda t: bank_d[:, t * P:(t + 1) * P], stats, mv, ve,
                                       stat_ready, ve_ready, b - 1)
                    if layer0(b):
                        dve.wait_ge(nm_hi_ready, b + 1)
                        dve.tensor_tensor(nm_lo[:, :], bank_c[:, :], nm_hi[:, :].bitcast(F32),
                                          ALU.subtract).then_inc(nm_lo_ready, 1)
                    if more0(b):
                        split_x(b + 1, o, q + p)
                    if norm0(b):
                        ge(dve, g1.y_ready, 2 * (b - 2))
                        dve_norm_apply(dve, lambda t: bank_d[:, t * P:(t + 1) * P], lambda t: g1.x_in[o][:, t, :],
                                       mv, rs, rs_ready, g1.x_ready, b - 1)
                    if layer1(b):
                        dve_select(dve, g1, c, p, 3)
                    if layer0(b):
                        dve.wait_ge(r_ready, b + 1)
                        dve.tensor_scalar(t_r[:, :], t_r[:, :], 0.5, 0.5, ALU.mult, ALU.add).then_inc(rr_ready, 1)
                        dve.wait_ge(hn_done, b + 1)
                        dve.wait_ge(rr_ready, b + 1)
                        dve.scalar_tensor_tensor(u[:, :], bank_d[:, :], cols[:, 13:14], t_r[:, :],
                                                 ALU.add, ALU.mult).then_inc(u_ready, 1)
                        dve.wait_ge(in_done, b + 1)
                        dve.wait_ge(u_ready, b + 1)
                        dve.tensor_tensor(u[:, :], bank_c[:, :], u[:, :], ALU.add).then_inc(v_ready, 1)
                split_x(0, 0, 0)
                steps(dve, body)


        with ExitStack() as tmp:
            def s4(n, shape, dt=F32):
                return tmp.enter_context(nc.sbuf_tensor("l2_" + n, shape, dt))

            def m4(n):
                return tmp.enter_context(nc.semaphore("l2_" + n))
            l2_w1 = s4("w1", [P, GROUPS, HID])
            l2_w2 = s4("w2", [P, 2 * GROUPS, D])
            l2_b1 = s4("b1", [P, 2 * GROUPS])
            l2_b2 = s4("b2", [P, GROUPS, D])
            l2_fw = s4("fw", [P, GROUPS])
            in_group = s4("in_group", [P, GROUPS])
            adjb, adji = s4("adjb", [P, P]), s4("adji", [P, P])
            group_row = s4("group_row", [P, GROUPS, P])
            ag = s4("ag", [P, GROUPS, P])
            deg, deg0, dinv = s4("deg", [P, GROUPS]), s4("deg0", [P, GROUPS]), s4("dinv", [P, GROUPS])
            nadj = s4("nadj", [P, GROUPS, P])
            x4 = s4("x4", [P, D])
            zt = s4("zt", [P, GROUPS, P])
            ht = s4("ht", [P, 2 * GROUPS, P])
            sup = s4("sup", [P, GROUPS, D])
            og = s4("og", [P, GROUPS, D])
            acc = s4("acc", [P, D])
            back = s4("back", [SLOT, PACK, D])
            fmax, fsum = s4("fmax", [P, 1]), s4("fsum", [P, 1])
            gw_n = s4("gw_n", [P, GROUPS])
            (cleared, wts_in, adj_in2, fw_sub, fw_exp, fw_ready, chain, pow_ready, tr_done, nadj_ready, x4_ready,
             z_done2, z_sb, h_done, h_sb, sup_done, sup_sb, o_done, o_read, acc_step, back_ready, pack_done) = (
                m4(n) for n in ("cleared wts_in adj_in fw_sub fw_exp fw_ready chain pow_ready tr_done nadj_ready "
                                "x4_ready z_done z_sb h_done h_sb sup_done sup_sb o_done o_read acc_step back_ready "
                                "pack_done").split())
            block = tmp.enter_context(nc.Block())
            NPACK = B // PACK
            split = ((slice(0, 4), 4), (slice(4, 5), 1))

            loads = [
                (l2_w1[:, :, :], a["l2_w1"].rearrange("g f e -> f g e")),
                (l2_w2[:, :, :], a["l2_w2"].rearrange("g (k e) d -> e (g k) d", k=2)),
                (l2_b1[:, :], a["l2_b1T"]),
                (l2_b2[:, :, :].rearrange("p g d -> p (g d)"), a["l2_b2"].partition_broadcast(P)),
                (l2_fw[:, :], a["l2_fw"].partition_broadcast(P)),
                (in_group[:, :], a["in_group"]),
                (group_row[:, :, :].rearrange("p g n -> p (g n)"), a["group_row"].partition_broadcast(P)),
            ]

            def packs(eng, body):
                body(0)
                with eng.Fori(1, NPACK) as q:
                    body(q)

            @block.sync
            def _(sp):
                for dst, src in loads:
                    sp.dma_start(dst, src).then_inc(wts_in, 16)
                sp.wait_ge(cleared, 1)

                def body(q):
                    ge(sp, chain, 5 * q)
                    for r in range(PACK):
                        sp.dma_start(adjb[SLOT * r:SLOT * r + NODES, SLOT * r:SLOT * r + NODES],
                                     a["adj_nodes"][bass.ds(PACK * q + r, 1)].rearrange("a n m -> (a n) m")
                                     ).then_inc(adj_in2, 16)
                packs(sp, body)

            @block.gpsimd
            def _(pool):
                pool.memset(adjb[:, :], 0.0).then_inc(cleared, 1)

                def body(q):
                    pool.wait_ge(chain, 5 * q + 4)
                    pool.tensor_tensor(deg[:, :], deg[:, :], mhalf[:, 0:GROUPS], ALU.pow).then_inc(pow_ready, 1)
                packs(pool, body)

            @block.tensor
            def _(pe):
                def body(q):
                    pe.wait_ge(chain, 5 * q + 5)
                    ge(pe, sup_sb, 2 * q)
                    ge(pe, z_sb, 2 * q)
                    ge(pe, o_read, 2 * q)
                    for g in range(GROUPS):
                        mm = pe.transpose(gat_ps[:, g // 4, (g % 4) * P:(g % 4 + 1) * P], ag[:, g, :], ident[:, :])
                    mm.then_inc(tr_done, 1)
                    pe.wait_ge(x4_ready, PACK * (q + 1))
                    pe.wait_ge(nadj_ready, 2 * q + 2)
                    for k, (gs, n) in enumerate(split):
                        pe.matmul(gat_ps[:, 2 + k, 0:n * P], x4[:, :],
                                  nadj[:, gs, :].rearrange("p g n -> p (g n)"), start=True, stop=True).then_inc(z_done2, 1)
                    pe.wait_ge(z_sb, 2 * q + 2)
                    ge(pe, h_sb, 2 * GROUPS * q)
                    for i in range(2 * GROUPS):
                        g, half = i // 2, i % 2
                        pe.matmul((bank_a, bank_b, bank_c)[i // 4][:, (i % 4) * P:(i % 4 + 1) * P],
                                  l2_w1[:, g, half * P:(half + 1) * P], zt[:, g, :],
                                  start=True, stop=True).then_inc(h_done, 1)
                    pe.wait_ge(h_sb, 2 * GROUPS * (q + 1))
                    for g in range(GROUPS):
                        out = bank_d[:, g * D:(g + 1) * D] if g < 4 else gat_ps[:, 0, 0:D]
                        for half in range(2):
                            mm = pe.matmul(out, ht[:, 2 * g + half, :], l2_w2[:, 2 * g + half, :],
                                           start=(half == 0), stop=(half == 1))
                        if g >= 3:
                            mm.then_inc(sup_done, 1)
                    pe.wait_ge(sup_sb, 2 * q + 2)
                    for g in range(GROUPS):
                        mm = pe.matmul(gat_ps[:, 1 + g // 4, (g % 4) * D:(g % 4 + 1) * D], nadj[:, g, :],
                                       sup[:, g, :], start=True, stop=True)
                        if g >= 3:
                            mm.then_inc(o_done, 1)
                packs(pe, body)

            @block.scalar
            def _(act):
                act.wait_ge(fw_sub, 1)
                act.activation(l2_fw[:, :], l2_fw[:, :], ACT.Exp).then_inc(fw_exp, 1)

                def body(q):
                    for k, (gs, n) in enumerate(split):
                        act.wait_ge(z_done2, 2 * q + k + 1)
                        ge(act, h_done, 2 * GROUPS * q)
                        act.activation(zt[:, gs, :].rearrange("p g n -> p (g n)"), gat_ps[:, 2 + k, 0:n * P],
                                       ACT.Copy).then_inc(z_sb, 1)
                    ge(act, sup_done, 2 * q)
                    for i in range(2 * GROUPS):
                        act.wait_ge(h_done, 2 * GROUPS * q + min(4 * (i // 4) + 4, 2 * GROUPS))
                        act.activation(ht[:, i, :], (bank_a, bank_b, bank_c)[i // 4][:, (i % 4) * P:(i % 4 + 1) * P],
                                       ACT.Relu, bias=l2_b1[:, i:i + 1]).then_inc(h_sb, 1)
                packs(act, body)

            @block.vector
            def _(dve):
                dve.wait_ge(wts_in, 16 * len(loads))
                dve.tensor_reduce(fmax[:, :], l2_fw[:, :], AX_X, ALU.max).then_inc(fw_ready, 1)
                dve.wait_ge(fw_ready, 1)
                dve.tensor_scalar(l2_fw[:, :], l2_fw[:, :], fmax[:, 0:1], None, ALU.subtract).then_inc(fw_sub, 1)
                dve.wait_ge(fw_exp, 1)
                dve.tensor_reduce(fsum[:, :], l2_fw[:, :], AX_X, ALU.add).then_inc(fw_ready, 1)
                dve.wait_ge(fw_ready, 2)
                dve.reciprocal(fsum[:, :], fsum[:, :]).then_inc(fw_ready, 1)
                dve.wait_ge(fw_ready, 3)
                dve.scalar_tensor_tensor(gw_n[:, :], l2_fw[:, :], fsum[:, 0:1], in_group[:, :],
                                         ALU.mult, ALU.mult).then_inc(fw_ready, 1)
                dve.wait_ge(fw_ready, 4)

                def body(q):
                    dve.wait_ge(adj_in2, 16 * PACK * (q + 1))
                    dve.tensor_tensor(adji[:, :], adjb[:, :], ident[:, :], ALU.add).then_inc(chain, 1)
                    dve.wait_ge(chain, 5 * q + 1)
                    ge(dve, tr_done, q)
                    for g in range(GROUPS):
                        mm = dve.scalar_tensor_tensor(ag[:, g, :], adji[:, :], in_group[:, g:g + 1],
                                                      group_row[:, g, :], ALU.mult, ALU.mult)
                    mm.then_inc(chain, 1)
                    dve.wait_ge(chain, 5 * q + 2)
                    dve.tensor_reduce(deg[:, :], ag[:, :, :], AX_X, ALU.add).then_inc(chain, 1)
                    dve.wait_ge(chain, 5 * q + 3)
                    dve.tensor_scalar(deg0[:, :], deg[:, :], 0.0, None, ALU.is_equal).then_inc(fw_ready, 1)
                    dve.wait_ge(fw_ready, 3 * q + 5)
                    dve.tensor_tensor(deg[:, :], deg[:, :], deg0[:, :], ALU.add).then_inc(chain, 1)
                    dve.tensor_scalar(deg0[:, :], deg0[:, :], -1.0, 1.0, ALU.mult, ALU.add).then_inc(fw_ready, 1)
                    dve.wait_ge(fw_ready, 3 * q + 6)
                    dve.wait_ge(pow_ready, q + 1)
                    dve.tensor_tensor(dinv[:, :], deg[:, :], deg0[:, :], ALU.mult).then_inc(fw_ready, 1)
                    dve.wait_ge(fw_ready, 3 * q + 7)
                    dve.tensor_tensor(ag[:, :, :], ag[:, :, :], dinv[:, :].unsqueeze(2).to_broadcast([P, GROUPS, P]),
                                      ALU.mult).then_inc(chain, 1)
                    ge(dve, z_done2, 2 * q)
                    for r in range(PACK):
                        dve.tensor_copy(x4[SLOT * r:SLOT * (r + 1), :],
                                        xres[0:SLOT, bass.ds(PACK * q + r, 1), 0, :].rearrange("p a d -> p (a d)")
                                        ).then_inc(x4_ready, 1)
                    dve.wait_ge(tr_done, q + 1)
                    ge(dve, o_done, 2 * q)
                    for k, (gs, n) in enumerate(split):
                        dve.tensor_tensor(nadj[:, gs, :], gat_ps[:, k, 0:n * P].rearrange("p (g n) -> p g n", n=P),
                                          dinv[:, gs].unsqueeze(2).to_broadcast([P, n, P]),
                                          ALU.mult).then_inc(nadj_ready, 1)
                    dve.wait_ge(sup_done, 2 * q + 2)
                    dve.tensor_copy(sup[:, 0:4, :].rearrange("p g d -> p (g d)"), bank_d[:, :]).then_inc(sup_sb, 1)
                    dve.tensor_copy(sup[:, 4, :], gat_ps[:, 0, 0:D]).then_inc(sup_sb, 1)
                    dve.wait_ge(o_done, 2 * q + 2)
                    for k, (gs, n) in enumerate(split):
                        dve.tensor_tensor(og[:, gs, :], gat_ps[:, 1 + k, 0:n * D].rearrange("p (g d) -> p g d", d=D),
                                          l2_b2[:, gs, :], ALU.add).then_inc(o_read, 1)
                    dve.wait_ge(o_read, 2 * q + 2)
                    dve.tensor_scalar(og[:, :, :], og[:, :, :], 0.0, None, ALU.max).then_inc(acc_step, 1)
                    dve.wait_ge(acc_step, 6 * q + 1)
                    dve.tensor_scalar(acc[:, :], og[:, 0, :], gw_n[:, 0:1], None, ALU.mult).then_inc(acc_step, 1)
                    for g in range(1, GROUPS):
                        dve.wait_ge(acc_step, 6 * q + 1 + g)
                        dve.scalar_tensor_tensor(acc[:, :], og[:, g, :], gw_n[:, g:g + 1], acc[:, :],
                                                 ALU.mult, ALU.add).then_inc(acc_step, 1)
                    dve.wait_ge(acc_step, 6 * q + 6)
                    for r in range(PACK):
                        dve.tensor_copy(back[:, r, :], acc[SLOT * r:SLOT * (r + 1), :]).then_inc(back_ready, 1)
                    dve.wait_ge(back_ready, PACK * (q + 1))
                    for r in range(PACK):
                        row = xres[0:NODES, bass.ds(PACK * q + r, 1), 0, :].rearrange("p a d -> p (a d)")
                        dve.tensor_tensor(row, row, back[0:NODES, r, :], ALU.add).then_inc(pack_done, 1)
                packs(dve, body)

        with ExitStack() as tmp:
            def s5(n, shape, dt=F32):
                return tmp.enter_context(nc.sbuf_tensor(n, shape, dt))

            def m5(n):
                return tmp.enter_context(nc.semaphore(n))
            g3 = attention(tmp, 1, "g3_", (bank_a[:, :], [bank_b[:, :], bank_a[:, :]], [bank_c[:, :], bank_d[:, :]]), 2, 2, True)
            adjT = [s5(f"c_adjT{i}", [P, NT, N]) for i in range(2)]
            out_t = [s5(f"out_t{i}", [P, NT, D]) for i in range(2)]
            stats, mv, ve, rs = (s5("c_stats", [P, NT, 6]), s5("c_mv", [P, NT, 2]), s5("c_ve", [P, NT]),
                                 s5("c_rs", [P, NT]))
            adj_in = [m5("c_adj_in0"), m5("c_adj_in1")]
            stored = [m5("stored0"), m5("stored1")]
            shift, shift3 = s5("shift", [P, NT]), s5("shift3", [P, NT])
            stat_ready, ve_ready, rs_ready = m5("c_stat_ready"), m5("c_ve_ready"), m5("c_rs_ready")
            shift_ready, shift3_ready, x_kept = m5("shift_ready"), m5("shift3_ready"), m5("x_kept")
            block = tmp.enter_context(nc.Block())

            def steps(eng, body):
                for n in range(4):
                    body(n, n % 2, n // 2)
                with eng.Fori(2, B // 2 - 1) as q:
                    for p in range(2):
                        body(2 * q + p, p, q)
                for n in range(B - 2, B + 2):
                    body(n, n % 2, n // 2)

            def works(n, first, last):
                return not isinstance(n, int) or first <= n <= last

            def front(n):
                return works(n, 0, B - 1)

            def main(n):
                return works(n, 1, B)

            def tail(n):
                return works(n, 2, B + 1)

            def more(n):
                return works(n, 0, B - 2)

            def x2(n, t):
                return xres[:, bass.ds(n, 1), t, :].rearrange("p a d -> p (a d)")

            @block.sync
            def _(sp):
                def body(n, p, q):
                    if front(n):
                        ge(sp, g3.mask_ready, n - 1)
                        sp.dma_start(adjT[p][:, :, :],
                                     a["adjT"][bass.ds(n, 1)].rearrange("a (t p) n -> p (a t) n", p=P)
                                     ).then_inc(adj_in[p], 16)
                    if tail(n):
                        sp.wait_ge(g3.out_ready, NT * (n - 1))
                        sp.dma_start(a["out"][bass.ds(n - 2, 1)].rearrange("a (t p) d -> p (a t) d", p=P),
                                     out_t[p][:, :, :]).then_inc(stored[p], 16)
                steps(sp, body)
                for p in range(2):
                    sp.wait_ge(stored[p], 16 * (B // 2))

            @block.tensor
            def _(pe):
                def prepare(m):
                    pe_transpose_x(pe, g3, m, lambda t: g3.x_in[0][:, t, :])
                    pe_project(pe, g3, m)
                    pe_a_row(pe, g3, m, 0)
                prepare(0)

                def body(n, p, q):
                    c, o = n - 1, 1 - p
                    if front(n):
                        pe_a_row(pe, g3, n, 1)
                    if main(n):
                        pe_head(pe, g3, c, o, 0)
                        pe_head(pe, g3, c, o, 1)
                    if front(n):
                        pe_a_row(pe, g3, n, 2)
                    if main(n):
                        pe_head(pe, g3, c, o, 2)
                        pe_head(pe, g3, c, o, 3)
                    if front(n):
                        pe_a_row(pe, g3, n, 3)
                    if more(n):
                        prepare(n + 1)
                    if front(n):
                        pe_mask_sums(pe, g3, n, p)
                steps(pe, body)

            @block.scalar
            def _(act):
                act.activation(warm[:, :], zero1[:, :], ACT.Exp)

                def norm2(m):
                    act.wait_ge(shift_ready, m + 1)
                    ge(act, g3.xt_done, m)
                    ge(act, x_kept, m)
                    for t in range(NT):
                        act.activation(g3.x_in[0][:, t, :], x2(m, t), ACT.Identity,
                                       bias=shift[:, t:t + 1], scale=rs[:, t:t + 1]).then_inc(g3.x_ready, 1)
                norm2(0)
                act_round_x(act, g3, 0)
                act_projection(act, g3, 0)

                def body(n, p, q):
                    if front(n):
                        act_signs(act, g3, n, p, 0)
                        act_exps(act, g3, n, p)
                    if tail(n):
                        act.wait_ge(shift3_ready, n - 1)
                        ge(act, stored[p], 16 * (q - 1))
                        for t in range(NT):
                            act.activation(out_t[p][:, t, :], g3.y[:, t, :], ACT.Identity,
                                           bias=shift3[:, t:t + 1], scale=g3.rs[:, t:t + 1]).then_inc(g3.out_ready, 1)
                    if front(n):
                        act_signs(act, g3, n, p, 1)
                        act_round_xy(act, g3, n, p)
                    if main(n):
                        act_masked(act, g3, n - 1)
                    if more(n):
                        norm2(n + 1)
                    if front(n):
                        act_signs(act, g3, n, p, 2)
                    if more(n):
                        act_round_x(act, g3, n + 1)
                    if front(n):
                        act_signs(act, g3, n, p, 3)
                    if more(n):
                        act_projection(act, g3, n + 1)
                steps(act, body)

            @block.gpsimd
            def _(pool):
                pool_rstd(pool, ve, rs, ve_ready, rs_ready, 0)

                def body(n, p, q):
                    if front(n):
                        pool_ball(pool, g3, n)
                    if more(n):
                        pool.wait_ge(g3.x_ready, NT * (n + 1))
                        pool_rstd(pool, ve, rs, ve_ready, rs_ready, n + 1)
                    if front(n):
                        pool_xy(pool, g3, n)
                        mask_signs(pool, g3, n, p, POOL_HEAD, g3.s_pool)
                        split_xy(pool, g3, n, p)
                    if main(n):
                        ge(pool, g3.out_ready, NT * (n - 1))
                        pool_rstd(pool, g3.ve, g3.rs, g3.ve_ready, g3.rs_ready, n - 1)
                steps(pool, body)

            @block.vector
            def _(dve):
                def norm_shift(mv, rs, rs_ready, dst, dst_ready, m):
                    dve.wait_ge(rs_ready, m + 1)
                    dve.scalar_tensor_tensor(dst[:, :], mv[:, :, 0], -1.0, rs[:, :], ALU.mult,
                                             ALU.mult).then_inc(dst_ready, 1)

                def stats2(m):
                    dve_norm_stats(dve, lambda t: x2(m, t), stats, mv, ve, stat_ready, ve_ready, m)

                def new_mask(n, p, q):
                    dve.wait_ge(adj_in[p], 16 * (q + 1))
                    ge(dve, g3.mask_mm, n - 1)
                    ge(dve, g3.s_pool, n - 1)
                    dve.tensor_scalar(g3.mask[p][:, :, :], adjT[p][:, :, :], 0.0, None,
                                      ALU.is_gt).then_inc(g3.mask_ready, 1)
                def keep_x(m):
                    dve.wait_ge(g3.x_ready, NT * (m + 1))
                    dve.nop(nofuse=True)
                    dve.tensor_copy(xres[:, bass.ds(m, 1), :, :].rearrange("p a t d -> p (a t) d"),
                                    g3.x_in[0][:, :, :]).then_inc(x_kept, 1)
                stats2(0)
                norm_shift(mv, rs, rs_ready, shift, shift_ready, 0)
                dve_xt_lo(dve, g3, 0)
                keep_x(0)

                def body(n, p, q):
                    c, o = n - 1, 1 - p
                    if front(n):
                        dve_scores(dve, g3, n, zero1[:, 0:1])
                    if tail(n):
                        norm_shift(g3.mv, g3.rs, g3.rs_ready, shift3, shift3_ready, n - 2)
                    if more(n):
                        stats2(n + 1)
                    if front(n):
                        new_mask(n, p, q)
                        dve_xy(dve, g3, n)
                    if more(n):
                        norm_shift(mv, rs, rs_ready, shift, shift_ready, n + 1)
                    if front(n):
                        mask_signs(dve, g3, n, p, 1, g3.s_built)
                    if main(n):
                        dve_sums(dve, g3, c, o)
                        dve_quotient(dve, g3, c)
                    if more(n):
                        dve_xt_lo(dve, g3, n + 1)
                        keep_x(n + 1)
                    if main(n):
                        dve.wait_ge(x_kept, n)
                        dve.wait_ge(g3.agg_ready, 2 * n)
                        dve.tensor_tensor(g3.y[:, :, :], g3.agg[:, :, :],
                                          xres[:, bass.ds(c, 1), :, :].rearrange("p a t d -> p (a t) d"),
                                          ALU.add).then_inc(g3.y_ready, 1)
                    if front(n):
                        mask_signs(dve, g3, n, p, 2, g3.s_built)
                    if main(n):
                        dve.wait_ge(g3.y_ready, n)
                        dve_norm_stats(dve, lambda t: g3.y[:, t, :], g3.stats, g3.mv, g3.ve,
                                       g3.stat_ready, g3.ve_ready, c)
                    if front(n):
                        mask_signs(dve, g3, n, p, 3, g3.s_built)
                steps(dve, body)


def kernel(**inputs):
    import numpy as _np
    import concourse.bacc as _bacc
    from concourse import mybir as _mybir
    from concourse.bass_utils import run_bass_kernel_spmd as _run

    x = {k: _np.asarray(v) for k, v in inputs.items()}
    p = "L0_gnn_"
    bn = [x[p + f"bn{i}_{c}"] for i in (1, 2) for c in "gbmv"]
    gate_b = [x[p + n].reshape(3, 128)[i] for n in ("b_ih", "b_hh") for i in range(3)]
    node_groups = [range(25), range(9), (0, *range(9, 15)), (6, 7, 8, 12, 13, 14), (3, 4, 5, 9, 10, 11)]
    member = _np.zeros((4, 32, 5), _np.float32)
    for g, nodes in enumerate(node_groups):
        member[:, list(nodes), g] = 1.0
    member = member.reshape(128, 5)
    arrays = {
        "xT": x["x"].transpose(0, 2, 1),
        "adjT": x["adj"].transpose(0, 2, 1),
        "adj_nodes": x["adj"][:, :25, :25],
        "conv1_wT": x[p + "conv1_w"][:, :, 0].T,
        "conv2_wT": x[p + "conv2_w"].transpose(1, 2, 0),
        "w_msgT": x[p + "w_msg"].T,
        "w_seT": x[p + "w_se"].T,
        "b_se": x[p + "b_se"].reshape(3, 1),
        "w_ihT": x[p + "w_ih"].T,
        "w_hhT": x[p + "w_hh"].T,
        "cols": _np.stack(bn + gate_b, axis=1),
        "b_msg": x[p + "b_msg"],
        "w1_proj": x["L1_gnn_W_proj"],
        "w1_projT": x["L1_gnn_W_proj"].T,
        "a1_w": x["L1_gnn_a_w"].reshape(65),
        "bias1": x["L1_gnn_bias"],
        "w3": x["L3_gnn_W"],
        "w3T": x["L3_gnn_W"].T,
        "a3": x["L3_gnn_a"].reshape(256),
        "l2_w1": x["L2_gnn_W1"],
        "l2_w2": x["L2_gnn_W2"],
        "l2_b1T": x["L2_gnn_b1"].reshape(10, 128).T,
        "l2_b2": x["L2_gnn_b2"].reshape(640),
        "l2_fw": x["L2_gnn_fusion_w"],
        "in_group": member,
        "group_row": member.T.reshape(640),
        "ident": _np.eye(128, dtype=_np.float32),
    }
    nc = _bacc.Bacc("TRN2", target_bir_lowering=False, num_devices=1)
    aps, feed = {}, {}
    for name, v in arrays.items():
        v = _np.ascontiguousarray(v)
        feed[f"in_{name}"] = v
        aps[name] = nc.dram_tensor(f"in_{name}", v.shape, _mybir.dt.from_np(v.dtype), kind="ExternalInput").ap()
    aps["out"] = nc.dram_tensor("out_0", x["x"].shape, _mybir.dt.float32, kind="ExternalOutput").ap()
    build_program(nc, aps)
    r = _run(nc, [feed], core_ids=[0])
    return r.results[0]["out_0"]
```

```python
from contextlib import ExitStack

import concourse.bass as bass
from concourse import mybir

F32 = mybir.dt.float32
F32R = mybir.dt.float32r
F16 = mybir.dt.float16
ALU = mybir.AluOpType
ACT = mybir.ActivationFunctionType
AX_X = mybir.AxisListType.X
RMAX = bass.bass_isa.ReduceOp.max

P = 128
B, N, D = 16, 512, 128
NT = N // P
TAPS, PAD = 17, 8
H, DH = 4, 32
HC = DH + 1
XY = 2 * HC
WP = D + 2 * H
RL_LO, RL = 32, 32 + H
NODES, SLOT, GROUPS = 25, 32, 5
POOL_HEAD = 0
PACK = P // SLOT
NPACK = B // PACK
HID = 256
EPS = 1e-5
LOG_SCALE = 5.545177444479562
C1, C2, CM, CS, CG = 0, D, D + TAPS * D, D + TAPS * D + D, D + TAPS * D + D + 96
NW = CG + 3 * 3 * D


def build_program(nc, a):
    with ExitStack() as ctx:
        def sb(name, shape, dt=F32):
            return ctx.enter_context(nc.sbuf_tensor(name, shape, dt))

        def sem(name):
            return ctx.enter_context(nc.semaphore(name))

        def ge(eng, s, n):
            if isinstance(n, int) and n <= 0:
                return
            eng.wait_ge(s, n)

        bank_a = ctx.enter_context(nc.psum_tensor("bank_a", [P, N], F32))
        bank_b = ctx.enter_context(nc.psum_tensor("bank_b", [P, N], F32))
        bank_c = ctx.enter_context(nc.psum_tensor("bank_c", [P, N], F32))
        bank_d = ctx.enter_context(nc.psum_tensor("bank_d", [P, N], F32))
        gat_ps = ctx.enter_context(nc.psum_tensor("gat_ps", [P, NT, 512], F32))
        gat_bank = [gat_ps[:, t, :] for t in range(NT)]

        consts = sb("consts", [P, 162])
        ident, cols = consts[:, 0:128], consts[:, 128:142]
        in_group, l2_b1 = consts[:, 142:147], consts[:, 147:157]
        bse = consts[0:96, 157:158]
        head_rows = consts[0:RL, 158:162]
        rows = sb("rows", [P, 262])
        bmsg, bias1, we, l2_fw = rows[:, 0:128], rows[:, 128:256], rows[:, 256:257], rows[:, 257:262]
        w_hi = sb("w_hi", [P, NW], F32R)
        w_lo = sb("w_lo", [P, NW], F32R)
        bn_sc = sb("bn_sc", [P, 2])
        bn_sh = sb("bn_sh", [P, 2])
        bn_t = sb("bn_t", [P, 2])
        half_b = sb("half_b", [P, 2])
        zero1 = sb("zero1", [P, 1])
        warm = sb("warm", [P, 1])
        ln_scale = sb("ln_scale", [P, 1])
        mhalf = sb("mhalf", [P, GROUPS * NPACK])
        gp_hi = [sb(f"gp_hi{l}", [P, WP], F32R) for l in range(2)]
        gp_lo = [sb(f"gp_lo{l}", [P, WP], F32R) for l in range(2)]
        g1_left_hi, g1_left_lo = sb("g1_left_hi", [P, RL], F32R), sb("g1_left_lo", [P, RL], F32R)
        g3_left_hi, g3_left_lo = sb("g3_left_hi", [P, H, P], F32R), sb("g3_left_lo", [P, H, P], F32R)
        spread = sb("spread", [RL, H, P], F32R)
        xres = sb("xres", [P, B, NT, D])
        nadj = sb("nadj", [P, GROUPS, NPACK, SLOT])
        adjT = [sb(f"adjT{i}", [P, NT, N]) for i in range(2)]
        expd = sb("expd", [P, NT, N])
        spare = [buf[:, :, :].rearrange("p t n -> p (t n)") for buf in (expd, adjT[0])]
        W1_END, B2_END = GROUPS * HID, GROUPS * (HID + D)
        l2_w1 = spare[0][:, 0:W1_END].rearrange("p (g e) -> p g e", g=GROUPS)
        l2_b2 = spare[0][:, W1_END:B2_END].rearrange("p (g d) -> p g d", g=GROUPS)
        l2_w2 = spare[1][:, 0:2 * GROUPS * D].rearrange("p (k d) -> p k d", d=D)
        gw_n = sb("gw_n", [P, GROUPS])
        l2_in = sem("l2_in")

        bn_v = cols[:, 0:8].rearrange("p (l c) -> p l c", c=4)

        scratch = xres[:, :, :, :].rearrange("p b t d -> p (b t d)")
        AT = B // 2 * NT * D
        adjb = scratch[:, AT:AT + NPACK * P].rearrange("p (k n) -> p k n", k=NPACK)
        group_row = scratch[:, AT + 512:AT + 512 + GROUPS * P].rearrange("p (g n) -> p g n", g=GROUPS)
        ag = scratch[:, AT + 1152:AT + 1152 + GROUPS * NPACK * P].rearrange("p (g k n) -> p g k n", g=GROUPS, k=NPACK)
        deg, deg0 = sb("deg", [P, GROUPS * NPACK]), sb("deg0", [P, GROUPS * NPACK])
        adj2_in = sem("adj2_in")

        with ExitStack() as tmp:
            wf = tmp.enter_context(nc.sbuf_tensor("wf", [P, NW], F32))
            gat_w = tmp.enter_context(nc.sbuf_tensor("gat_w", [P, 4 * P + 4 * H], F32))
            gpf = [tmp.enter_context(nc.sbuf_tensor(f"gpf{l}", [P, WP], F32)) for l in range(2)]
            fmax, fsum = (tmp.enter_context(nc.sbuf_tensor(n, [P, 1], F32)) for n in ("fmax", "fsum"))
            gw_proj = [gat_w[:, l * P:(l + 1) * P] for l in range(2)]
            gw = [gat_w[:, (2 + l) * P:(3 + l) * P] for l in range(2)]
            bd = [gat_w[:, 4 * P + 2 * H * l:4 * P + 2 * H * (l + 1)] for l in range(2)]
            CHUNKS = 4
            w_in = [tmp.enter_context(nc.semaphore(f"w_in{i}")) for i in range(CHUNKS)]
            (small_in, const_set, w_rounded, score_w, gp_step, bn_ready, bn_pow,
             fw_sub, fw_exp, fw_step) = (tmp.enter_context(nc.semaphore(n)) for n in (
                 "small_in const_set w_rounded score_w gp_step bn_ready bn_pow "
                 "fw_sub fw_exp fw_step").split())
            block = tmp.enter_context(nc.Block())
            chunk = [slice(NW * i // CHUNKS, NW * (i + 1) // CHUNKS) for i in range(CHUNKS)]

            @block.sync
            def _(sp):
                for dst, src in ((consts[:, :], a["consts"]), (gat_w[:, :], a["gat_w"]),
                                 (rows[:, :], a["rows"].partition_broadcast(P))):
                    sp.dma_start(dst, src).then_inc(small_in, 16)
                for i, cs in enumerate(chunk):
                    sp.dma_start(wf[:, cs], a["weights"][:, cs]).then_inc(w_in[i], 16)
                sp.dma_start(adjb.rearrange("p k n -> p (k n)"), a["adj_packs"]).then_inc(adj2_in, 16)
                sp.dma_start(group_row.rearrange("p g n -> p (g n)"), a["group_row"].partition_broadcast(P)
                             ).then_inc(adj2_in, 16)

            @block.gpsimd
            def _(pool):
                pool.memset(mhalf[:, :], -0.5).then_inc(const_set, 1)
                pool.memset(g1_left_hi[:, :].bitcast(F32), 0.0).then_inc(const_set, 1)
                pool.memset(g1_left_lo[:, :].bitcast(F32), 0.0).then_inc(const_set, 1)
                pool.memset(zero1[:, :], 0.0)
                pool.memset(ln_scale[:, :], LOG_SCALE)
                pool.wait_ge(const_set, 3)
                pool.wait_ge(bn_ready, 1)
                pool.tensor_tensor(bn_t[:, :], bn_t[:, :], mhalf[:, 0:2], ALU.pow).then_inc(bn_pow, 1)

            @block.scalar
            def _(act):
                act.wait_ge(fw_sub, 1)
                act.activation(l2_fw, l2_fw, ACT.Exp).then_inc(fw_exp, 1)
                for i, cs in enumerate(chunk):
                    act.wait_ge(w_in[i], 16)
                    act.activation(w_hi[:, cs], wf[:, cs], ACT.Copy).then_inc(w_rounded, 1)

            @block.tensor
            def _(pe):
                pe.wait_ge(small_in, 16 * 3)
                for l in range(2):
                    pe.matmul(bank_a[:, 8 * l:8 * l + 8], gw[l], bd[l], start=True, stop=True).then_inc(score_w, 1)

            @block.vector
            def _(dve):
                dve.wait_ge(small_in, 16 * 3)
                dve.tensor_scalar(bn_t[:, :], bn_v[:, :, 3], EPS, None, ALU.add).then_inc(bn_ready, 1)
                dve.tensor_reduce(fmax[:, :], l2_fw, AX_X, ALU.max).then_inc(fw_step, 1)
                dve.wait_ge(fw_step, 1)
                dve.tensor_scalar(l2_fw, l2_fw, fmax[:, 0:1], None, ALU.subtract).then_inc(fw_sub, 1)
                for l in range(2):
                    dve.tensor_copy(gpf[l][:, 0:D], gw_proj[l]).then_inc(gp_step, 1)
                dve.wait_ge(score_w, 2)
                for l in range(2):
                    dve.tensor_copy(gpf[l][:, D:WP], bank_a[:, 8 * l:8 * l + 8]).then_inc(gp_step, 1)
                dve.wait_ge(gp_step, 4)
                for l in range(2):
                    dve.tensor_copy(gp_hi[l][:, :], gpf[l][:, :]).then_inc(gp_step, 1)
                dve.wait_ge(gp_step, 6)
                for l in range(2):
                    dve.tensor_tensor(gp_lo[l][:, :], gpf[l][:, :], gp_hi[l][:, :].bitcast(F32),
                                      ALU.subtract).then_inc(gp_step, 1)
                dve.wait_ge(fw_exp, 1)
                dve.tensor_reduce(fsum[:, :], l2_fw, AX_X, ALU.add).then_inc(fw_step, 1)
                dve.wait_ge(fw_step, 2)
                dve.reciprocal(fsum[:, :], fsum[:, :]).then_inc(fw_step, 1)
                dve.wait_ge(fw_step, 3)
                dve.scalar_tensor_tensor(gw_n[:, :], l2_fw, fsum[:, 0:1], in_group, ALU.mult, ALU.mult)
                dve.tensor_tensor(half_b[:, :], cols[:, 8:10], cols[:, 11:13], ALU.add).then_inc(bn_ready, 1)
                dve.wait_ge(bn_pow, 1)
                dve.tensor_tensor(bn_sc[:, :], bn_v[:, :, 0], bn_t[:, :], ALU.mult).then_inc(bn_ready, 1)
                dve.wait_ge(bn_ready, 3)
                dve.tensor_scalar(half_b[:, :], half_b[:, :], 0.5, None, ALU.mult)
                dve.tensor_tensor(bn_t[:, :], bn_v[:, :, 2], bn_sc[:, :], ALU.mult).then_inc(bn_ready, 1)
                dve.wait_ge(bn_ready, 4)
                dve.tensor_tensor(bn_sh[:, :], bn_v[:, :, 1], bn_t[:, :], ALU.subtract)
                for i, cs in enumerate(chunk):
                    dve.wait_ge(w_rounded, i + 1)
                    dve.tensor_tensor(w_lo[:, cs], wf[:, cs], w_hi[:, cs].bitcast(F32), ALU.subtract)
                dve.wait_ge(gp_step, 8)
                for src, dst in ((gp_hi, g3_left_hi), (gp_lo, g3_left_lo)):
                    dve.tensor_copy(dst[:, :, :], src[1][:, D:D + H].bitcast(F32).unsqueeze(2).to_broadcast([P, H, P]))
                dve.wait_ge(const_set, 3)
                for src, dst in ((gp_hi, g1_left_hi), (gp_lo, g1_left_lo)):
                    for at in (0, RL_LO):
                        dve.tensor_copy(dst[:, at:at + H], src[0][:, D:D + H].bitcast(F32))
                dve.tensor_copy(spread[:, :, :], head_rows.unsqueeze(2).to_broadcast([RL, H, P]))

        class Attention:
            pass

        def attention(ctx2, l, tag, front, agg_steps, depth, signs):
            g = Attention()

            def s2(n, shape, dt=F32):
                return ctx2.enter_context(nc.sbuf_tensor(tag + n, shape, dt))

            def m2(n):
                return ctx2.enter_context(nc.semaphore(tag + n))
            g.l = l
            g.agg_steps = agg_steps
            g.depth = depth
            g.signs = signs
            g.x_bank, g.proj_bank, g.row_bank = front
            g.x_in = [s2(f"x_in{i}", [P, NT, D]) for i in range(1 if signs else 2)]
            g.mask = [s2(f"mask{i}", [P, NT, N], F16) for i in range(2)]
            g.xt_hi, g.xt_lo = ([s2(f"{n}{i}", [P, N], F32R) for i in range(depth)] * (2 // depth)
                                for n in ("xt_hi", "xt_lo"))
            g.proj = [s2(f"proj{i}", [P, NT, WP]) for i in range(depth)] * (2 // depth)
            if not signs:
                g.rows = s2("rows", [RL, N], F32R)
                g.a_row = s2("a_row", [P, H, N])
            g.bmax, g.ball = s2("bmax", [P, H]), s2("ball", [P, H])
            g.b_rel, g.t, g.nb = (s2(n, [P, NT, H]) for n in ("b_rel", "t", "nb"))
            g.r = [s2(f"r{i}", [P, NT, H]) for i in range(depth)] * (2 // depth)
            g.xy = s2("xy", [P, NT, H, XY])
            g.xy_hi = [s2(f"xy_hi{i}", [P, NT, H, XY], F16) for i in range(depth)] * (2 // depth)
            g.xy_lo = [s2(f"xy_lo{i}", [P, NT, H, XY], F16) for i in range(depth)] * (2 // depth)
            g.s = [s2(f"s{i}", [P, H, NT, N], F16) for i in range(depth)] * (2 // depth)
            g.masked = s2("masked", [P, NT, H, HC])
            g.num = s2("num", [P, NT, H, HC])
            g.rden = s2("rden", [P, NT, H])
            g.agg = [s2(f"agg{i}", [P, NT, D]) for i in range(depth)] * (2 // depth)
            if not signs:
                g.xb = s2("xb", [P, NT, D])
            g.y = g.agg
            g.stats, g.mv, g.ve, g.rs = s2("stats", [P, NT, 6]), s2("mv", [P, NT, 2]), s2("ve", [P, NT]), s2("rs", [P, NT])
            g.x_ready = m2("x_ready")
            g.mask_ready = m2("mask_ready")
            g.xt_done = m2("xt_done")
            g.xt_hi_ready = m2("xt_hi_ready")
            g.xt_lo_ready = m2("xt_lo_ready")
            g.proj_done = m2("proj_done")
            g.proj_sb = m2("proj_sb")
            g.arow_done = m2("arow_done")
            g.bmax_ready = m2("bmax_ready")
            g.ball_ready = m2("ball_ready")
            g.rel_ready = m2("rel_ready")
            g.t_ready = m2("t_ready")
            g.exp_ready = m2("exp_ready")
            g.xy_ready = m2("xy_ready")
            g.hi_ready = m2("hi_ready")
            g.lo_ready = m2("lo_ready")
            g.s_built = m2("s_built")
            g.mask_mm = m2("mask_mm")
            g.s_mm = m2("s_mm")
            g.masked_sb = m2("masked_sb")
            g.num_ready = m2("num_ready")
            g.agg_ready = m2("agg_ready")
            g.y_ready = m2("y_ready")
            g.stat_ready = m2("stat_ready")
            g.ve_ready = m2("ve_ready")
            g.shift, g.shift_ready = s2("shift", [P, NT]), m2("shift_ready")
            g.rs_ready = m2("rs_ready")
            g.out_ready = m2("out_ready")
            if signs:
                g.sign_ready, g.s_pool = m2("sign_ready"), m2("s_pool")
            else:
                g.arow_sb, g.small_ready, g.xb_ready = m2("arow_sb"), m2("small_ready"), m2("xb_ready")
                g.rows_done, g.rows_hi_ready, g.rows_lo_ready = m2("rows_done"), m2("rows_hi_ready"), m2("rows_lo_ready")
            return g

        def pe_transpose_x(pe, g, c, src):
            pe.wait_ge(g.x_ready, NT * (c + 1))
            if g.signs:
                ge(pe, g.proj_sb, 2 * c)
            else:
                ge(pe, g.arow_sb, H * c)
            if g.x_bank is gat_bank[0]:
                ge(pe, g.num_ready, 3 * c)
            for t in range(NT):
                mm = pe.transpose(g.x_bank[:, t * P:(t + 1) * P], src(t), ident[:, :])
            mm.then_inc(g.xt_done, 1)

        def pe_project(pe, g, c, p):
            pe.wait_ge(g.xt_lo_ready, c + 1)
            ge(pe, g.proj_sb, 2 * c)
            for t in range(NT):
                out = g.proj_bank[t // 2][:, (t % 2) * WP:(t % 2 + 1) * WP]
                tok = slice(t * P, (t + 1) * P)
                pe.matmul(out, g.xt_lo[p][:, tok], gp_hi[g.l][:, :], start=True, stop=False)
                pe.matmul(out, g.xt_hi[p][:, tok], gp_lo[g.l][:, :], start=False, stop=False)
                mm = pe.matmul(out, g.xt_hi[p][:, tok], gp_hi[g.l][:, :], start=False, stop=True)
                if t % 2:
                    mm.then_inc(g.proj_done, 1)

        def pe_a_row(pe, g, c, p, h):
            if g.signs:
                ge(pe, g.sign_ready, NT * (H * c + h - 1))
            elif h >= 2:
                pe.wait_ge(g.arow_sb, H * c + h - 1)
            out = g.row_bank[h % 2]
            if g.signs:
                pe.matmul(out, g3_left_lo[:, h, :], g.xt_hi[p][:, :], start=True, stop=False)
                pe.matmul(out, g3_left_hi[:, h, :], g.xt_lo[p][:, :], start=False, stop=False)
                pe.matmul(out, g3_left_hi[:, h, :], g.xt_hi[p][:, :], start=False, stop=True).then_inc(g.arow_done, 1)
            else:
                pe.wait_ge(g.rows_lo_ready, c + 1)
                pe.matmul(out, spread[:, h, :], g.rows[:, :], start=True, stop=True).then_inc(g.arow_done, 1)

        def pe_rows(pe, g, c, p):
            pe.wait_ge(g.xt_lo_ready, c + 1)
            out = g.row_bank[0][0:RL, :]
            pe.matmul(out, g1_left_lo[:, :], g.xt_hi[p][:, :], start=True, stop=False)
            pe.matmul(out, g1_left_hi[:, :], g.xt_lo[p][:, :], start=False, stop=False)
            pe.matmul(out, g1_left_hi[:, :], g.xt_hi[p][:, :], start=False, stop=True).then_inc(g.rows_done, 1)

        def pe_mask_sums(pe, g, c, p):
            pe.wait_ge(g.mask_ready, c + 1)
            pe.wait_ge(g.hi_ready, c + 1)
            pe.wait_ge(g.lo_ready, c + 1)
            if not g.signs:
                pe.wait_ge(g.proj_sb, 2 * c + 2)
                pe.wait_ge(g.arow_sb, H * c + H)
            ge(pe, g.num_ready, 3 * c)
            for it in range(NT):
                for jt in range(NT):
                    for k, part in enumerate((g.xy_lo[p], g.xy_hi[p])):
                        mm = pe.matmul(gat_ps[:, it, H * XY:H * XY + H * HC],
                                       g.mask[p][:, jt, it * P:(it + 1) * P], part[:, jt, :, HC:XY],
                                       start=(jt == 0 and k == 0), stop=(jt == NT - 1 and k == 1),
                                       skip_group_check=True)
                        if g.signs:
                            mm = pe.matmul(gat_ps[:, it, 0:H * XY].rearrange("p (h e) -> p h e", h=H)[:, :, 0:HC],
                                           g.mask[p][:, jt, it * P:(it + 1) * P], part[:, jt, :, 0:HC],
                                           start=False, stop=False, skip_group_check=True)
            mm.then_inc(g.mask_mm, 1)

        def pe_head(pe, g, c, p, h):
            if not g.signs:
                pe.wait_ge(g.s_built, NT * (H * c + h + 1))
            elif h == POOL_HEAD:
                pe.wait_ge(g.s_pool, c + 1)
            else:
                pe.wait_ge(g.s_built, (H - 1) * c + h)
            for it in range(NT):
                for jt in range(NT):
                    for k, part in enumerate((g.xy_lo[p], g.xy_hi[p])):
                        mm = pe.matmul(gat_ps[:, it, h * XY:(h + 1) * XY],
                                       g.s[p][:, h, jt, it * P:(it + 1) * P], part[:, jt, h, :],
                                       start=False, stop=(jt == NT - 1 and k == 1),
                                       skip_group_check=True)
            mm.then_inc(g.s_mm, 1)

        def act_round_x(act, g, c, p):
            act.wait_ge(g.xt_done, c + 1)
            ge(act, g.arow_done, H * (c - g.depth + 1))
            act.activation(g.xt_hi[p][:, :], g.x_bank, ACT.Copy).then_inc(g.xt_hi_ready, 1)

        def act_rows(act, g, c):
            act.wait_ge(g.rows_done, c + 1)
            ge(act, g.arow_done, H * c)
            act.activation(g.rows[:, :], g.row_bank[0][0:RL, :], ACT.Copy).then_inc(g.rows_hi_ready, 1)

        def act_projection(act, g, c, p):
            for k in range(2):
                act.wait_ge(g.proj_done, 2 * c + k + 1)
                if k == 0:
                    ge(act, g.xy_ready, 2 * (c - g.depth + 1))
                    ge(act, g.t_ready, 2 * (c - g.depth + 1))
                    if g.signs:
                        ge(act, g.sign_ready, NT * H * (c - g.depth + 1))
                act.activation(g.proj[p][:, 2 * k:2 * k + 2, :],
                               g.proj_bank[k][:, 0:2 * WP].rearrange("p (t w) -> p t w", w=WP),
                               ACT.Copy).then_inc(g.proj_sb, 1)

        def act_a_row(act, g, c, h):
            act.wait_ge(g.arow_done, H * c + h + 1)
            ge(act, g.s_built, NT * H * (c - 1) + NT * (h + 1))
            act.activation(g.a_row[:, h, :], g.row_bank[h % 2], ACT.Copy).then_inc(g.arow_sb, 1)

        def act_signs(act, g, c, p, h):
            act.wait_ge(g.arow_done, H * c + h + 1)
            act.wait_ge(g.proj_sb, 2 * c + 2)
            ge(act, g.s_mm, H * (c - g.depth) + h + 1)
            for jt in range(NT):
                act.activation(g.s[p][:, h, jt, :], g.row_bank[h % 2], ACT.Sign,
                               bias=g.proj[p][:, jt, D + H + h:D + H + h + 1]).then_inc(g.sign_ready, 1)

        def act_exps(act, g, c, p):
            act.wait_ge(g.rel_ready, c + 1)
            ge(act, g.lo_ready, c)
            act.activation(g.xy[:, :, :, DH], g.b_rel[:, :, :], ACT.Exp, bias=ln_scale[:, 0:1]).then_inc(g.exp_ready, 1)
            act.activation(g.xy[:, :, :, HC + DH], g.b_rel[:, :, :], ACT.Exp, bias=ln_scale[:, 0:1],
                           scale=0.2).then_inc(g.exp_ready, 1)
            act.wait_ge(g.t_ready, 2 * c + 2)
            ge(act, g.num_ready, 3 * (c - g.depth + 1))
            act.activation(g.r[p][:, :, :], g.t[:, :, :], ACT.Exp, scale=-0.8).then_inc(g.exp_ready, 1)

        def act_round_xy(act, g, c, p):
            act.wait_ge(g.xy_ready, 2 * c + 2)
            ge(act, g.s_mm, H * (c - g.depth + 1))
            act.activation(g.xy_hi[p][:, :, :, :], g.xy[:, :, :, :], ACT.Copy).then_inc(g.hi_ready, 1)

        def act_masked(act, g, c):
            act.wait_ge(g.s_mm, H * c + H)
            act.activation(g.masked[:, :, :, :].rearrange("p t h e -> p t (h e)"),
                           gat_ps[:, :, H * XY:H * XY + H * HC], ACT.Copy).then_inc(g.masked_sb, 1)

        def pool_ball(pool, g, c):
            pool.wait_ge(g.bmax_ready, c + 1)
            ge(pool, g.t_ready, 2 * c)
            pool.nop(nofuse=True)
            pool.partition_all_reduce(g.ball[:, :], g.bmax[:, :], P, RMAX).then_inc(g.ball_ready, 1)

        def pool_xy(pool, g, c, p):
            pool.wait_ge(g.exp_ready, 3 * c + 2)
            pool.wait_ge(g.proj_sb, 2 * c + 2)
            pool.tensor_tensor(g.xy[:, :, :, HC:HC + DH], g.proj[p][:, :, 0:D].rearrange("p t (h e) -> p t h e", h=H),
                               g.xy[:, :, :, HC + DH:XY].to_broadcast([P, NT, H, DH]), ALU.mult).then_inc(g.xy_ready, 1)

        def pool_bias(pool, g, c, p):
            pool.wait_ge(g.x_ready, NT * (c + 1))
            ge(pool, g.agg_ready, 3 * c)
            pool.tensor_tensor(g.xb[:, :, :], g.x_in[p][:, :, :],
                               bias1[:, :].unsqueeze(1).to_broadcast([P, NT, D]), ALU.add).then_inc(g.xb_ready, 1)

        def pool_rstd(pool, ve, rs, ve_ready, rs_ready, c):
            pool.wait_ge(ve_ready, c + 1)
            pool.tensor_tensor(rs[:, :], ve[:, :], mhalf[:, 0:NT], ALU.pow).then_inc(rs_ready, 1)

        def dve_xt_lo(dve, g, c, p):
            dve.wait_ge(g.xt_hi_ready, c + 1)
            dve.tensor_tensor(g.xt_lo[p][:, :], g.x_bank, g.xt_hi[p][:, :].bitcast(F32),
                              ALU.subtract).then_inc(g.xt_lo_ready, 1)

        def dve_rows_lo(dve, g, c):
            dve.wait_ge(g.rows_hi_ready, c + 1)
            dve.tensor_tensor(g.rows[RL_LO:RL, :], g.row_bank[0][RL_LO:RL, :], g.rows[RL_LO:RL, :].bitcast(F32),
                              ALU.subtract).then_inc(g.rows_lo_ready, 1)

        def dve_bmax(dve, g, c, p, we_col):
            dve.wait_ge(g.proj_sb, 2 * c + 2)
            ge(dve, g.ball_ready, c)
            right = g.proj[p][:, :, D + H:WP]
            dve.tensor_reduce(g.bmax[:, :], right.rearrange("p t h -> p h t"), AX_X, ALU.max).then_inc(g.bmax_ready, 1)
            if not g.signs:
                ge(dve, g.s_built, NT * H * c)
                dve.tensor_scalar(g.nb[:, :, :], right, -1.0, we_col, ALU.mult, ALU.subtract).then_inc(g.small_ready, 1)

        def dve_scores(dve, g, c, p, we_col):
            left, right = g.proj[p][:, :, D:D + H], g.proj[p][:, :, D + H:WP]
            dve.wait_ge(g.ball_ready, c + 1)
            ball = g.ball[:, :].unsqueeze(1).to_broadcast([P, NT, H])
            ge(dve, g.exp_ready, 3 * c)
            dve.tensor_tensor(g.b_rel[:, :, :], right, ball, ALU.subtract).then_inc(g.rel_ready, 1)
            dve.tensor_tensor(g.t[:, :, :], left, ball, ALU.add).then_inc(g.t_ready, 1)
            dve.wait_ge(g.t_ready, 2 * c + 1)
            dve.tensor_scalar(g.t[:, :, :], g.t[:, :, :], we_col, 0.0, ALU.add, ALU.max).then_inc(g.t_ready, 1)

        def dve_xy(dve, g, c, p):
            dve.wait_ge(g.exp_ready, 3 * c + 1)
            dve.tensor_tensor(g.xy[:, :, :, 0:DH], g.proj[p][:, :, 0:D].rearrange("p t (h e) -> p t h e", h=H),
                              g.xy[:, :, :, DH:HC].to_broadcast([P, NT, H, DH]), ALU.mult).then_inc(g.xy_ready, 1)

        def split_xy(eng, g, c, p):
            eng.wait_ge(g.hi_ready, c + 1)
            ge(eng, g.s_mm, H * (c - g.depth + 1))
            eng.tensor_tensor(g.xy_lo[p][:, :, :, :].rearrange("p t h e -> p (t h e)"),
                              g.xy[:, :, :, :].rearrange("p t h e -> p (t h e)"),
                              g.xy_hi[p][:, :, :, :].rearrange("p t h e -> p (t h e)"), ALU.subtract).then_inc(g.lo_ready, 1)

        def dve_select(dve, g, c, p, h):
            dve.wait_ge(g.small_ready, c + 1)
            dve.wait_ge(g.arow_sb, H * c + h + 1)
            dve.wait_ge(g.mask_ready, c + 1)
            ge(dve, g.s_mm, H * (c - 1) + h + 1)
            for jt in range(NT):
                dve.scalar_tensor_tensor(g.s[p][:, h, jt, :], g.a_row[:, h, :], g.nb[:, jt, h:h + 1],
                                         g.mask[p][:, jt, :], ALU.is_gt, ALU.mult).then_inc(g.s_built, 1)

        def mask_signs(eng, g, c, p, h, done):
            eng.wait_ge(g.sign_ready, NT * (H * c + h + 1))
            eng.wait_ge(g.mask_ready, c + 1)
            eng.tensor_tensor(g.s[p][:, h, :, :].rearrange("p t n -> p (t n)"), g.s[p][:, h, :, :].rearrange("p t n -> p (t n)"),
                              g.mask[p][:, :, :].rearrange("p t n -> p (t n)"), ALU.mult).then_inc(done, 1)

        def dve_sums(dve, g, c, p):
            dve.wait_ge(g.masked_sb, c + 1)
            sums = gat_ps[:, :, 0:H * XY].rearrange("p t (h e) -> p t h e", h=H)
            dve.tensor_tensor(g.num[:, :, :, :], g.masked[:, :, :, :], sums[:, :, :, HC:XY],
                              ALU.subtract).then_inc(g.num_ready, 1)
            dve.wait_ge(g.num_ready, 3 * c + 1)
            dve.tensor_tensor(g.num[:, :, :, :], g.num[:, :, :, :],
                              g.r[p][:, :, :].unsqueeze(3).to_broadcast([P, NT, H, HC]), ALU.mult).then_inc(g.num_ready, 1)
            dve.wait_ge(g.num_ready, 3 * c + 2)
            dve.tensor_tensor(g.num[:, :, :, :], g.num[:, :, :, :], sums[:, :, :, 0:HC],
                              ALU.add).then_inc(g.num_ready, 1)

        def dve_quotient(dve, g, c, p):
            dve.wait_ge(g.num_ready, 3 * c + 3)
            dve.reciprocal(g.rden[:, :, :], g.num[:, :, :, DH]).then_inc(g.agg_ready, 1)
            dve.wait_ge(g.agg_ready, g.agg_steps * c + 1)
            ge(dve, g.out_ready, NT * (c - g.depth + 1))
            dve.tensor_tensor(g.agg[p][:, :, :].rearrange("p t (h e) -> p t h e", h=H), g.num[:, :, :, 0:DH],
                              g.rden[:, :, :].unsqueeze(3).to_broadcast([P, NT, H, DH]), ALU.mult).then_inc(g.agg_ready, 1)
            dve.wait_ge(g.agg_ready, g.agg_steps * c + 2)

        def dve_norm_stats(dve, src, stats, mv, ve, stat_ready, ve_ready, c):
            for t in range(NT):
                dve.bn_stats(stats[:, t, :], src(t)).then_inc(stat_ready, 1)
            dve.wait_ge(stat_ready, 2 * NT * c + NT)
            dve.nop(nofuse=True)
            for t in range(NT):
                dve.bn_aggr(mv[:, t, :], stats[:, t, :]).then_inc(stat_ready, 1)
            dve.wait_ge(stat_ready, 2 * NT * (c + 1))
            dve.tensor_scalar(ve[:, :], mv[:, :, 1], EPS, None, ALU.add).then_inc(ve_ready, 1)

        def dve_norm_shift(dve, mv, rs, rs_ready, shift, shift_ready, used, c):
            dve.wait_ge(rs_ready, c + 1)
            ge(dve, used, NT * c)
            dve.scalar_tensor_tensor(shift[:, :], mv[:, :, 0], -1.0, rs[:, :], ALU.mult,
                                     ALU.mult).then_inc(shift_ready, 1)

        def act_norm_apply(act, src, dst, shift, rs, shift_ready, out_ready, c):
            act.wait_ge(shift_ready, c + 1)
            for t in range(NT):
                act.activation(dst(t), src(t), ACT.Identity, bias=shift[:, t:t + 1],
                               scale=rs[:, t:t + 1]).then_inc(out_ready, 1)

        with ExitStack() as tmp:
            def s3(n, shape, dt=F32):
                return tmp.enter_context(nc.sbuf_tensor(n, shape, dt))

            def m3(n):
                return tmp.enter_context(nc.semaphore(n))
            g1 = attention(tmp, 0, "g1_", (gat_bank[0], gat_bank[1:3], [gat_bank[3], gat_bank[0]]), 3, 1, False)
            xT = [s3(f"xT{i}", [P, N]) for i in range(2)]
            xs_hi = [s3(f"x_hi{i}", [P, N], F32R) for i in range(2)]
            xs_lo = [s3(f"x_lo{i}", [P, N], F32R) for i in range(2)]
            h32 = s3("h32", [P, N])
            xc = h32
            h_hi, h_lo = s3("h_hi", [P, N + 2 * PAD], F32R), s3("h_lo", [P, N + 2 * PAD], F32R)
            s_l, s_r = s3("s_l", [96, N]), s3("s_r", [96, N])
            msg = s3("msg", [P, NT, D])
            xc_hi, xc_lo = s3("xc_hi", [P, N], F32R), s3("xc_lo", [P, N], F32R)
            nm_hi, nm_lo = s3("nm_hi", [P, N], F32R), s3("nm_lo", [P, N], F32R)
            t_r, t_z, u, cand, diff, xn, yT = (s3(n, [P, N]) for n in
                                                  ("t_r", "t_z", "u", "cand", "diff", "xn", "yT"))
            stats, mv, ve, rs = s3("stats", [P, NT, 6]), s3("mv", [P, NT, 2]), s3("ve", [P, NT]), s3("rs", [P, NT])
            shift, shift_ready = s3("shift0", [P, NT]), m3("shift0_ready")

            x_in = [m3("x_in0"), m3("x_in1")]
            adj_in = [m3("adj_in0"), m3("adj_in1")]
            (const_ready, x_hi_ready, x_lo_ready, conv1_done, h_ready, h_hi_ready, h_lo_ready, s_done, s_rows, l_rows,
             msg_done, msg_sum, msg_ready, dist_done, exp_done, att_ready, conv2_done, pre_ready, xc_ready, xc_hi_ready,
             xc_lo_ready, nmp_done, nm_hi_ready, nm_lo_ready, r_done, z_done, in_done, hn_done, r_ready, z_ready,
             rr_ready, u_ready, v_ready, cand_ready, diff_ready, xn_ready, w_ready, y_ready, yt_done, stat_ready,
             ve_ready, rs_ready) = (m3(n) for n in (
                 "const_ready x_hi_ready x_lo_ready conv1_done h_ready h_hi_ready h_lo_ready s_done s_rows l_rows "
                 "msg_done msg_sum msg_ready dist_done exp_done att_ready conv2_done pre_ready xc_ready xc_hi_ready "
                 "xc_lo_ready nmp_done nm_hi_ready nm_lo_ready r_done z_done in_done hn_done r_ready z_ready "
                 "rr_ready u_ready v_ready cand_ready diff_ready xn_ready w_ready y_ready yt_done stat_ready "
                 "ve_ready rs_ready").split())
            adj_step, deg_pow, deg0_ready, tr_done, nadj_ready = (
                m3(n) for n in "adj_step deg_pow deg0_ready tr_done nadj_ready".split())
            block = tmp.enter_context(nc.Block())
            N_CONST = 6

            def steps(eng, body):
                for b in range(4):
                    body(b, b % 2, b // 2)
                with eng.Fori(2, B // 2 - 1) as q:
                    for p in range(2):
                        body(2 * q + p, p, q)
                for b in range(B - 2, B + 3):
                    body(b, b % 2, b // 2)

            def works(b, first, last):
                return not isinstance(b, int) or first <= b <= last

            def layer0(b):
                return works(b, 0, B - 1)

            def second(b):
                return isinstance(b, int) and b == 1

            def first(b):
                return isinstance(b, int) and b == 0

            def more0(b):
                return works(b, 0, B - 2)

            def norm0(b):
                return works(b, 1, B)

            def layer1(b):
                return works(b, 2, B + 1)

            def norm1(b):
                return works(b, 3, B + 2)

            @block.sync
            def _(sp):
                def body(b, p, q):
                    if layer0(b):
                        row = bass.ds(b, 1)
                        ge(sp, xn_ready, b - 1)
                        sp.dma_start(xT[p][:, :], a["xT"][row].rearrange("a f n -> (a f) n")).then_inc(x_in[p], 16)
                        ge(sp, att_ready, NT * (b - 1))
                        ge(sp, g1.mask_ready, b - 1)
                        sp.dma_start(adjT[p][:, :, :],
                                     a["adjT"][row].rearrange("a (t p) n -> p (a t) n", p=P)).then_inc(adj_in[p], 16)
                steps(sp, body)
                sp.wait_ge(nmp_done, B)
                sp.wait_ge(g1.mask_ready, B - 1)
                for dst, src in (
                        (l2_w1, a["l2_w1"].rearrange("g f e -> f g e")),
                        (l2_w2, a["l2_w2"].rearrange("g (k e) d -> e (g k) d", k=2)),
                        (spare[0][:, W1_END:B2_END], a["l2_b2"].partition_broadcast(P))):
                    sp.dma_start(dst, src).then_inc(l2_in, 16)

            def w(c, part):
                return (w_hi, w_lo)[part][:, c:c + D]

            def mm3(pe, out, wc, hi, lo, first, last):
                pe.matmul(out, w(wc, 1), hi, start=first, stop=False)
                pe.matmul(out, w(wc, 0), lo, start=False, stop=False)
                return pe.matmul(out, w(wc, 0), hi, start=False, stop=last)

            @block.tensor
            def _(pe):
                def adjacency_transposes(g):
                    pe.wait_ge(adj_step, 6)
                    if g == 4:
                        pe.wait_ge(nadj_ready, PACK)
                    for k in range(NPACK):
                        mm = pe.transpose(gat_bank[g % 4][:, k * P:(k + 1) * P], ag[:, g, k, :], ident[:, :])
                    mm.then_inc(tr_done, 1)

                def conv2_taps(b, lo, hi):
                    for k in range(lo, hi):
                        mm = mm3(pe, bank_b[:, :], C2 + k * D, h_hi[:, k:k + N], h_lo[:, k:k + N],
                                 k == 0, k == TAPS - 1)
                    return mm

                def distance(b, t):
                    if t >= 2:
                        pe.wait_ge(exp_done, NT * b + t - 1)
                    pe.matmul((bank_c, bank_d)[t % 2][:, :], s_l[:, t * P:(t + 1) * P], s_r[:, :],
                              start=True, stop=True).then_inc(dist_done, 1)

                def body(b, p, q):
                    c = b - 2
                    x_hi, x_lo = xs_hi[p], xs_lo[p]
                    if layer0(b):
                        pe.wait_ge(x_hi_ready, b + 1)
                        pe.wait_ge(x_lo_ready, b + 1)
                        ge(pe, r_ready, b)
                        mm3(pe, bank_a[:, :], C1, x_hi[:, :], x_lo[:, :], True, True).then_inc(conv1_done, 1)
                        ge(pe, z_ready, b)
                        wlo, whi = w_lo[:, CS:CS + 96], w_hi[:, CS:CS + 96]
                        pe.matmul(bank_b[0:96, :], wlo, x_hi[:, :], start=True, stop=False)
                        pe.matmul(bank_b[0:96, :], whi, x_lo[:, :], start=False, stop=False)
                        pe.matmul(bank_b[0:96, :], whi, x_hi[:, :], start=False, stop=True).then_inc(s_done, 1)
                    if norm1(b):
                        pe_head(pe, g1, c - 1, 1 - p, 3)
                    if layer0(b):
                        pe.wait_ge(h_ready, b + 1)
                        for t in range(NT):
                            out = bank_a[:, t * D:(t + 1) * D]
                            tok = slice(t * P, (t + 1) * P)
                            pe.matmul(out, x_lo[:, tok], w(CM, 0), start=True, stop=False)
                            pe.matmul(out, x_hi[:, tok], w(CM, 1), start=False, stop=False)
                            mm = pe.matmul(out, x_hi[:, tok], w(CM, 0), start=False, stop=True)
                        mm.then_inc(msg_done, 1)
                        if first(b):
                            pe.wait_ge(const_ready, N_CONST)
                        pe.wait_ge(l_rows, 2 * b + 2)
                        ge(pe, v_ready, b)
                        ge(pe, u_ready, b)
                        distance(b, 0)
                        distance(b, 1)
                    if isinstance(b, int) and b == 2:
                        pe.wait_ge(nadj_ready, GROUPS * PACK)
                    if layer1(b):
                        pe_transpose_x(pe, g1, c, lambda t: g1.x_in[p][:, t, :])
                    if layer0(b):
                        distance(b, 2)
                        distance(b, 3)
                    if layer1(b):
                        pe_rows(pe, g1, c, p)
                        pe_project(pe, g1, c, p)
                    if layer0(b):
                        pe.wait_ge(h_hi_ready, b + 1)
                        pe.wait_ge(h_lo_ready, b + 1)
                        conv2_taps(b, 0, 3)
                    if layer1(b):
                        pe_a_row(pe, g1, c, p, 0)
                        pe_a_row(pe, g1, c, p, 1)
                    if layer0(b):
                        conv2_taps(b, 3, 5)
                    if layer1(b):
                        pe_a_row(pe, g1, c, p, 2)
                        pe_a_row(pe, g1, c, p, 3)
                    if layer0(b):
                        conv2_taps(b, 5, TAPS).then_inc(conv2_done, 1)
                    if second(b):
                        for g in range(4):
                            adjacency_transposes(g)
                    if layer1(b):
                        pe_mask_sums(pe, g1, c, p)
                        pe_head(pe, g1, c, p, 0)
                    if norm0(b):
                        pe.wait_ge(y_ready, b)
                        ge(pe, exp_done, NT * (b + 1) if layer0(b) else 0)
                        for t in range(NT):
                            mm = pe.transpose(bank_d[:, t * P:(t + 1) * P], yT[:, t * P:(t + 1) * P], ident[:, :])
                        mm.then_inc(yt_done, 1)
                    if layer0(b):
                        pe.wait_ge(att_ready, NT * (b + 1))
                        pe.wait_ge(msg_ready, b + 1)
                        pe.wait_ge(exp_done, NT * (b + 1))
                        for t in range(NT):
                            mm = pe.matmul(bank_c[:, :], msg[:, t, :], expd[:, t, :], start=(t == 0), stop=(t == NT - 1))
                        mm.then_inc(nmp_done, 1)
                        mm3(pe, bank_a[:, :], CG + 6 * D, x_hi[:, :], x_lo[:, :], True, False)
                    if layer1(b):
                        pe_head(pe, g1, c, p, 1)
                    if layer0(b):
                        pe.wait_ge(xc_hi_ready, b + 1)
                        pe.wait_ge(xc_lo_ready, b + 1)
                        mm3(pe, bank_a[:, :], CG, xc_hi[:, :], xc_lo[:, :], False, False)
                        mm3(pe, bank_b[:, :], CG + 7 * D, x_hi[:, :], x_lo[:, :], True, False)
                        mm3(pe, bank_b[:, :], CG + D, xc_hi[:, :], xc_lo[:, :], False, False)
                    if layer1(b):
                        pe_head(pe, g1, c, p, 2)
                    if layer0(b):
                        pe.wait_ge(nm_lo_ready, b + 1)
                        mm3(pe, bank_a[:, :], CG + 3 * D, nm_hi[:, :], nm_lo[:, :], False, True).then_inc(r_done, 1)
                        ge(pe, g1.x_ready, NT * b)
                        mm3(pe, bank_d[:, :], CG + 8 * D, x_hi[:, :], x_lo[:, :], True, True).then_inc(hn_done, 1)
                        mm3(pe, bank_c[:, :], CG + 2 * D, xc_hi[:, :], xc_lo[:, :], True, False)
                        mm3(pe, bank_c[:, :], CG + 5 * D, nm_hi[:, :], nm_lo[:, :], False, True).then_inc(in_done, 1)
                        mm3(pe, bank_b[:, :], CG + 4 * D, nm_hi[:, :], nm_lo[:, :], False, True).then_inc(z_done, 1)
                    if second(b):
                        adjacency_transposes(4)
                steps(pe, body)

            @block.scalar
            def _(act):
                act.activation(warm[:, :], zero1[:, :], ACT.Exp)

                def body(b, p, q):
                    c = b - 2

                    def distances_exp(t):
                        act.wait_ge(dist_done, NT * b + t + 1)
                        ge(act, nmp_done, b)
                        act.activation(expd[:, t, :], (bank_c, bank_d)[t % 2][:, :], ACT.Exp).then_inc(exp_done, 1)
                    if layer0(b):
                        act.wait_ge(conv1_done, b + 1)
                        ge(act, xc_hi_ready, b)
                        ge(act, xc_lo_ready, b)
                        act.activation(h32[:, :], bank_a[:, :], ACT.Relu, bias=bn_sh[:, 0:1],
                                       scale=bn_sc[:, 0:1]).then_inc(h_ready, 1)
                        if first(b):
                            act.wait_ge(const_ready, N_CONST)
                        act.wait_ge(s_done, b + 1)
                        ge(act, dist_done, NT * b)
                        act.activation(s_r[0:32, :], bank_b[0:32, :], ACT.Identity,
                                       bias=bse[0:32, :]).then_inc(s_rows, 1)
                        act.activation(s_r[64:96, :], bank_b[64:96, :], ACT.Square,
                                       bias=bse[64:96, :]).then_inc(s_rows, 1)
                    if norm1(b):
                        act_masked(act, g1, c - 1)
                    if layer0(b):
                        distances_exp(0)
                        distances_exp(1)
                    if layer1(b):
                        act_round_x(act, g1, c, p)
                    if layer0(b):
                        distances_exp(2)
                        distances_exp(3)
                    if layer1(b):
                        act_rows(act, g1, c)
                        act_projection(act, g1, c, p)
                        act_a_row(act, g1, c, 0)
                        act_a_row(act, g1, c, 1)
                        act_exps(act, g1, c, p)
                        act_a_row(act, g1, c, 2)
                        act_a_row(act, g1, c, 3)
                        act_round_xy(act, g1, c, p)
                    if norm1(b):
                        act_norm_apply(act, lambda t: g1.y[1 - p][:, t, :],
                                       lambda t: xres[:, bass.ds(b - 3, 1), t, :].rearrange("p a d -> p (a d)"),
                                       g1.shift, g1.rs, g1.shift_ready, g1.out_ready, b - 3)
                    if layer0(b):
                        act.wait_ge(pre_ready, b + 1)
                        act.activation(xc[:, :], xc[:, :], ACT.Relu, bias=bn_sh[:, 1:2]).then_inc(xc_ready, 1)
                        act.wait_ge(nmp_done, b + 1)
                        ge(act, z_done, b)
                        act.activation(nm_hi[:, :], bank_c[:, :], ACT.Copy).then_inc(nm_hi_ready, 1)
                    if norm0(b):
                        ge(act, g1.y_ready, 2 * (b - 2))
                        act_norm_apply(act, lambda t: bank_d[:, t * P:(t + 1) * P], lambda t: g1.x_in[1 - p][:, t, :],
                                       shift, rs, shift_ready, g1.x_ready, b - 1)
                    if layer0(b):
                        act.wait_ge(r_done, b + 1)
                        ge(act, u_ready, b)
                        act.activation(t_r[:, :], bank_a[:, :], ACT.Tanh, bias=half_b[:, 0:1],
                                       scale=0.5).then_inc(r_ready, 1)
                        act.wait_ge(z_done, b + 1)
                        ge(act, w_ready, b)
                        act.activation(t_z[:, :], bank_b[:, :], ACT.Tanh, bias=half_b[:, 1:2],
                                       scale=0.5).then_inc(z_ready, 1)
                        act.wait_ge(v_ready, b + 1)
                        ge(act, xn_ready, b)
                        act.activation(cand[:, :], u[:, :], ACT.Tanh, bias=cols[:, 10:11]).then_inc(cand_ready, 1)
                steps(act, body)

            @block.gpsimd
            def _(pool):
                def split_x(b, p):
                    pool.wait_ge(x_hi_ready, b + 1)
                    ge(pool, z_done, b - 1)
                    pool.tensor_tensor(xs_lo[p][:, :], xT[p][:, :], xs_hi[p][:, :].bitcast(F32),
                                       ALU.subtract).then_inc(x_lo_ready, 1)

                def body(b, p, q):
                    c, o = b - 2, 1 - p
                    if layer0(b):
                        pool.wait_ge(h_hi_ready, b + 1)
                        pool.tensor_tensor(h_lo[:, PAD:PAD + N], h32[:, :], h_hi[:, PAD:PAD + N].bitcast(F32),
                                           ALU.subtract).then_inc(h_lo_ready, 1)
                    if norm0(b):
                        pool.wait_ge(cand_ready, b)
                        ge(pool, w_ready, b - 1)
                        pool.tensor_tensor(diff[:, :], xT[o][:, :], cand[:, :], ALU.subtract).then_inc(diff_ready, 1)
                        ge(pool, y_ready, b - 1)
                        pool.tensor_tensor(xn[:, :], xT[o][:, :], cand[:, :], ALU.add).then_inc(xn_ready, 1)
                    if layer1(b):
                        pool_ball(pool, g1, c)
                        pool_xy(pool, g1, c, p)
                    if norm1(b):
                        ge(pool, g1.out_ready, NT * (b - 3))
                        pool_rstd(pool, g1.ve, g1.rs, g1.ve_ready, g1.rs_ready, c - 1)
                    if layer1(b):
                        split_xy(pool, g1, c, p)
                    if layer0(b):
                        pool.wait_ge(adj_in[p], 16 * (q + 1))
                        for t in range(NT):
                            pool.wait_ge(exp_done, NT * b + t + 1)
                            pool.tensor_tensor(expd[:, t, :], expd[:, t, :], adjT[p][:, t, :],
                                               ALU.mult).then_inc(att_ready, 1)
                    if first(b):
                        pool.wait_ge(adj_step, 4)
                        pool.tensor_tensor(deg[:, :], deg[:, :], mhalf[:, :], ALU.pow).then_inc(deg_pow, 1)
                    if layer1(b):
                        pool_bias(pool, g1, c, p)
                    if layer0(b):
                        pool.wait_ge(xc_hi_ready, b + 1)
                        pool.tensor_tensor(xc_lo[:, :], xc[:, :], xc_hi[:, :].bitcast(F32),
                                           ALU.subtract).then_inc(xc_lo_ready, 1)
                    if norm0(b):
                        ge(pool, g1.x_ready, NT * (b - 1))
                        pool_rstd(pool, ve, rs, ve_ready, rs_ready, b - 1)
                    if more0(b):
                        split_x(b + 1, o)
                split_x(0, 0)
                for k, (dst, value) in enumerate((
                        (s_l[:, :], 0.0), (s_r[:, :], 0.0), (s_l[64:96, :], -1.0), (s_r[32:64, :], 1.0),
                        (h_hi[:, :].bitcast(F32), 0.0), (h_lo[:, :].bitcast(F32), 0.0))):
                    ge(pool, const_ready, k)
                    pool.memset(dst, value).then_inc(const_ready, 1)
                pool.wait_ge(const_ready, N_CONST)
                steps(pool, body)

            @block.vector
            def _(dve):
                def split_x(b, p, q):
                    dve.wait_ge(x_in[p], 16 * (q + 1))
                    ge(dve, z_done, b - 1)
                    dve.tensor_copy(xs_hi[p][:, :], xT[p][:, :]).then_inc(x_hi_ready, 1)

                def adjacency_degrees():
                    dve.wait_ge(adj2_in, 16 * 2)
                    dve.tensor_tensor(adjb, adjb, ident.unsqueeze(1).to_broadcast([P, NPACK, P]),
                                      ALU.add).then_inc(adj_step, 1)
                    dve.wait_ge(adj_step, 1)
                    for g in range(GROUPS):
                        part = dve.scalar_tensor_tensor(ag[:, g, :, :], adjb, in_group[:, g:g + 1],
                                                        group_row[:, g, :].unsqueeze(1).to_broadcast([P, NPACK, P]),
                                                        ALU.mult, ALU.mult)
                    part.then_inc(adj_step, 1)
                    dve.wait_ge(adj_step, 2)
                    dve.tensor_reduce(deg[:, :], ag.rearrange("p g k n -> p (g k) n"), AX_X,
                                      ALU.add).then_inc(adj_step, 1)
                    dve.wait_ge(adj_step, 3)
                    dve.tensor_scalar(deg0[:, :], deg[:, :], 0.0, None, ALU.is_equal).then_inc(deg0_ready, 1)
                    dve.wait_ge(deg0_ready, 1)
                    dve.tensor_tensor(deg[:, :], deg[:, :], deg0[:, :], ALU.add).then_inc(adj_step, 1)
                    dve.tensor_scalar(deg0[:, :], deg0[:, :], -1.0, 1.0, ALU.mult, ALU.add).then_inc(deg0_ready, 1)

                def adjacency_rows():
                    dve.wait_ge(deg_pow, 1)
                    dve.wait_ge(deg0_ready, 2)
                    dve.tensor_tensor(deg[:, :], deg[:, :], deg0[:, :], ALU.mult).then_inc(adj_step, 1)
                    dve.wait_ge(adj_step, 5)
                    rows = ag.rearrange("p g k n -> p (g k) n")
                    dve.tensor_tensor(rows, rows, deg[:, :].unsqueeze(2).to_broadcast([P, GROUPS * NPACK, P]),
                                      ALU.mult).then_inc(adj_step, 1)

                def adjacency_out(g):
                    dve.wait_ge(tr_done, g + 1)
                    blocks = gat_bank[g % 4].rearrange("p (k n) -> p k n", n=P)
                    for r in range(PACK):
                        at = slice(SLOT * r, SLOT * (r + 1))
                        dve.tensor_tensor(nadj[at, g, :, :], blocks[at, :, at],
                                          deg[at, g * NPACK:(g + 1) * NPACK].unsqueeze(2).to_broadcast([SLOT, NPACK, SLOT]),
                                          ALU.mult).then_inc(nadj_ready, 1)

                def body(b, p, q):
                    c, e, o = b - 2, b - 3, 1 - p
                    if layer0(b):
                        dve.wait_ge(h_ready, b + 1)
                        ge(dve, conv2_done, b)
                        dve.tensor_copy(h_hi[:, PAD:PAD + N], h32[:, :]).then_inc(h_hi_ready, 1)
                        dve.wait_ge(s_rows, 2 * b + 2)
                        dve.tensor_scalar(s_l[0:32, :], s_r[0:32, :], 2.0, None, ALU.mult).then_inc(l_rows, 1)
                        dve.tensor_scalar(s_l[32:64, :], s_r[64:96, :], -1.0, None, ALU.mult).then_inc(l_rows, 1)
                    if norm1(b):
                        dve_sums(dve, g1, e, o)
                    if layer0(b):
                        dve.wait_ge(msg_done, b + 1)
                        ge(dve, nmp_done, b)
                        dve.tensor_tensor(msg[:, :, :], bank_a[:, :].rearrange("p (t d) -> p t d", t=NT),
                                          bmsg[:, :].unsqueeze(1).to_broadcast([P, NT, D]), ALU.add).then_inc(msg_sum, 1)
                        dve.wait_ge(msg_sum, b + 1)
                        dve.tensor_scalar(msg[:, :, :], msg[:, :, :], 0.0, None, ALU.max).then_inc(msg_ready, 1)
                    if first(b):
                        adjacency_degrees()
                    if second(b):
                        adjacency_rows()
                    if layer1(b):
                        dve_xt_lo(dve, g1, c, p)
                    if norm1(b):
                        dve_quotient(dve, g1, e, o)
                        dve.wait_ge(g1.xb_ready, e + 1)
                        dve.tensor_tensor(g1.agg[o][:, :, :], g1.agg[o][:, :, :], g1.xb[:, :, :],
                                          ALU.add).then_inc(g1.agg_ready, 1)
                    if layer1(b):
                        dve_rows_lo(dve, g1, c)
                    if norm1(b):
                        dve.wait_ge(g1.agg_ready, 3 * e + 3)
                        dve.scalar_tensor_tensor(g1.y[o][:, :, :], g1.agg[o][:, :, :], 0.5, g1.agg[o][:, :, :],
                                                 ALU.mult, ALU.max).then_inc(g1.y_ready, 1)
                        dve.wait_ge(g1.y_ready, 2 * e + 1)
                        dve.tensor_tensor(g1.y[o][:, :, :], g1.y[o][:, :, :], g1.x_in[o][:, :, :],
                                          ALU.add).then_inc(g1.y_ready, 1)
                        dve.wait_ge(g1.y_ready, 2 * e + 2)
                        dve_norm_stats(dve, lambda t: g1.y[o][:, t, :], g1.stats, g1.mv, g1.ve,
                                       g1.stat_ready, g1.ve_ready, e)
                    if layer1(b):
                        dve_bmax(dve, g1, c, p, we[:, 0:1])
                        dve_scores(dve, g1, c, p, we[:, 0:1])
                    if norm0(b):
                        dve.wait_ge(diff_ready, b)
                        dve.wait_ge(z_ready, b)
                        dve.scalar_tensor_tensor(u[:, :], t_z[:, :], 1.0, diff[:, :],
                                                 ALU.add, ALU.mult).then_inc(w_ready, 1)
                        dve.wait_ge(w_ready, b)
                        dve.wait_ge(xn_ready, b)
                        ge(dve, yt_done, b - 1)
                        dve.scalar_tensor_tensor(yT[:, :], u[:, :], 0.5, xn[:, :],
                                                 ALU.mult, ALU.add).then_inc(y_ready, 1)
                    if layer1(b):
                        dve_xy(dve, g1, c, p)
                    if norm1(b):
                        dve_norm_shift(dve, g1.mv, g1.rs, g1.rs_ready, g1.shift, g1.shift_ready, g1.out_ready, e)
                    if layer1(b):
                        dve_select(dve, g1, c, p, 0)
                        dve_select(dve, g1, c, p, 1)
                    if norm0(b):
                        if norm1(b):
                            dve.wait_ge(g1.s_built, NT * H * (e + 1))
                            dve.wait_ge(g1.mask_mm, e + 1)
                        dve.wait_ge(adj_in[o], 16 * (q + p))
                        dve.tensor_scalar(g1.mask[o][:, :, :], adjT[o][:, :, :], 0.0, None,
                                          ALU.is_gt).then_inc(g1.mask_ready, 1)
                    if layer0(b):
                        dve.wait_ge(conv2_done, b + 1)
                        dve.wait_ge(h_lo_ready, b + 1)
                        dve.scalar_tensor_tensor(xc[:, :], bank_b[:, :], bn_sc[:, 1:2], xT[p][:, :],
                                                 ALU.mult, ALU.add).then_inc(pre_ready, 1)
                    if layer1(b):
                        dve_select(dve, g1, c, p, 2)
                    if layer0(b):
                        dve.wait_ge(xc_ready, b + 1)
                        ge(dve, z_done, b)
                        dve.tensor_copy(xc_hi[:, :], xc[:, :]).then_inc(xc_hi_ready, 1)
                    if second(b):
                        for g in range(4):
                            adjacency_out(g)
                    if norm0(b):
                        dve.wait_ge(yt_done, b)
                        dve_norm_stats(dve, lambda t: bank_d[:, t * P:(t + 1) * P], stats, mv, ve,
                                       stat_ready, ve_ready, b - 1)
                    if layer0(b):
                        dve.wait_ge(nm_hi_ready, b + 1)
                        dve.tensor_tensor(nm_lo[:, :], bank_c[:, :], nm_hi[:, :].bitcast(F32),
                                          ALU.subtract).then_inc(nm_lo_ready, 1)
                    if more0(b):
                        split_x(b + 1, o, q + p)
                    if norm0(b):
                        dve_norm_shift(dve, mv, rs, rs_ready, shift, shift_ready, g1.x_ready, b - 1)
                    if layer1(b):
                        dve_select(dve, g1, c, p, 3)
                    if layer0(b):
                        dve.wait_ge(r_ready, b + 1)
                        dve.tensor_scalar(t_r[:, :], t_r[:, :], 0.5, 0.5, ALU.mult, ALU.add).then_inc(rr_ready, 1)
                        dve.wait_ge(hn_done, b + 1)
                        dve.wait_ge(rr_ready, b + 1)
                        dve.scalar_tensor_tensor(u[:, :], bank_d[:, :], cols[:, 13:14], t_r[:, :],
                                                 ALU.add, ALU.mult).then_inc(u_ready, 1)
                        dve.wait_ge(in_done, b + 1)
                        dve.wait_ge(u_ready, b + 1)
                        dve.tensor_tensor(u[:, :], bank_c[:, :], u[:, :], ALU.add).then_inc(v_ready, 1)
                    if second(b):
                        adjacency_out(4)
                split_x(0, 0, 0)
                dve.wait_ge(const_ready, N_CONST)
                steps(dve, body)


        with ExitStack() as tmp:
            def s4(n, shape, dt=F32):
                return tmp.enter_context(nc.sbuf_tensor("l2_" + n, shape, dt))

            def m4(n):
                return tmp.enter_context(nc.semaphore("l2_" + n))
            nadj_z, nadj_o = s4("nadj_z", [P, GROUPS, P]), s4("nadj_o", [P, GROUPS, P])
            x4 = s4("x4", [P, D])
            zt = s4("zt", [P, GROUPS, P])
            ht = s4("ht", [P, 2 * GROUPS, P])
            sup = s4("sup", [P, GROUPS, D])
            og = s4("og", [P, GROUPS, D])
            acc = s4("acc", [P, D])
            back = s4("back", [SLOT, PACK, D])
            (nadj_zeroed, nadjz_ready, x4_ready, nadj_placed, z_done2, z_sb, h_done, h_sb, sup_done, sup_sb, o_done, o_read, acc_step,
             back_ready, pack_done) = (
                m4(n) for n in ("nadj_zeroed nadjz_ready x4_ready nadj_placed z_done z_sb h_done h_sb sup_done sup_sb o_done o_read acc_step "
                                "back_ready pack_done").split())
            block = tmp.enter_context(nc.Block())
            z_banks, sup_banks, o_banks = gat_bank[1:3], (bank_d[:, :], gat_bank[0]), (gat_bank[3], gat_bank[0])
            halves = ((slice(0, 4), 4), (slice(4, 5), 1))

            def packs(eng, body):
                body(0)
                with eng.Fori(1, NPACK - 1) as q:
                    body(q)
                body(NPACK - 1)

            def diagonal(dst, q, r):
                at = slice(SLOT * r, SLOT * (r + 1))
                return dst[at, :, at], nadj[at, :, bass.ds(q, 1), :].rearrange("p g a n -> p (g a) n")

            def has_next(q):
                return not isinstance(q, int) or q < NPACK - 1

            def has_last(q):
                return not isinstance(q, int) or q > 0

            @block.gpsimd
            def _(pool):
                pool.memset(nadj_z[:, :, :], 0.0).then_inc(nadj_zeroed, 1)
                pool.memset(nadj_o[:, :, :], 0.0).then_inc(nadj_zeroed, 1)

            @block.tensor
            def _(pe):
                def product_z(q):
                    pe.wait_ge(x4_ready, PACK * (q + 1))
                    pe.wait_ge(nadjz_ready, PACK * (q + 1))
                    ge(pe, z_sb, 2 * q)
                    for k, (gs, n) in enumerate(halves):
                        pe.matmul(z_banks[k][:, 0:n * P], x4[:, :], nadj_z[:, gs, :].rearrange("p g n -> p (g n)"),
                                  start=True, stop=True).then_inc(z_done2, 1)

                def product_o(q):
                    pe.wait_ge(sup_sb, 2 * q + 2)
                    pe.wait_ge(nadj_placed, PACK * (q + 1))
                    ge(pe, o_read, 2 * q)
                    for g in range(GROUPS):
                        mm = pe.matmul(o_banks[g // 4][:, (g % 4) * D:(g % 4 + 1) * D], nadj_o[:, g, :],
                                       sup[:, g, :], start=True, stop=True)
                        if g >= 3:
                            mm.then_inc(o_done, 1)
                pe.wait_ge(l2_in, 16 * 3)
                product_z(0)

                def body(q):
                    pe.wait_ge(z_sb, 2 * q + 2)
                    ge(pe, h_sb, 2 * GROUPS * q)
                    for i in range(2 * GROUPS):
                        g, half = i // 2, i % 2
                        pe.matmul((bank_a, bank_b, bank_c)[i // 4][:, (i % 4) * P:(i % 4 + 1) * P],
                                  l2_w1[:, g, half * P:(half + 1) * P], zt[:, g, :],
                                  start=True, stop=True).then_inc(h_done, 1)
                    if has_last(q):
                        product_o(q - 1)
                    if has_next(q):
                        product_z(q + 1)
                    for g in range(GROUPS):
                        pe.wait_ge(h_sb, 2 * GROUPS * q + 2 * g + 2)
                        if g == 4:
                            ge(pe, o_read, 2 * q)
                        for half in range(2):
                            mm = pe.matmul(sup_banks[g // 4][:, (g % 4) * D:(g % 4 + 1) * D],
                                           ht[:, 2 * g + half, :], l2_w2[:, 2 * g + half, :],
                                           start=(half == 0), stop=(half == 1))
                        if g >= 3:
                            mm.then_inc(sup_done, 1)
                packs(pe, body)
                product_o(NPACK - 1)

            @block.scalar
            def _(act):
                def copy_z(q):
                    ge(act, h_done, 2 * GROUPS * q)
                    for k, (gs, n) in enumerate(halves):
                        act.wait_ge(z_done2, 2 * q + k + 1)
                        act.activation(zt[:, gs, :].rearrange("p g n -> p (g n)"), z_banks[k][:, 0:n * P],
                                       ACT.Copy).then_inc(z_sb, 1)
                act.wait_ge(l2_in, 16 * 3)
                act.wait_ge(nadj_zeroed, 2)
                copy_z(0)

                def body(q):
                    ge(act, sup_done, 2 * q)
                    for i in range(2 * GROUPS):
                        act.wait_ge(h_done, 2 * GROUPS * q + min(4 * (i // 4) + 4, 2 * GROUPS))
                        act.activation(ht[:, i, :], (bank_a, bank_b, bank_c)[i // 4][:, (i % 4) * P:(i % 4 + 1) * P],
                                       ACT.Relu, bias=l2_b1[:, i:i + 1]).then_inc(h_sb, 1)
                    if has_next(q):
                        copy_z(q + 1)
                    ge(act, o_done, 2 * q)
                    for r in range(PACK):
                        act.activation(*diagonal(nadj_o, q, r), ACT.Copy).then_inc(nadj_placed, 1)
                    for k, (gs, n) in enumerate(halves):
                        act.wait_ge(sup_done, 2 * q + k + 1)
                        act.activation(sup[:, gs, :].rearrange("p g d -> p (g d)"), sup_banks[k][:, 0:n * D],
                                       ACT.Copy).then_inc(sup_sb, 1)
                packs(act, body)

            @block.vector
            def _(dve):
                dve.wait_ge(l2_in, 16 * 3)

                def gather(q):
                    ge(dve, z_done2, 2 * q)
                    for r in range(PACK):
                        dve.tensor_copy(x4[SLOT * r:SLOT * (r + 1), :],
                                        xres[0:SLOT, bass.ds(PACK * q + r, 1), 0, :].rearrange("p a d -> p (a d)")
                                        ).then_inc(x4_ready, 1)
                    for r in range(PACK):
                        dve.tensor_copy(*diagonal(nadj_z, q, r)).then_inc(nadjz_ready, 1)

                def finish(q):
                    for k, (gs, n) in enumerate(halves):
                        dve.wait_ge(o_done, 2 * q + k + 1)
                        dve.tensor_tensor(og[:, gs, :], o_banks[k][:, 0:n * D].rearrange("p (g d) -> p g d", d=D),
                                          l2_b2[:, gs, :], ALU.add).then_inc(o_read, 1)
                    dve.wait_ge(o_read, 2 * q + 2)
                    dve.tensor_scalar(og[:, :, :], og[:, :, :], 0.0, None, ALU.max).then_inc(acc_step, 1)
                    dve.wait_ge(acc_step, 6 * q + 1)
                    dve.tensor_scalar(acc[:, :], og[:, 0, :], gw_n[:, 0:1], None, ALU.mult).then_inc(acc_step, 1)
                    for g in range(1, GROUPS):
                        dve.wait_ge(acc_step, 6 * q + 1 + g)
                        dve.scalar_tensor_tensor(acc[:, :], og[:, g, :], gw_n[:, g:g + 1], acc[:, :],
                                                 ALU.mult, ALU.add).then_inc(acc_step, 1)
                    dve.wait_ge(acc_step, 6 * q + 6)
                    for r in range(PACK):
                        dve.tensor_copy(back[:, r, :], acc[SLOT * r:SLOT * (r + 1), :]).then_inc(back_ready, 1)
                    dve.wait_ge(back_ready, PACK * (q + 1))
                    for r in range(PACK):
                        row = xres[0:NODES, bass.ds(PACK * q + r, 1), 0, :].rearrange("p a d -> p (a d)")
                        dve.tensor_tensor(row, row, back[0:NODES, r, :], ALU.add).then_inc(pack_done, 1)
                dve.wait_ge(nadj_zeroed, 2)
                gather(0)

                def body(q):
                    if has_next(q):
                        gather(q + 1)
                    if has_last(q):
                        finish(q - 1)
                packs(dve, body)
                finish(NPACK - 1)

        with ExitStack() as tmp:
            def s5(n, shape, dt=F32):
                return tmp.enter_context(nc.sbuf_tensor(n, shape, dt))

            def m5(n):
                return tmp.enter_context(nc.semaphore(n))
            g3 = attention(tmp, 1, "g3_", (bank_a[:, :], [bank_b[:, :], bank_a[:, :]], [bank_c[:, :], bank_d[:, :]]), 2, 2, True)
            out_t = [s5(f"out_t{i}", [P, NT, D]) for i in range(2)]
            stats, mv, ve, rs = (s5("c_stats", [P, NT, 6]), s5("c_mv", [P, NT, 2]), s5("c_ve", [P, NT]),
                                 s5("c_rs", [P, NT]))
            adj_in = [m5("c_adj_in0"), m5("c_adj_in1")]
            stored = [m5("stored0"), m5("stored1")]
            shift = s5("shift", [P, NT])
            stat_ready, ve_ready, rs_ready = m5("c_stat_ready"), m5("c_ve_ready"), m5("c_rs_ready")
            shift_ready, x_kept = m5("shift_ready"), m5("x_kept")
            block = tmp.enter_context(nc.Block())

            def steps(eng, body):
                for n in range(4):
                    body(n, n % 2, n // 2)
                with eng.Fori(2, B // 2 - 1) as q:
                    for p in range(2):
                        body(2 * q + p, p, q)
                for n in range(B - 2, B + 2):
                    body(n, n % 2, n // 2)

            def works(n, first, last):
                return not isinstance(n, int) or first <= n <= last

            def front(n):
                return works(n, 0, B - 1)

            def main(n):
                return works(n, 1, B)

            def tail(n):
                return works(n, 2, B + 1)

            def more(n):
                return works(n, 0, B - 2)

            def more2(n):
                return works(n, 0, B - 3)

            def x2(n, t):
                return xres[:, bass.ds(n, 1), t, :].rearrange("p a d -> p (a d)")

            @block.sync
            def _(sp):
                def load_adj(m, p):
                    ge(sp, g3.mask_ready, m - 1)
                    sp.dma_start(adjT[p][:, :, :],
                                 a["adjT"][bass.ds(m, 1)].rearrange("a (t p) n -> p (a t) n", p=P)
                                 ).then_inc(adj_in[p], 16)
                load_adj(0, 0)

                def body(n, p, q):
                    if more(n):
                        load_adj(n + 1, 1 - p)
                    if tail(n):
                        sp.wait_ge(g3.out_ready, NT * (n - 1))
                        sp.dma_start(a["out"][bass.ds(n - 2, 1)].rearrange("a (t p) d -> p (a t) d", p=P),
                                     out_t[p][:, :, :]).then_inc(stored[p], 16)
                steps(sp, body)
                for p in range(2):
                    sp.wait_ge(stored[p], 16 * (B // 2))

            @block.tensor
            def _(pe):
                pe_transpose_x(pe, g3, 0, lambda t: g3.x_in[0][:, t, :])
                pe_project(pe, g3, 0, 0)
                pe_a_row(pe, g3, 0, 0, 0)

                def body(n, p, q):
                    c, o = n - 1, 1 - p
                    if front(n):
                        pe_a_row(pe, g3, n, p, 1)
                    if more(n):
                        pe_transpose_x(pe, g3, n + 1, lambda t: g3.x_in[0][:, t, :])
                    if main(n):
                        pe_head(pe, g3, c, o, 0)
                        pe_head(pe, g3, c, o, 1)
                    if front(n):
                        pe_a_row(pe, g3, n, p, 2)
                    if main(n):
                        pe_head(pe, g3, c, o, 2)
                    if more(n):
                        pe_project(pe, g3, n + 1, o)
                    if main(n):
                        pe_head(pe, g3, c, o, 3)
                    if front(n):
                        pe_a_row(pe, g3, n, p, 3)
                    if more(n):
                        pe_a_row(pe, g3, n + 1, o, 0)
                    if front(n):
                        pe_mask_sums(pe, g3, n, p)
                steps(pe, body)

            @block.scalar
            def _(act):
                act.activation(warm[:, :], zero1[:, :], ACT.Exp)

                def norm2(m):
                    ge(act, g3.xt_done, m)
                    ge(act, x_kept, m)
                    act_norm_apply(act, lambda t: x2(m, t), lambda t: g3.x_in[0][:, t, :],
                                   shift, rs, shift_ready, g3.x_ready, m)
                norm2(0)
                act_round_x(act, g3, 0, 0)
                act_projection(act, g3, 0, 0)

                def body(n, p, q):
                    o = 1 - p
                    if front(n):
                        act_signs(act, g3, n, p, 0)
                        act_exps(act, g3, n, p)
                    if more(n):
                        norm2(n + 1)
                    if front(n):
                        act_signs(act, g3, n, p, 1)
                    if more(n):
                        act_round_x(act, g3, n + 1, o)
                    if front(n):
                        act_round_xy(act, g3, n, p)
                        act_signs(act, g3, n, p, 2)
                    if more(n):
                        act_projection(act, g3, n + 1, o)
                    if main(n):
                        act_masked(act, g3, n - 1)
                    if front(n):
                        act_signs(act, g3, n, p, 3)
                steps(act, body)

            @block.gpsimd
            def _(pool):
                pool_rstd(pool, ve, rs, ve_ready, rs_ready, 0)
                pool_ball(pool, g3, 0)
                pool.wait_ge(g3.x_ready, NT)
                pool_rstd(pool, ve, rs, ve_ready, rs_ready, 1)

                def body(n, p, q):
                    if tail(n):
                        ge(pool, g3.out_ready, NT * (n - 2))
                        pool_rstd(pool, g3.ve, g3.rs, g3.ve_ready, g3.rs_ready, n - 2)
                    if front(n):
                        pool_xy(pool, g3, n, p)
                        mask_signs(pool, g3, n, p, POOL_HEAD, g3.s_pool)
                        split_xy(pool, g3, n, p)
                    if more(n):
                        pool_ball(pool, g3, n + 1)
                    if tail(n):
                        pool.wait_ge(g3.shift_ready, n - 1)
                        ge(pool, stored[p], 16 * (q - 1))
                        pool.nop(nofuse=True)
                        for t in range(NT):
                            pool.tensor_scalar(out_t[p][:, t, :], g3.y[p][:, t, :], g3.rs[:, t:t + 1],
                                               g3.shift[:, t:t + 1], ALU.mult, ALU.add).then_inc(g3.out_ready, 1)
                    if more2(n):
                        pool.wait_ge(g3.x_ready, NT * (n + 2))
                        pool_rstd(pool, ve, rs, ve_ready, rs_ready, n + 2)
                steps(pool, body)

            @block.vector
            def _(dve):
                def stats2(m):
                    dve_norm_stats(dve, lambda t: x2(m, t), stats, mv, ve, stat_ready, ve_ready, m)

                def new_mask(n, p, q):
                    dve.wait_ge(adj_in[p], 16 * (q + 1))
                    ge(dve, g3.mask_mm, n - 1)
                    ge(dve, g3.s_pool, n - 1)
                    dve.tensor_scalar(g3.mask[p][:, :, :], adjT[p][:, :, :], 0.0, None,
                                      ALU.is_gt).then_inc(g3.mask_ready, 1)
                def keep_x(m):
                    dve.wait_ge(g3.x_ready, NT * (m + 1))
                    dve.nop(nofuse=True)
                    dve.tensor_copy(xres[:, bass.ds(m, 1), :, :].rearrange("p a t d -> p (a t) d"),
                                    g3.x_in[0][:, :, :]).then_inc(x_kept, 1)
                def shift2(m):
                    dve_norm_shift(dve, mv, rs, rs_ready, shift, shift_ready, g3.x_ready, m)
                stats2(0)
                shift2(0)
                dve_xt_lo(dve, g3, 0, 0)
                keep_x(0)
                dve_bmax(dve, g3, 0, 0, zero1[:, 0:1])
                dve_scores(dve, g3, 0, 0, zero1[:, 0:1])
                stats2(1)
                shift2(1)

                def body(n, p, q):
                    c, o = n - 1, 1 - p
                    if tail(n):
                        dve.wait_ge(g3.y_ready, n - 1)
                        dve_norm_stats(dve, lambda t: g3.y[p][:, t, :], g3.stats, g3.mv, g3.ve,
                                       g3.stat_ready, g3.ve_ready, n - 2)
                    if front(n):
                        new_mask(n, p, q)
                        dve_xy(dve, g3, n, p)
                    if tail(n):
                        dve_norm_shift(dve, g3.mv, g3.rs, g3.rs_ready, g3.shift, g3.shift_ready, g3.out_ready, n - 2)
                    if more(n):
                        dve_xt_lo(dve, g3, n + 1, o)
                        keep_x(n + 1)
                    if front(n):
                        mask_signs(dve, g3, n, p, 1, g3.s_built)
                    if more2(n):
                        stats2(n + 2)
                    if more(n):
                        dve_bmax(dve, g3, n + 1, o, zero1[:, 0:1])
                    if main(n):
                        dve_sums(dve, g3, c, o)
                    if front(n):
                        mask_signs(dve, g3, n, p, 2, g3.s_built)
                    if main(n):
                        dve_quotient(dve, g3, c, o)
                    if more(n):
                        dve_scores(dve, g3, n + 1, o, zero1[:, 0:1])
                    if more2(n):
                        shift2(n + 2)
                    if front(n):
                        mask_signs(dve, g3, n, p, 3, g3.s_built)
                    if main(n):
                        dve.wait_ge(x_kept, n)
                        dve.wait_ge(g3.agg_ready, 2 * n)
                        dve.tensor_tensor(g3.y[o][:, :, :], g3.agg[o][:, :, :],
                                          xres[:, bass.ds(c, 1), :, :].rearrange("p a t d -> p (a t) d"),
                                          ALU.add).then_inc(g3.y_ready, 1)
                steps(dve, body)


def kernel(**inputs):
    import numpy as _np
    import concourse.bacc as _bacc
    from concourse import mybir as _mybir
    from concourse.bass_utils import run_bass_kernel_spmd as _run

    x = {k: _np.asarray(v) for k, v in inputs.items()}
    p = "L0_gnn_"
    consts = _np.zeros((128, 162), _np.float32)
    consts[0:4, 158:162] = consts[32:36, 158:162] = _np.eye(4)
    consts[:, 0:128] = _np.eye(128)
    for i, n in enumerate(("bn1_g", "bn1_b", "bn1_m", "bn1_v", "bn2_g", "bn2_b", "bn2_m", "bn2_v")):
        consts[:, 128 + i] = x[p + n]
    consts[:, 136:139] = x[p + "b_ih"].reshape(3, 128).T
    consts[:, 139:142] = x[p + "b_hh"].reshape(3, 128).T
    node_groups = [range(25), range(9), (0, *range(9, 15)), (6, 7, 8, 12, 13, 14), (3, 4, 5, 9, 10, 11)]
    member = _np.zeros((4, 32, 5), _np.float32)
    for g, nodes in enumerate(node_groups):
        member[:, list(nodes), g] = 1.0
    member = member.reshape(128, 5)
    consts[:, 142:147] = member
    consts[:, 147:157] = x["L2_gnn_b1"].reshape(10, 128).T
    w_se = _np.zeros((128, 96), _np.float32)
    for r in range(3):
        consts[32 * r:32 * r + 3, 157] = x[p + "b_se"]
        w_se[:, 32 * r:32 * r + 3] = x[p + "w_se"].T
    w_ih = x[p + "w_ih"].T
    gat_w = _np.zeros((128, 528), _np.float32)
    gat_w[:, 0:512] = _np.concatenate([x["L1_gnn_W_proj"].T, x["L3_gnn_W"], x["L1_gnn_W_proj"], x["L3_gnn_W"].T], 1)
    for h in range(4):
        at = slice(32 * h, 32 * h + 32)
        for side in range(2):
            gat_w[at, 512 + 4 * side + h] = x["L1_gnn_a_w"][0, 32 * side:32 * side + 32]
            gat_w[at, 520 + 4 * side + h] = x["L3_gnn_a"][h, 32 * side:32 * side + 32]
    adj_packs = _np.zeros((4, 32, 4, 4, 32), x["adj"].dtype)
    for r in range(4):
        adj_packs[r, :25, :, r, :25] = x["adj"][r::4, :25, :25].transpose(1, 0, 2)
    arrays = {
        "xT": x["x"].transpose(0, 2, 1),
        "adjT": x["adj"].transpose(0, 2, 1),
        "adj_packs": adj_packs.reshape(128, 512),
        "consts": consts,
        "rows": _np.concatenate([x[p + "b_msg"], x["L1_gnn_bias"], x["L1_gnn_a_w"][0, 64:65], x["L2_gnn_fusion_w"]]),
        "weights": _np.concatenate([x[p + "conv1_w"][:, :, 0].T, x[p + "conv2_w"].transpose(1, 2, 0).reshape(128, -1),
                                    x[p + "w_msg"].T, w_se, w_ih[0:128], w_ih[128:256], x[p + "w_hh"].T], axis=1),
        "gat_w": gat_w,
        "l2_w1": x["L2_gnn_W1"],
        "l2_w2": x["L2_gnn_W2"],
        "l2_b2": x["L2_gnn_b2"].reshape(640),
        "group_row": member.T.reshape(640),
    }
    nc = _bacc.Bacc("TRN2", target_bir_lowering=False, num_devices=1)
    aps, feed = {}, {}
    for name, v in arrays.items():
        v = _np.ascontiguousarray(v)
        feed[f"in_{name}"] = v
        aps[name] = nc.dram_tensor(f"in_{name}", v.shape, _mybir.dt.from_np(v.dtype), kind="ExternalInput").ap()
    aps["out"] = nc.dram_tensor("out_0", x["x"].shape, _mybir.dt.float32, kind="ExternalOutput").ap()
    build_program(nc, aps)
    r = _run(nc, [feed], core_ids=[0])
    return r.results[0]["out_0"]
```
